# Optimizing a Trainium2 kernel written in Bass

```python
import numpy as np
import jax
import jax.numpy as jnp

def _softmax(x, axis=-1):
    return jax.nn.softmax(x, axis=axis)

def _gelu(x):
    return jax.nn.gelu(x, approximate=True)

def _silu(x):
    return jax.nn.silu(x)

def _sigmoid(x):
    return jax.nn.sigmoid(x)

def _layernorm(x, axis=-1, eps=1e-05):
    m = jnp.mean(x, axis=axis, keepdims=True)
    v = jnp.var(x, axis=axis, keepdims=True)
    return (x - m) / jnp.sqrt(v + eps)

def _scatter_add(tgt, idx, src, axis=0):
    return tgt.at[idx].add(src)

def _segment_sum(src, seg, n):
    return jax.ops.segment_sum(src, seg, n)
kernel_name = 'mk_gnn_ffn_d1_gnn_r8_162dd4'

def setup_inputs(seed: int=0):
    np.random.seed(seed)
    _w = jnp.asarray

    def _rec_inputs():
        import jax
        import jax.numpy as jnp
        _gk = jax.random.key(seed)
        x = -0.0001126 + 1 * jax.random.normal(jax.random.fold_in(_gk, 1), (1250, 768), jnp.float32)
        _s = jax.random.randint(jax.random.fold_in(_gk, 2), (10000,), 0, 1250, jnp.int32)
        _d = jax.random.randint(jax.random.fold_in(_gk, 3), (10000,), 0, 1250, jnp.int32)
        _loop = jnp.arange(1250, dtype=jnp.int32)
        src = jnp.concatenate([_s, _d, _loop])
        dst = jnp.concatenate([_d, _s, _loop])
        _o = jnp.argsort(dst, stable=True)
        src = src[_o]
        dst = dst[_o]
        return (x, src, dst)
    x, src, dst = _rec_inputs()

    def _L0_gnn_setup():
        import jax, jax.numpy as jnp
        import numpy as np
        N_NODES = 1250
        N_EDGES = 20000
        NEG_SLOPE = 0.2

        def _gat_layer(x, src, dst, W, a_src, a_dst, bias, concat):
            N = x.shape[0]
            H, C = a_src.shape
            h = (x @ W).reshape(N, H, C)
            al_s = jnp.einsum('nhc,hc->nh', h, a_src)
            al_d = jnp.einsum('nhc,hc->nh', h, a_dst)
            e = jax.nn.leaky_relu(al_s[src] + al_d[dst], NEG_SLOPE)
            m = jax.ops.segment_max(e, dst, num_segments=N)
            ex = jnp.exp(e - m[dst])
            denom = jax.ops.segment_sum(ex, dst, num_segments=N)
            alpha = ex / (denom[dst] + 1e-16)
            msg = h[src] * alpha[:, :, None]
            out = jax.ops.segment_sum(msg, dst, num_segments=N)
            out = out.reshape(N, H * C) if concat else out.mean(axis=1)
            return out + bias
        key = jax.random.key(seed)
        ks = jax.random.split(key, 10)
        in_dim, hid, out_dim, heads = (768, 512, 768, 4)
        x = jax.random.normal(ks[0], (N_NODES, in_dim), dtype=jnp.float32)
        edge_index = jax.random.randint(ks[1], (2, N_EDGES), 0, N_NODES, dtype=jnp.int64)
        g = lambda k, shape, fan: jax.random.normal(k, shape, jnp.float32) / np.sqrt(fan)
        return {'x': x, 'edge_index': edge_index, 'W1': g(ks[2], (in_dim, heads * hid), in_dim), 'att_src1': g(ks[3], (heads, hid), hid), 'att_dst1': g(ks[4], (heads, hid), hid), 'b1': jnp.zeros((heads * hid,), jnp.float32), 'W2': g(ks[5], (heads * hid, out_dim), heads * hid), 'att_src2': g(ks[6], (1, out_dim), out_dim), 'att_dst2': g(ks[7], (1, out_dim), out_dim), 'b2': jnp.zeros((out_dim,), jnp.float32)}
    _L0_gnn_all = _L0_gnn_setup()
    _L0_gnn_in = {k: v for k, v in _L0_gnn_all.items() if k in ('W1', 'att_src1', 'att_dst1', 'b1', 'W2', 'att_src2', 'att_dst2', 'b2')}
    del _L0_gnn_all

    def _L0_ffn_setup():
        import math
        import jax, jax.numpy as jnp
        import numpy as np
        NUM_EXPERTS = 8
        TOP_K = 2
        CAPACITY_FACTOR = 1.25
        H = 768
        INNER = 384
        B, S = (2, 256)
        key = jax.random.key(seed)
        ks = jax.random.split(key, 9)
        scale = 0.02
        x = jax.random.normal(ks[0], (B, S, H), dtype=jnp.float32)
        Wr = jax.random.normal(ks[1], (H, NUM_EXPERTS), dtype=jnp.float32) * scale
        w1 = jax.random.normal(ks[2], (NUM_EXPERTS, H, INNER), dtype=jnp.float32) * scale
        w3 = jax.random.normal(ks[3], (NUM_EXPERTS, H, INNER), dtype=jnp.float32) * scale
        w2 = jax.random.normal(ks[4], (NUM_EXPERTS, INNER, H), dtype=jnp.float32) * scale
        s1 = jax.random.normal(ks[5], (H, INNER), dtype=jnp.float32) * scale
        s3 = jax.random.normal(ks[6], (H, INNER), dtype=jnp.float32) * scale
        s2 = jax.random.normal(ks[7], (INNER, H), dtype=jnp.float32) * scale
        return {'x': x, 'Wr': Wr, 'w1': w1, 'w3': w3, 'w2': w2, 's1': s1, 's3': s3, 's2': s2}
    _L0_ffn_all = _L0_ffn_setup()
    _L0_ffn_in = {k: v for k, v in _L0_ffn_all.items() if k in ('Wr', 'w1', 'w3', 'w2', 's1', 's3', 's2')}
    del _L0_ffn_all
    return {'x': x, 'src': src, 'dst': dst, 'L0_gnn_W1': _L0_gnn_in['W1'], 'L0_gnn_att_src1': _L0_gnn_in['att_src1'], 'L0_gnn_att_dst1': _L0_gnn_in['att_dst1'], 'L0_gnn_b1': _L0_gnn_in['b1'], 'L0_gnn_W2': _L0_gnn_in['W2'], 'L0_gnn_att_src2': _L0_gnn_in['att_src2'], 'L0_gnn_att_dst2': _L0_gnn_in['att_dst2'], 'L0_gnn_b2': _L0_gnn_in['b2'], 'L0_ffn_Wr': _L0_ffn_in['Wr'], 'L0_ffn_w1': _L0_ffn_in['w1'], 'L0_ffn_w3': _L0_ffn_in['w3'], 'L0_ffn_w2': _L0_ffn_in['w2'], 'L0_ffn_s1': _L0_ffn_in['s1'], 'L0_ffn_s3': _L0_ffn_in['s3'], 'L0_ffn_s2': _L0_ffn_in['s2']}

def reference(x, src, dst, L0_gnn_W1, L0_gnn_att_src1, L0_gnn_att_dst1, L0_gnn_b1, L0_gnn_W2, L0_gnn_att_src2, L0_gnn_att_dst2, L0_gnn_b2, L0_ffn_Wr, L0_ffn_w1, L0_ffn_w3, L0_ffn_w2, L0_ffn_s1, L0_ffn_s3, L0_ffn_s2):
    import jax
    import jax.numpy as jnp

    def _L0_gnn_ref(x, edge_index, W1, att_src1, att_dst1, b1, W2, att_src2, att_dst2, b2):
        import jax, jax.numpy as jnp
        import numpy as np
        N_NODES = 1250
        N_EDGES = 20000
        NEG_SLOPE = 0.2

        def _gat_layer(x, src, dst, W, a_src, a_dst, bias, concat):
            N = x.shape[0]
            H, C = a_src.shape
            h = (x @ W).reshape(N, H, C)
            al_s = jnp.einsum('nhc,hc->nh', h, a_src)
            al_d = jnp.einsum('nhc,hc->nh', h, a_dst)
            e = jax.nn.leaky_relu(al_s[src] + al_d[dst], NEG_SLOPE)
            m = jax.ops.segment_max(e, dst, num_segments=N)
            ex = jnp.exp(e - m[dst])
            denom = jax.ops.segment_sum(ex, dst, num_segments=N)
            alpha = ex / (denom[dst] + 1e-16)
            msg = h[src] * alpha[:, :, None]
            out = jax.ops.segment_sum(msg, dst, num_segments=N)
            out = out.reshape(N, H * C) if concat else out.mean(axis=1)
            return out + bias
        N = x.shape[0]
        loops = jnp.arange(N, dtype=edge_index.dtype)
        src = jnp.concatenate([edge_index[0], loops])
        dst = jnp.concatenate([edge_index[1], loops])
        h = jax.nn.elu(_gat_layer(x, src, dst, W1, att_src1, att_dst1, b1, concat=True))
        out = _gat_layer(h, src, dst, W2, att_src2, att_dst2, b2, concat=False)
        return out

    def _L0_ffn_ref(x, Wr, w1, w3, w2, s1, s3, s2):
        import math
        import jax, jax.numpy as jnp
        import numpy as np
        NUM_EXPERTS = 8
        TOP_K = 2
        CAPACITY_FACTOR = 1.25
        H = 768
        INNER = 384
        B, S = (2, 256)
        b, s, h = x.shape
        n = b * s
        flat = x.reshape(n, h)
        logits = flat @ Wr
        probs = jax.nn.softmax(logits, axis=-1)
        topk_p, topk_i = jax.lax.top_k(probs, TOP_K)
        topk_p = topk_p / jnp.clip(topk_p.sum(-1, keepdims=True), 1e-09)
        capacity = max(1, math.ceil(n * TOP_K / NUM_EXPERTS * CAPACITY_FACTOR))
        onehot = topk_i[None, :, :] == jnp.arange(NUM_EXPERTS)[:, None, None]
        w_tok = jnp.sum(topk_p[None] * onehot, axis=-1)
        assigned = jnp.any(onehot, axis=-1)
        score = jnp.where(assigned, w_tok, -jnp.inf)
        order = jnp.argsort(-score, axis=1)[:, :capacity]
        score_sel = jnp.take_along_axis(score, order, axis=1)
        valid = jnp.isfinite(score_sel)
        weight_sel = jnp.where(valid, score_sel, 0.0)
        dispatch = flat[order]
        gate = jax.nn.silu(jnp.einsum('ech,ehi->eci', dispatch, w1))
        up = jnp.einsum('ech,ehi->eci', dispatch, w3)
        expert_out = jnp.einsum('eci,eih->ech', gate * up, w2)
        expert_out = expert_out * weight_sel[..., None]
        routed = jnp.zeros((n, h), dtype=flat.dtype)
        routed = routed.at[order.reshape(-1)].add(expert_out.reshape(-1, h))
        shared = jax.nn.silu(flat @ s1) * (flat @ s3) @ s2
        out = routed + shared
        return out.reshape(b, s, h)
    edge_index = jnp.stack([src, dst])
    x = x + _L0_gnn_ref(_layernorm(x, axis=-1), edge_index, L0_gnn_W1, L0_gnn_att_src1, L0_gnn_att_dst1, L0_gnn_b1, L0_gnn_W2, L0_gnn_att_src2, L0_gnn_att_dst2, L0_gnn_b2)
    x = x + _L0_ffn_ref(_layernorm(x, axis=-1)[None], L0_ffn_Wr, L0_ffn_w1, L0_ffn_w3, L0_ffn_w2, L0_ffn_s1, L0_ffn_s3, L0_ffn_s2)[0]
    return x

_drawn_inputs = setup_inputs


def setup_inputs(seed=0):
    import zlib

    import numpy as np

    out = dict(_drawn_inputs(seed))
    spreads = {'L0_gnn_b1': (0.0, 0.1), 'L0_gnn_b2': (0.0, 0.1)}
    factors = {'L0_gnn_att_dst1': 3.535, 'L0_gnn_att_src2': 2.98, 'L0_gnn_att_dst2': 8.0}
    for name, (base, spread) in spreads.items():
        noise = np.random.default_rng([zlib.crc32(name.encode()), seed]).standard_normal(out[name].shape)
        drawn = base * np.exp(spread * noise) if base else spread * noise
        out[name] = jnp.asarray(drawn.astype(out[name].dtype))
    for name, factor in factors.items():
        out[name] = (out[name] * factor).astype(out[name].dtype)
    return out
```

```python
from contextlib import ExitStack

import numpy as np
import concourse.bass as bass
from concourse import mybir

ALU = mybir.AluOpType
ACT = mybir.ActivationFunctionType
AX = mybir.AxisListType
F32 = mybir.dt.float32
F16 = mybir.dt.float16
BF16 = mybir.dt.bfloat16
I32 = mybir.dt.int32
U32 = mybir.dt.uint32

SX = 64.0
SW = 1024.0
SA = 256.0
NEG = -1.0e30
EPS = 1e-5
SLOPE = 0.2


def build(nc, x, src, dst, W1, as1, ad1, b1, W2, as2, ad2, b2, Wr, w1, w3, w2, s1, s3, s2, out):
    N, D = x.shape
    NE = src.shape[0]
    H, C = as1.shape
    E, _, INNER = w1.shape
    T = 125
    NT = N // T
    KD = D // 128
    CH = C // 128
    NCH = H * CH
    KI = INNER // 128
    CAP = -(-N * 2 * 5 // (E * 4))
    SLOTS = CAP + CAP % 2
    SC = SLOTS // 4
    DH = D // 2
    BLK = [(0, 417), (417, 417), (834, 416)]
    assert NT * T == N and NE % T == 0 and SLOTS % 4 == 0

    ET = NE // T
    DC = 50
    NC = N // DC
    GC = 5
    GT = ET // (NC // GC)
    PADT = 4
    MARGIN = 250
    KC = NT * DC
    window = []
    for c in range(GC):
        lo = (c * DC * NE // N - MARGIN) // T
        hi = -(-((c + 1) * DC * NE // N + MARGIN) // T)
        window.append((lo + PADT, hi + PADT))
    assert window[0][0] >= 0 and window[-1][1] <= GT + 2 * PADT
    KT = ET + 2 * PADT
    selfs = [sorted({(c * DC) // T, (c * DC + DC - 1) // T}) for c in range(GC)]
    jobs = [[("e", t) for t in range(*window[c])] + [("s", t) for t in selfs[c]] for c in range(GC)]
    NJ = sum(len(j) for j in jobs)
    KA = KT + NT
    TOTAL = NE + N

    BASE = 16512
    names = [0]

    def at(off, shape, dt):
        names[0] += 1
        return nc.alloc_sbuf_tensor_at(f"sb{names[0]}", list(shape), dt, offset=BASE + off)

    o_ct, o_p, o_h, o_e = 0, 25024, 75040, 116000
    CT = at(o_ct, [T, NT, N], F16)
    P = at(o_p, [T, NT, 2, N], F16)
    OL = at(o_p, [T, KA, T], F16)
    XA = at(o_p, [T, NT, D], F32)
    HB = [at(o_h + b * 20480, [T, NT, 2, C], F16) for b in range(2)]
    ED = at(o_h + 20480, [85, 2, 2, T], I32)
    EF = at(o_h + 20480 + 2048, [85, 2, 2 * T], F32)
    EQ = at(o_h + 20480 + 4096, [85, 2, 2 * T], I32)
    EG = at(o_h + 20480 + 6144, [85, 2, 2 * T], F32)
    EK = at(o_h + 20480 + 8192, [85, 2, 2 * T], F32)
    OR = at(o_h + 20480 + 10240, [T, 4, KC], F16)
    H2 = at(o_h, [T, NT, 2, D + 2], F16)
    HT = [at(o_h + 32000, [128, 2, NCH, T], F16), None]
    o = o_e
    ROW = at(o, [T, 2, N], F32); o += 10016
    TMP = at(o, [T, 3, N], F32)
    W2G = [at(o + 3072 * b, [128, D], F32) for b in range(3)]; o += 15008
    MSK = at(o, [T, 2, N], BF16); o += 5024
    o_w2s = o
    XTR = at(o, [128, 3, 2, KD, T], F16); o += 9024
    W1S = at(o, [128, KD, 2, C], F16); o += 12288
    WST = at(o, [128, 2, D], F32); o += 6144
    YB = at(o, [128, 3, 417], F32)
    VJ = at(o, [128, D], F32); o += 5024
    RB = at(o, [128, 2, 417], F32); o += 3360
    H1O = at(o, [128, 2, 2, N], F16); o += 10016
    RDEN = at(o, [128, N], F32); o += 5024
    AR1 = at(o, [T, 2, 2, C], F32); o += 8192
    JNK = at(o, [T, C], F16); o += 1024
    assert o <= 207000
    A2R = at(o_e + 10016, [128, 2, D], F32)
    W2S = at(o_w2s, [128, NCH, 2, D], F16)
    HT[1] = at(o_w2s + 49152, [128, 2, NCH, T], F16)
    assert o_w2s + 49152 + 8000 <= 207000
    X2 = at(o_w2s, [T, NT, D], F32)
    B2R = at(o_w2s + 30720, [T, D], F32)
    XN2 = at(0, [T, NT, D], F32)
    X2T = at(30720, [128, 2, KD, N], F16)
    WG = at(60736, [128, 3 * 2304], F32)
    WS = [at(88384 + b * 27648, [128, 2, 3 * 2304], F16) for b in range(2)]
    o_f = 177760
    AB = at(o_f, [128, 2, KI, N], F16); o = o_f + 15008
    AE = [at(o_f + b * 4704, [128, 2, KI, SLOTS], F16) for b in range(2)]
    SG = at(o, [128, 2, 512], F32); o += 4096
    YO = at(o, [SC, 2, D], F32); o += 6144
    assert o <= 203328 and o_w2s + 30720 <= o_f
    IND = at(0, [T, 2, NT, SLOTS], F16)
    XG = at(15680, [SC, 2, D], F32)
    S3T = at(21824, [24, N], BF16)
    O3T = [at(24352 + k * 2528, [24, N], BF16) for k in range(2)]
    XGT = [at(30720 + b * 9408, [128, 2, KD, SLOTS], F16) for b in range(2)]
    JN2 = at(30720 + 20000, [T, N], BF16)
    GR = at(0, [T, 4, D], F32)

    o = 207008

    def small(shape, dt):
        nonlocal o
        size = int(np.prod(shape[1:])) * {F32: 4, I32: 4, U32: 4, F16: 2, BF16: 2}[dt]
        t = at(o, shape, dt)
        o += -(-size // 32) * 32
        assert BASE + o <= 229344, o
        return t

    idf = small([128, 128], F32)
    idh = small([128, 128], F16)
    idb = small([128, 128], BF16)
    ones = small([T, 128], F16)
    TRI = small([T, T], F16)
    io392 = small([T, SLOTS], F16)
    tokid = small([T, NT], F32)
    io8 = small([T, E], F32)
    LG = small([T, NT, E], F32)
    o_k = o_h + 20480 + 16000
    iok = at(o_k, [T, KC], F16)
    iot = at(o_k + 1024, [T, T], F16)
    KEY = at(o_k + 1280, [T, KA], F32)
    SLO = at(o_k + 2048, [T, KA], F32)
    onesf = at(o_k + 2816, [T, 128], F32)
    b1c = small([128, NCH], F32)
    V2F = small([128, NCH, 2], F32)
    V2S = small([128, NCH, 2, 2], F16)
    AL = small([T, 2, H + 1, NT], F32)
    ALF = small([T, H + 1, NT], F32)
    A2C = small([T, 2 * NT], F32)
    MX = small([T, NT], F32)
    ZZ = small([T, NT], F32)
    MM = small([T, NT], F32)
    AA = small([T, 2, NT], F32)
    TR = small([2 * NT, T], F32)
    CS = small([T, NC], F32)
    flag = small([128, 1], I32)
    QI = small([T, NT], I32)
    SD = small([T, NT], F32)
    def mid(shape, dt):
        nonlocal o
        size = int(np.prod(shape[1:])) * {F32: 4, I32: 4, U32: 4, F16: 2, BF16: 2}[dt]
        t = at(o, shape, dt)
        o += -(-size // 32) * 32
        return t

    o = 143680
    assert o + 2300 <= o_w2s
    M8 = mid([T, NT, 8], F32)
    I8 = mid([T, NT, 8], U32)
    OK = [mid([T, NT, E], F32) for _ in range(2)]
    SS = mid([T, NT, E], F32)
    IK = mid([T, 2, NT], F32)
    WK = mid([T, 2, NT], F32)
    CA = mid([T, 3, 2, NT], F32)
    assert o <= o_w2s, (o, o_w2s)
    o = 203328
    OT = [mid([T, NT, E], F16) for _ in range(2)]
    RK = mid([T, 2, NT], F32)
    S3 = mid([T, NT, 24], BF16)
    O3 = [mid([T, NT, 24], BF16) for _ in range(2)]
    IDX = mid([T, 2, NT], U32)
    TOK = mid([SC, 4, E], U32)
    WRS = mid([128, KD, 2, E], F16)
    WRG = mid([128, KD, E], F32)
    MV = mid([T, NT, 2], F32)
    assert o <= 207008, o
    BS = at(o_f, [T, NT, 2, 6], F32)
    BS1 = at(o_h + 20480 + 14336, [T, NT, 2, 6], F32)
    MV1 = at(o_h + 20480 + 15360, [T, NT, 2], F32)

    def dram(name, shape, dt):
        return nc.dram_tensor(name, list(shape), dt, kind="Internal").ap()

    XTD = dram("xt_d", [NT, 128, 2 * KD * T], F16)
    MSKD = dram("mask_d", [NT, T, N], BF16)
    ALD = dram("al_d", [H + 1, NT, T], F32)
    AAD = dram("aa_d", [H + 1, 2 * NT, T], F32)
    H1D = dram("h1_d", [NT, 128, 2, NCH, T], F16)
    XND = dram("xn_d", [N, D], F32)
    YD = dram("y_d", [E * SLOTS, D], F32)

    ctx = ExitStack()
    with ctx:
        PS = ctx.enter_context(nc.psum_tensor("PS", [128, 8, 512], F32))
        PSF = PS[:, :, :].rearrange("p b n -> p (b n)")

        def ps16(dt):
            return PSF.bitcast(dt)

        PH, PB = ps16(F16), ps16(BF16)

        def col16(b, i):
            return 1024 * (b + i // 5) + (T + 1) * (i % 5)

        def blocks16(v, rows, b):
            return v[0:rows, 1024 * b:1024 * b + 2048].rearrange("p (a r) -> p a r", a=2)[
                :, :, 0:5 * (T + 1)].rearrange("p a (i n) -> p a i n", n=T + 1)[:, :, :, 0:T]

        def sem(name):
            return ctx.enter_context(nc.semaphore(name))

        s_const = sem("consts_made")
        s_edges = sem("edges_loaded")
        s_x = sem("x_loaded")
        s_b1 = sem("b1_loaded")
        s_a2v = sem("a2_loaded")
        s_dve = sem("dve_step")
        s_act = sem("act_step")
        s_keys = sem("keys_made")
        s_keyT = sem("keys_transposed")
        s_var = sem("variance_made")
        s_sd = sem("deviation_made")
        s_xn = sem("x_normalised")
        s_xT = sem("x_transposed")
        s_xth = sem("xT_hi_made")
        s_xtl = sem("xT_lo_made")
        s_xts = [sem(f"xT_slot{b}") for b in range(3)]
        s_wst = [sem(f"weights_in_slot{b}") for b in range(2)]
        s_wh = sem("weight_hi_made")
        s_wl = sem("weight_slot_used")
        s_arep = sem("attention_vectors_loaded")
        s_proj = sem("projection_done")
        s_hh = sem("h_hi_made")
        s_hl = sem("h_used")
        s_ol = sem("source_onehots_made")
        s_or = sem("pair_onehot_made")
        s_cm = sem("pair_onehot_used")
        s_k2 = sem("keys_advanced")
        s_ce = sem("chunk_kept")
        s_cs = sem("count_sum_made")
        s_ct1 = sem("count_total_made")
        s_flag = sem("count_flag_made")
        s_go = sem("general_onehot_made")
        s_gu = sem("general_onehot_used")
        s_gd = sem("general_chunk_done")
        s_gk = sem("general_chunk_kept")
        s_ctok = sem("counts_final")
        s_mt = sem("mask_transposed")
        s_mm = sem("mask_made")
        s_ms = [sem(f"mask_stored{b}") for b in range(2)]
        s_ml = [sem(f"mask_loaded{b}") for b in range(2)]
        s_mu = sem("mask_used")
        s_v2 = sem("v2_made")
        s_alt = sem("al_transposed")
        s_alc = sem("al_row_made")
        s_ald = sem("al_row_stored")
        s_row = sem("al_row_broadcast")
        s_aa = sem("shifts_made")
        s_aat = sem("shifts_transposed")
        s_aac = sem("shift_rows_made")
        s_aad = sem("shift_rows_stored")
        s_rows = sem("shift_rows_broadcast")
        s_al = sem("al_complete")
        s_p1 = sem("p_second_branch")
        s_p2 = sem("p_leaky")
        s_p3 = sem("p_exp")
        s_p4 = sem("p_counted")
        s_p5 = sem("p_hi")
        s_p6 = sem("p_lo")
        s_att = sem("attention_group_done")
        s_atr = sem("attention_group_read")
        s_rd = sem("denominator_made")
        s_y1 = sem("y_divided")
        s_yr = sem("y_relu")
        s_y2 = sem("y_exp")
        s_y3 = sem("y_elu1")
        s_y4 = sem("y_scaled")
        s_y5 = sem("h1_hi")
        s_y6 = sem("h1_lo")
        s_h1s = [sem(f"h1_stored{b}") for b in range(2)]
        s_a2 = sem("al2_part_done")
        s_al4 = sem("al2_made")
        s_a2r = sem("al2_part_added")
        s_w2g = [sem(f"w2_in_slot{b}") for b in range(3)]
        s_w2h = sem("w2_hi")
        s_w2l = sem("w2_lo")
        s_ht = [sem(f"h1_loaded{b}") for b in range(2)]
        s_pj2 = sem("projection2_done")
        s_h2h = sem("h2_hi")
        s_h2l = sem("h2_lo")
        s_h2o = sem("h2_ones")
        s_x2l = sem("x_again")
        s_xb = sem("x_plus_bias")
        s_at2 = sem("attention2_done")
        s_x2 = sem("x2_made")
        s_var2 = sem("variance2_made")
        s_sd2 = sem("deviation2_made")
        s_xn2 = sem("x2_normalised")
        s_xns = sem("xn2_stored")
        s_x2t = sem("x2_transposed")
        s_x2h = sem("x2T_hi")
        s_x2lo = sem("x2T_lo")
        s_wrl = sem("router_loaded")
        s_wrh = sem("router_hi")
        s_wrs = sem("router_split")
        s_lg = sem("logits_done")
        s_lgm = sem("logits_shifted")
        s_pe = sem("probs_exp")
        s_wg = sem("ffn_weights_loaded")
        s_wgh = sem("ffn_weights_hi")
        s_wgl = sem("ffn_weights_lo")
        s_gu2 = sem("gate_up_done")
        s_sg = sem("silu_made")
        s_gx = sem("gate_times_up")
        s_ah = sem("act_hi")
        s_alo = sem("act_lo")
        s_s3 = sem("scores_split")
        s_s3t = sem("scores_transposed")
        s_s3c = sem("scores_rows_made")
        s_sd3 = sem("shared_down_done")
        s_sdr = sem("shared_added")
        s_rr = sem("rank_rows_done")
        s_rk = sem("rank_rows_used")
        s_ind = sem("slots_onehot_made")
        s_tk = sem("token_table_done")
        s_tok = sem("token_table_made")
        s_xg = [sem(f"rows_gathered{b}") for b in range(2)]
        s_xgt = sem("rows_transposed")
        s_xgh = sem("rows_hi")
        s_xgl = sem("rows_lo")
        s_ed = sem("expert_down_done")
        s_yo = sem("expert_rows_made")
        s_ys = [sem(f"expert_rows_stored{b}") for b in range(2)]
        s_gz = sem("gather_cleared")
        s_gg = [sem(f"expert_rows_gathered{b}") for b in range(4)]
        s_g1 = sem("expert_rows_added")
        s_fin = sem("out_stored")

        block = ctx.enter_context(nc.Block())

        def w1_use(h, k):
            return k if h == 0 else KD + NCH + (h - 1) * KD + k

        def v2_use(ch):
            return KD + ch

        HALF = 2304

        def ffn_weights(n):
            if n == 0:
                return s1, s3, s2
            return w1[n - 1], w3[n - 1], w2[n - 1]

        @block.sync
        def _(sp):
            sp.dma_start(ED[:, 0], src.rearrange("(a q p) -> q a p", a=2, p=T)).then_inc(s_edges, 16)
            sp.dma_start(ED[:, 1], dst.rearrange("(a q p) -> q a p", a=2, p=T)).then_inc(s_edges, 16)
            sp.dma_start(XA[:, :, :], x.rearrange("(i p) d -> p i d", p=T)).then_inc(s_x, 16)
            with nc.allow_non_contiguous_dma(reason="one small column load"):
                sp.dma_start(b1c[:, :], b1.rearrange("(c p) -> p c", p=128)).then_inc(s_b1, 16)

            def load_w(u, view):
                if u >= 2:
                    sp.wait_ge(s_wl, u - 1)
                sp.dma_start(WST[:, u % 2, 0:view.shape[1]], view).then_inc(s_wst[u % 2], 16)

            def load_w1(h):
                load_al(h)
                load_w1_rows(h, range(KD))

            def load_al(h):
                if h >= 2:
                    sp.wait_ge(s_hl, NT * (h - 1))
                sp.dma_start(AR1[:, h % 2, 0, :], as1[h:h + 1, :].to_broadcast([T, C])).then_inc(s_arep, 16)
                sp.dma_start(AR1[:, h % 2, 1, :], ad1[h:h + 1, :].to_broadcast([T, C])).then_inc(s_arep, 16)

            def load_w1_rows(h, ks):
                for k in ks:
                    load_w(w1_use(h, k), W1[128 * k:128 * k + 128, C * h:C * h + C])

            def store_xt(i):
                sp.wait_ge(s_xtl, i + 1)
                sp.dma_start(XTD[i], XTR[:, i % 3].rearrange("p a k n -> p (a k n)")).then_inc(s_xts[i % 3], 16)

            def slot_uses(v):
                return 16 * (v // 3 + 1)

            def load_xt(h, i):
                v = NT + NT * h + i
                if v - 3 < NT:
                    sp.wait_ge(s_xts[v % 3], slot_uses(v - 3))
                else:
                    sp.wait_ge(s_proj, v - 3 - NT + 1)
                if h == 0:
                    sp.wait_ge(s_xts[i % 3], slot_uses(i))
                sp.dma_start(XTR[:, v % 3].rearrange("p a k n -> p (a k n)"), XTD[i]).then_inc(s_xts[v % 3], 16)

            load_al(0)
            load_w1_rows(0, range(2))
            for i in range(NT):
                store_xt(i)
            load_w1_rows(0, range(2, KD))
            for i in range(NT):
                load_xt(0, i)
            for j in range(NT):
                sp.wait_ge(s_mm, j + 1)
                sp.dma_start(MSKD[j], MSK[:, j % 2, :]).then_inc(s_ms[j % 2], 16)
            sp.wait_ge(s_xn, NT)
            sp.dma_start(A2R[:, 0, :], as2.to_broadcast([128, D])).then_inc(s_a2v, 16)
            sp.dma_start(A2R[:, 1, :], ad2.to_broadcast([128, D])).then_inc(s_a2v, 16)
            for ch in range(NCH):
                load_w(v2_use(ch), W2[128 * ch:128 * ch + 128, :])

            def chain_row(h):
                sp.wait_ge(s_alc, h + 1)
                sp.dma_start(ALD[h], TR[0:NT, :]).then_inc(s_ald, 16)
                sp.wait_ge(s_ald, 16 * (h + 1))
                if h:
                    sp.wait_ge(s_p1, NT * h)
                    sp.wait_ge(s_p2, NT * h)
                sp.dma_start(ROW[:, 0, :], ALD[h:h + 1].rearrange("o a n -> o (a n)").to_broadcast([T, N])
                             ).then_inc(s_row, 16)

            def chain_mask(h, js):
                for j in js:
                    n = NT * h + j
                    if n < 2:
                        sp.wait_ge(s_ms[0], 16 * (NT // 2))
                        sp.wait_ge(s_ms[1], 16 * (NT // 2))
                    else:
                        sp.wait_ge(s_mu, n - 1)
                    sp.dma_start(MSK[:, j % 2, :], MSKD[j]).then_inc(s_ml[j % 2], 16)

            def chain_shift(h):
                sp.wait_ge(s_aac, h + 1)
                sp.dma_start(AAD[h], TR[:, :]).then_inc(s_aad, 16)
                sp.wait_ge(s_aad, 16 * (h + 1))
                sp.dma_start(ROW[:, :, :].rearrange("p a n -> p (a n)"),
                             AAD[h:h + 1].rearrange("o a n -> o (a n)").to_broadcast([T, 2 * N])
                             ).then_inc(s_rows, 16)

            def store_h1(h, c):
                g = CH * h + c
                sp.wait_ge(s_y6, 3 * (g + 1))
                for part in range(2):
                    sp.dma_start(H1D[:, :, part, g, :].rearrange("j p n -> p j n"),
                                 H1O[:, g % 2, part, :].rearrange("p (j n) -> p j n", n=T)
                                 ).then_inc(s_h1s[g % 2], 16)

            chain_row(0)
            chain_mask(0, range(NT))
            chain_shift(0)
            load_w1(1)
            for i in range(NT):
                load_xt(1, i)
            for h in range(H):
                if h + 1 < H:
                    chain_row(h + 1)
                    chain_mask(h + 1, range(NT // 2))
                store_h1(h, 0)
                if h + 1 < H:
                    chain_mask(h + 1, range(NT // 2, NT))
                if h + 2 < H:
                    load_w1(h + 2)
                store_h1(h, 1)
                if h + 1 < H:
                    chain_shift(h + 1)
                if h + 2 < H:
                    for i in range(3):
                        load_xt(h + 2, i)
                store_h1(h, 2)
                store_h1(h, 3)
                if h + 2 < H:
                    for i in range(3, NT):
                        load_xt(h + 2, i)

            sp.wait_ge(s_p6, NT * H)
            for ch in range(NCH):
                if ch >= 3:
                    sp.wait_ge(s_w2l, ch - 2)
                sp.dma_start(W2G[ch % 3][:, :], W2[128 * ch:128 * ch + 128, :]).then_inc(s_w2g[ch % 3], 16)

            def load_ht(j):
                if j == 0:
                    for b in range(2):
                        sp.wait_ge(s_h1s[b], 16 * NCH)
                    sp.wait_ge(s_att, 5 * H)
                if j >= 2:
                    sp.wait_ge(s_pj2, j - 1)
                sp.dma_start(HT[j % 2][:, :, :, :].rearrange("p a c n -> p (a c n)"),
                             H1D[j].rearrange("p a c n -> p (a c n)")).then_inc(s_ht[j % 2], 16)

            load_ht(0)
            chain_row(H)
            load_ht(1)
            chain_mask(H, range(NT))
            chain_shift(H)
            for j in range(2, NT):
                load_ht(j)
            sp.wait_ge(s_pj2, NT)
            sp.dma_start(X2[:, :, :], x.rearrange("(i p) d -> p i d", p=T)).then_inc(s_x2l, 16)
            sp.dma_start(B2R[:, :], b2.rearrange("(o d) -> o d", o=1).to_broadcast([T, D])).then_inc(s_x2l, 16)
            sp.wait_ge(s_at2, NT)
            sp.dma_start(WRG[:, :, :], Wr.rearrange("(k p) e -> p k e", p=128)).then_inc(s_wrl, 16)

            def load_ffn(n):
                a, b, c = ffn_weights(n)
                if n:
                    sp.wait_ge(s_wgh, 3 * n)
                    sp.wait_ge(s_wgl, 3 * n)
                sp.dma_start(WG[:, 0:HALF].rearrange("p (k i) -> p k i", k=KD),
                             a.rearrange("(k p) i -> p k i", p=128)).then_inc(s_wg, 16)
                sp.dma_start(WG[:, HALF:2 * HALF].rearrange("p (k i) -> p k i", k=KD),
                             b.rearrange("(k p) i -> p k i", p=128)).then_inc(s_wg, 16)
                sp.dma_start(WG[:, 2 * HALF:].rearrange("p (k i) -> p k i", k=KI),
                             c.rearrange("(k p) i -> p k i", p=128)).then_inc(s_wg, 16)

            load_ffn(0)
            for i in range(NT):
                sp.wait_ge(s_xn2, i + 1)
                sp.dma_start(XND[T * i:T * i + T, :], XN2[:, i, :]).then_inc(s_xns, 16)
            load_ffn(1)
            for e in range(E):
                if e + 2 <= E:
                    load_ffn(e + 2)
                for c in range(4):
                    g = 4 * e + c
                    sp.wait_ge(s_yo, g + 1)
                    sp.dma_start(YD[SLOTS * e + SC * c:SLOTS * e + SC * c + SC, :], YO[:, g % 2, :]
                                 ).then_inc(s_ys[g % 2], 16)
            for j in range(NT):
                sp.wait_ge(s_g1, 2 * (j + 1))
                sp.dma_start(out[T * j:T * j + T, :], X2[:, j, :]).then_inc(s_fin, 16)
            sp.wait_ge(s_fin, 16 * NT)

        @block.gpsimd
        def _(pool):
            made = [0]

            def link(ins):
                made[0] += 1
                ins.then_inc(s_const, 1)
                pool.wait_ge(s_const, made[0])

            for t in (idf, idh, idb):
                link(nc.gpsimd.memset(t[:, :], 0.0))
                link(nc.gpsimd.affine_select(out=t[:, :], in_=t[:, :], compare_op=ALU.not_equal, fill=1.0,
                                             base=0, pattern=[[-1, 128]], channel_multiplier=1))
            link(nc.gpsimd.iota(iok[:, :], [[1, KC]], base=0, channel_multiplier=0,
                                allow_small_or_imprecise_dtypes=True))
            link(nc.gpsimd.iota(iot[:, :], [[1, T]], base=0, channel_multiplier=0,
                                allow_small_or_imprecise_dtypes=True))
            link(nc.gpsimd.memset(ones[:, :], 1.0))
            link(nc.gpsimd.memset(onesf[:, :], 1.0))
            link(nc.gpsimd.memset(KEY[:, 0:KT], -1.0))
            link(nc.gpsimd.memset(SLO[:, 0:KT], -1.0))
            link(nc.gpsimd.iota(SLO[:, KT:KA], [[0, NT]], base=0, channel_multiplier=1,
                                allow_small_or_imprecise_dtypes=True))
            link(nc.gpsimd.iota(MX[:, :], [[T, NT]], base=0, channel_multiplier=1,
                                allow_small_or_imprecise_dtypes=True))
            link(nc.gpsimd.iota(ZZ[:, :], [[T + DC, NT]], base=0, channel_multiplier=1,
                                allow_small_or_imprecise_dtypes=True))

            def p_lo(h, i):
                q = NT * h + i
                pool.wait_ge(s_p5, q + 1)
                nc.gpsimd.tensor_tensor(P[:, i, 1, :], TMP[:, q % 3, :], P[:, i, 0, :], ALU.subtract
                                        ).then_inc(s_p6, 1)

            def h1_lo(h, c, b):
                g = CH * h + c
                y = 3 * g + b
                lo, n = BLK[b]
                pool.wait_ge(s_y3, y + 1)
                nc.gpsimd.tensor_scalar(YB[:, y % 3, 0:n], YB[:, y % 3, 0:n], SX, -SX, ALU.mult, ALU.add
                                        ).then_inc(s_y4, 1)
                pool.wait_ge(s_y5, y + 1)
                nc.gpsimd.tensor_tensor(H1O[:, g % 2, 1, lo:lo + n], YB[:, y % 3, 0:n],
                                        H1O[:, g % 2, 0, lo:lo + n], ALU.subtract).then_inc(s_y6, 1)

            for i in range(NT):
                p_lo(0, i)
            for h in range(H):
                for c in range(CH):
                    for b in range(3):
                        h1_lo(h, c, b)
                if h + 1 < H:
                    for i in range(NT):
                        p_lo(h + 1, i)
            for i in range(NT):
                p_lo(H, i)
            pool.wait_ge(s_x2l, 32)
            for j in range(NT):
                nc.gpsimd.tensor_tensor(X2[:, j, :], X2[:, j, :], B2R[:, :], ALU.add).then_inc(s_xb, 1)

            pool.wait_ge(s_at2, NT)
            link(nc.gpsimd.memset(TRI[:, :], 1.0))
            link(nc.gpsimd.affine_select(out=TRI[:, :], in_=TRI[:, :], compare_op=ALU.is_gt, fill=0.0,
                                         base=0, pattern=[[-1, T]], channel_multiplier=1))
            link(nc.gpsimd.iota(io392[:, :], [[1, SLOTS]], base=0, channel_multiplier=0,
                                allow_small_or_imprecise_dtypes=True))
            link(nc.gpsimd.iota(tokid[:, :], [[T, NT]], base=0, channel_multiplier=1,
                                allow_small_or_imprecise_dtypes=True))
            link(nc.gpsimd.iota(io8[:, :], [[1, E]], base=0, channel_multiplier=0,
                                allow_small_or_imprecise_dtypes=True))

            def act_lo(n, dst, src_, hi):
                pool.wait_ge(s_ah, n + 1)
                nc.gpsimd.tensor_tensor(dst, src_, hi, ALU.subtract).then_inc(s_alo, 1)

            for m in range(KI):
                for b, (lo, w) in enumerate(BLK):
                    n = 3 * m + b
                    act_lo(n, AB[:, 1, m, lo:lo + w], SG[:, n % 2, 0:w], AB[:, 0, m, lo:lo + w])

            def gather(g):
                e, c = divmod(g, 4)
                if g >= 2:
                    pool.wait_ge(s_xgt, g - 1)
                nc.gpsimd.indirect_dma_start(
                    out=XG[:, g % 2, :], out_offset=None, in_=XND[:, :],
                    in_offset=bass.IndirectOffsetOnAxis(ap=TOK[:, c, e:e + 1], axis=0),
                ).then_inc(s_xg[g % 2], 16)

            pool.wait_ge(s_tok, 1)
            pool.wait_ge(s_xns, 16 * NT)
            for g in range(4):
                gather(g)
            for e in range(E):
                if e + 1 < E:
                    for c in range(4):
                        gather(4 * (e + 1) + c)
                for m in range(KI):
                    n = 9 + KI * e + m
                    act_lo(n, AE[e % 2][:, 1, m, :], SG[:, n % 2, 0:SLOTS], AE[e % 2][:, 0, m, :])

            pool.wait_ge(s_xgt, 4 * E)
            pool.wait_ge(s_tk, 1)
            for b in range(2):
                pool.wait_ge(s_ys[b], 16 * 2 * E)
            for n in range(2 * NT):
                j, k = divmod(n, 2)
                b = n % 4
                if n >= 4:
                    pool.wait_ge(s_g1, n - 3)
                nc.gpsimd.memset(GR[:, b, :], 0.0).then_inc(s_gz, 1)
                pool.wait_ge(s_gz, n + 1)
                nc.gpsimd.indirect_dma_start(
                    out=GR[:, b, :], out_offset=None, in_=YD[:, :],
                    in_offset=bass.IndirectOffsetOnAxis(ap=IDX[:, k, j:j + 1], axis=0),
                    bounds_check=E * SLOTS - 1, oob_is_err=False,
                ).then_inc(s_gg[b], 16)

        @block.scalar
        def _(act):
            A = nc.scalar.activation
            act.wait_ge(s_var, 1)
            A(SD[:, :], MV1[:, :, 1], ACT.Sqrt).then_inc(s_sd, 1)
            for i in range(NT):
                act.wait_ge(s_xT, i + 1)
                if i >= 3:
                    act.wait_ge(s_xts[i % 3], 16 * (i // 3))
                b = 6 - 2 * (i % 2)
                A(XTR[:, i % 3, 0].rearrange("p (a k) n -> p a (k n)", a=2), PS[:, b:b + 2, 0:375],
                  ACT.Copy).then_inc(s_xth, 1)

            def w1_hi(h):
                if h:
                    act.wait_ge(s_proj, NT * h)
                for k in range(KD):
                    u = w1_use(h, k)
                    act.wait_ge(s_wst[u % 2], 16 * (u // 2 + 1))
                    A(W1S[:, k, 0, :], WST[:, u % 2, 0:C], ACT.Copy, scale=SW).then_inc(s_wh, 1)

            def h_hi(h, i):
                act.wait_ge(s_proj, NT * h + i + 1)
                if h >= 2 and i == 0:
                    act.wait_ge(s_att, 5 * (h - 1))
                A(HB[h % 2][:, i, 0, :], PS[0:T, 6 + i % 2, :], ACT.Copy, scale=1.0 / SW).then_inc(s_hh, 1)

            w1_hi(0)
            for i in range(NT):
                h_hi(0, i)
            act.sem_inc(s_ce, 1)
            with act.Fori(0, NC // GC) as g:
                for c in range(GC):
                    act.wait_ge(s_cm, 1 + g * NJ + sum(len(j) for j in jobs[:c + 1]))
                    A(CT[:, :, bass.ds((GC * g + c) * DC, DC)],
                      PS[0:T, c, 0:KC].rearrange("p (i n) -> p i n", n=DC), ACT.Copy,
                      accum_out=CS[:, bass.ds(GC * g + c, 1)]).then_inc(s_ce, 1)

            def p_branch(h, i):
                q = NT * h + i
                if i == 0:
                    act.wait_ge(s_rows, 16 * (h + 1))
                    act.wait_ge(s_al, h + 1)
                if q >= 3:
                    act.wait_ge(s_p6, q - 2)
                A(TMP[:, q % 3, :], ROW[:, 1, :], ACT.Identity, bias=ALF[:, h, i:i + 1]).then_inc(s_p1, 1)

            def p_exp(h, i):
                q = NT * h + i
                act.wait_ge(s_p2, q + 1)
                A(TMP[:, q % 3, :], TMP[:, q % 3, :], ACT.Exp).then_inc(s_p3, 1)

            def p_hi(h, i):
                q = NT * h + i
                act.wait_ge(s_p4, q + 1)
                if i == 0 and 0 < h <= H:
                    act.wait_ge(s_att, 5 * h)
                if q == 0:
                    act.wait_ge(s_ctok, 1)
                A(P[:, i, 0, :], TMP[:, q % 3, :], ACT.Copy).then_inc(s_p5, 1)

            def p_step(h, i):
                if i < NT:
                    p_branch(h, i)
                if 1 <= i <= NT:
                    p_exp(h, i - 1)
                if 2 <= i:
                    p_hi(h, i - 2)

            def y_step(h, c, b):
                g = CH * h + c
                y = 3 * g + b
                lo, n = BLK[b]
                act.wait_ge(s_y1, y + 1)
                if y >= 2:
                    act.wait_ge(s_y3, y - 1)
                if y == 0:
                    act.wait_ge(s_b1, 16)
                A(RB[:, y % 2, 0:n], YB[:, y % 3, 0:n], ACT.Relu, bias=b1c[:, g:g + 1], scale=1.0 / SX
                  ).then_inc(s_yr, 1)
                A(YB[:, y % 3, 0:n], YB[:, y % 3, 0:n], ACT.Exp, bias=b1c[:, g:g + 1], scale=1.0 / SX
                  ).then_inc(s_y2, 1)

            def y_hi(h, c, b):
                g = CH * h + c
                y = 3 * g + b
                lo, n = BLK[b]
                act.wait_ge(s_y4, y + 1)
                if b == 0 and g >= 2:
                    act.wait_ge(s_h1s[g % 2], 32 * (g // 2))
                    act.wait_ge(s_a2, g - 1)
                A(H1O[:, g % 2, 0, lo:lo + n], YB[:, y % 3, 0:n], ACT.Copy).then_inc(s_y5, 1)

            w1_hi(1)
            for i in range(NT + 2):
                if i < NT:
                    h_hi(1, i)
                p_step(0, i)
            for h in range(H):
                for c in range(CH):
                    for b in range(4):
                        if b < 3:
                            y_step(h, c, b)
                        if b:
                            y_hi(h, c, b - 1)
                    if c == 1 and h + 2 < H:
                        w1_hi(h + 2)
                if h + 1 < H:
                    for i in range(NT + 2):
                        if h + 2 < H and i < NT:
                            h_hi(h + 2, i)
                        p_step(h + 1, i)
            act.wait_ge(s_a2, NCH)
            for b in range(2):
                act.wait_ge(s_h1s[b], 16 * NCH)
            for ch in range(NCH):
                act.wait_ge(s_w2g[ch % 3], 16 * (ch // 3 + 1))
                A(W2S[:, ch, 0, :], W2G[ch % 3][:, :], ACT.Copy, scale=SW).then_inc(s_w2h, 1)

            def h2_hi(j):
                act.wait_ge(s_pj2, j + 1)
                b = 2 * (j % 2)
                A(H2[:, j, 0, 0:D].rearrange("p (a n) -> p a n", a=2), PS[0:T, b:b + 2, 0:DH], ACT.Copy,
                  scale=1.0 / SW).then_inc(s_h2h, 1)

            act.wait_ge(s_w2l, NCH)
            for i in range(NT + 2):
                p_step(H, i)
                if i < NT:
                    h2_hi(i)

            act.wait_ge(s_var2, 1)
            A(SD[:, :], MV[:, :, 1], ACT.Sqrt).then_inc(s_sd2, 1)
            act.wait_ge(s_wrl, 16)
            A(WRS[:, :, 0, :], WRG[:, :, :], ACT.Copy, scale=SW).then_inc(s_wrh, 1)

            def ffn_hi(n):
                act.wait_ge(s_wg, 48 * (n + 1))
                if n >= 2:
                    if n == 2:
                        act.wait_ge(s_sd3, NT)
                    else:
                        act.wait_ge(s_ed, 4 * (n - 2))
                for q in range(3):
                    A(WS[n % 2][:, 0, HALF * q:HALF * q + HALF], WG[:, HALF * q:HALF * q + HALF], ACT.Copy,
                      scale=SW).then_inc(s_wgh, 1)

            ffn_hi(0)
            for i in range(NT):
                act.wait_ge(s_x2t, i + 1)
                b = 2 * (i % 2)
                A(X2T[:, 0, :, T * i:T * i + T].rearrange("p (a k) n -> p a k n", a=2),
                  PS[:, b:b + 2, 0:375].rearrange("p a (k n) -> p a k n", n=T), ACT.Copy).then_inc(s_x2h, 1)
            act.wait_ge(s_lgm, 1)
            A(LG[:, :, :], LG[:, :, :], ACT.Exp).then_inc(s_pe, 1)

            def silu(n, w):
                act.wait_ge(s_gu2, n + 1)
                if n >= 2:
                    act.wait_ge(s_alo, n - 1)
                A(SG[:, n % 2, 0:w], PS[:, 2 * (n % 2), 0:w], ACT.Silu, scale=1.0 / (SX * SW)).then_inc(s_sg, 1)

            def act_hi(n, dst_, w):
                act.wait_ge(s_gx, n + 1)
                A(dst_, SG[:, n % 2, 0:w], ACT.Copy).then_inc(s_ah, 1)

            ffn_hi(1)
            for n in range(10):
                if n < 9:
                    silu(n, BLK[n % 3][1])
                if n:
                    lo, w = BLK[(n - 1) % 3]
                    act_hi(n - 1, AB[:, 0, (n - 1) // 3, lo:lo + w], w)

            def xg_hi(g):
                e, c = divmod(g, 4)
                act.wait_ge(s_xgt, g + 1)
                if c == 0 and e >= 2:
                    act.wait_ge(s_gu2, 9 + KI * (e - 1))
                b = 4 + 2 * (g % 2)
                A(XGT[e % 2][:, 0, :, SC * c:SC * c + SC].rearrange("p (a k) n -> p a k n", a=2),
                  PS[:, b:b + 2, 0:3 * SC].rearrange("p a (k n) -> p a k n", n=SC), ACT.Copy).then_inc(s_xgh, 1)

            for c in range(4):
                xg_hi(c)
            for e in range(E):
                if e + 2 <= E:
                    ffn_hi(e + 2)
                if e + 1 < E:
                    for c in range(4):
                        xg_hi(4 * (e + 1) + c)
                for m in range(KI + 1):
                    n = 9 + KI * e + m
                    if m < KI:
                        silu(n, SLOTS)
                    if m:
                        if m == 1 and e >= 2:
                            act.wait_ge(s_ed, 4 * (e - 1))
                        act_hi(n - 1, AE[e % 2][:, 0, m - 1, :], SLOTS)
                for c in range(4):
                    g = 4 * e + c
                    act.wait_ge(s_ed, g + 1)
                    if g >= 2:
                        act.wait_ge(s_ys[g % 2], 16 * (g // 2))
                    b = 2 * (c % 2)
                    A(YO[:, g % 2, :].rearrange("p (a n) -> p a n", a=2), PS[0:SC, b:b + 2, 0:DH], ACT.Copy,
                      scale=1.0 / (SA * SW)).then_inc(s_yo, 1)

        @block.vector
        def _(dve):
            V = nc.vector
            made = [0]

            def link(ins):
                made[0] += 1
                ins.then_inc(s_dve, 1)
                dve.wait_ge(s_dve, made[0])

            dve.wait_ge(s_edges, 32)
            link(V.tensor_copy(EF[:, :, :], ED[:, :, :, :].rearrange("q s a p -> q s (a p)")))
            link(V.tensor_scalar(EQ[:, 0, :], EF[:, 0, :], 1.0 / T, 0.5 / T - 0.5, ALU.mult, ALU.add))
            link(V.tensor_scalar(EQ[:, 1, :], EF[:, 1, :], 1.0 / DC, 0.5 / DC - 0.5, ALU.mult, ALU.add))
            link(V.tensor_copy(EG[:, :, :], EQ[:, :, :]))
            link(V.scalar_tensor_tensor(EK[:, 1, :], EG[:, 0, :], -float(T), EF[:, 0, :], ALU.mult, ALU.add))
            link(V.scalar_tensor_tensor(EK[:, 0, :], EG[:, 1, :], 1000.0 - DC, EF[:, 1, :], ALU.mult, ALU.add))
            V.scalar_tensor_tensor(EK[:, 0, :], EG[:, 0, :], float(DC), EK[:, 0, :], ALU.mult, ALU.add
                                   ).then_inc(s_keys, 1)
            dve.wait_ge(s_const, 15)
            link(V.tensor_scalar(QI[:, :], MX[:, :], 1.0 / DC, 0.5 / DC - 0.5, ALU.mult, ALU.add))
            link(V.tensor_copy(MM[:, :], QI[:, :]))
            link(V.scalar_tensor_tensor(KEY[:, KT:KA], MM[:, :], 1000.0 - DC, ZZ[:, :], ALU.mult, ALU.add))
            dve.wait_ge(s_keyT, 1)
            link(V.tensor_copy(KEY[:, PADT:PADT + ET], PS[0:T, 7, 0:ET]))
            link(V.tensor_copy(SLO[:, PADT:PADT + ET], PS[0:T, 7, ET:2 * ET]))

            def norm(X, BSt, MVt, s_in, n_in, s_v, s_d):
                for i in range(NT):
                    if s_in is not None:
                        dve.wait_ge(s_in, n_in if n_in else i + 1)
                    for a in range(2):
                        V.bn_stats(BSt[:, i, a, :], X[:, i, DH * a:DH * a + DH]).then_inc(s_dve, 1)
                        made[0] += 1
                dve.wait_ge(s_dve, made[0])
                for i in range(NT):
                    V.bn_aggr(MVt[:, i, :], BSt[:, i, :, :].rearrange("p a s -> p (a s)")).then_inc(s_dve, 1)
                    made[0] += 1
                dve.wait_ge(s_dve, made[0])
                V.tensor_scalar(MVt[:, :, 1], MVt[:, :, 1], EPS, None, ALU.add).then_inc(s_v, 1)
                dve.wait_ge(s_d, 1)
                link(V.reciprocal(SD[:, :], SD[:, :]))
                link(V.tensor_scalar(SD[:, :], SD[:, :], SX, None, ALU.mult))

            norm(XA, BS1, MV1, s_x, 16, s_var, s_sd)
            for i in range(NT):
                V.tensor_scalar(XA[:, i, :], XA[:, i, :], MV1[:, i, 0:1], SD[:, i:i + 1], ALU.subtract, ALU.mult
                                ).then_inc(s_xn, 1)
            for i in range(NT):
                dve.wait_ge(s_xth, i + 1)
                b = 6 - 2 * (i % 2)
                V.tensor_tensor(XTR[:, i % 3, 1].rearrange("p (a k) n -> p a (k n)", a=2), PS[:, b:b + 2, 0:375],
                                XTR[:, i % 3, 0].rearrange("p (a k) n -> p a (k n)", a=2), ALU.subtract
                                ).then_inc(s_xtl, 1)

            def w1_lo(h):
                for k in range(KD):
                    u = w1_use(h, k)
                    dve.wait_ge(s_wh, KD * h + k + 1)
                    V.scalar_tensor_tensor(W1S[:, k, 1, :], WST[:, u % 2, 0:C], SW, W1S[:, k, 0, :], ALU.mult,
                                           ALU.subtract).then_inc(s_wl, 1)

            def h_lo(h, i):
                q = NT * h + i
                if i == 0:
                    dve.wait_ge(s_arep, 32 * (h + 1))
                dve.wait_ge(s_hh, q + 1)
                for a in range(2):
                    V.tensor_tensor_reduce(JNK[:, :], PS[0:T, 6 + i % 2, :], AR1[:, h % 2, a, :],
                                           1.0 / (SX * SW), 0.0, ALU.mult, ALU.add, AL[:, a, h, i:i + 1]
                                           ).then_inc(s_dve, 1)
                    made[0] += 1
                    dve.wait_ge(s_dve, made[0])
                V.scalar_tensor_tensor(HB[h % 2][:, i, 1, :], PS[0:T, 6 + i % 2, :], 1.0 / SW,
                                       HB[h % 2][:, i, 0, :], ALU.mult, ALU.subtract).then_inc(s_hl, 1)

            w1_lo(0)
            for i in range(NT):
                h_lo(0, i)

            dve.wait_ge(s_xT, NT)
            with dve.Fori(0, KA // 4) as t:
                for u in range(4):
                    V.tensor_scalar(OL[:, bass.ds(4 * t + u, 1), :], iot[:, :].rearrange("p (o n) -> p o n", o=1),
                                    SLO[:, bass.ds(4 * t + u, 1)], None, ALU.is_equal).then_inc(s_ol, 1)
            with dve.Fori(0, NC // GC) as g:
                n = 0
                for c in range(GC):
                    for kind, t in jobs[c]:
                        col = (t + GT * g) if kind == "e" else (KT + t + 2 * g)
                        if n >= 4:
                            dve.wait_ge(s_cm, g * NJ + n - 2)
                        else:
                            dve.wait_ge(s_cm, g * NJ + 1)
                        V.tensor_scalar(OR[:, n % 4, :], iok[:, :], 1000.0 * c, KEY[:, bass.ds(col, 1)],
                                        ALU.add, ALU.is_equal).then_inc(s_or, 1)
                        n += 1
                dve.wait_ge(s_or, (g + 1) * NJ)
                V.tensor_scalar(KEY[:, :], KEY[:, :], -1000.0 * GC, None, ALU.add).then_inc(s_k2, 1)
                dve.wait_ge(s_k2, g + 1)
            dve.wait_ge(s_ce, 1 + NC)
            V.tensor_reduce(MX[:, 0:1], CS[:, :], AX.X, ALU.add).then_inc(s_cs, 1)
            dve.wait_ge(s_ct1, 1)
            V.tensor_copy(flag[:, :], PS[:, 7, 0:1]).then_inc(s_flag, 1)
            dve.wait_ge(s_flag, 1)
            total = dve.value_load(flag[0:1, 0:1])
            with dve.If(total != TOTAL):
                V.tensor_scalar(KEY[:, :], KEY[:, :], 1000.0 * NC, None, ALU.add).then_inc(s_gk, 1)
                dve.wait_ge(s_gk, 1)
                with dve.Fori(0, NC) as c:
                    with dve.Fori(0, KA // 2) as t:
                        for u in range(2):
                            dve.wait_ge(s_gu, 1 + c * KA + 2 * t + u)
                            V.tensor_scalar(OR[:, u, :], iok[:, :], 0.0, KEY[:, bass.ds(2 * t + u, 1)],
                                            ALU.add, ALU.is_equal).then_inc(s_go, 1)
                    dve.wait_ge(s_gd, c + 1)
                    V.tensor_copy(CT[:, :, bass.ds(c * DC, DC)],
                                  PS[0:T, 5, 0:KC].rearrange("p (i n) -> p i n", n=DC)).then_inc(s_gk, 1)
                    V.tensor_scalar(KEY[:, :], KEY[:, :], -1000.0, None, ALU.add).then_inc(s_gk, 1)
                    dve.wait_ge(s_gk, 2 * c + 3)
            V.tensor_copy(MX[:, 0:1], CS[:, 0:1]).then_inc(s_ctok, 1)

            for j in range(NT):
                dve.wait_ge(s_mt, j + 1)
                if j >= 2:
                    dve.wait_ge(s_ms[j % 2], 16 * (j // 2))
                b = 2 * (j % 3)
                V.tensor_scalar(MSK[:, j % 2, :].rearrange("p (a i n) -> p a i n", a=2, n=T),
                                blocks16(PH, T, b), 0.0, NEG, ALU.is_equal, ALU.mult).then_inc(s_mm, 1)

            dve.wait_ge(s_a2v, 32)
            for ch in range(NCH):
                u = v2_use(ch)
                dve.wait_ge(s_wst[u % 2], 16 * (u // 2 + 1))
                dve.wait_ge(s_wl, u)
                for a in range(2):
                    ins = V.tensor_tensor_reduce(VJ[:, :], WST[:, u % 2, :], A2R[:, a, :], SW, 0.0, ALU.mult,
                                                 ALU.add, V2F[:, ch, a:a + 1])
                    if a == 0:
                        link(ins)
                ins.then_inc(s_wl, 1)
            dve.wait_ge(s_wl, KD + NCH)
            link(V.tensor_copy(V2S[:, :, 0, :], V2F[:, :, :]))
            link(V.tensor_tensor(V2S[:, :, 1, :], V2F[:, :, :], V2S[:, :, 0, :], ALU.subtract))
            link(V.memset(A2C[:, :], 0.0))

            def chain_row(h):
                dve.wait_ge(s_alt, h + 1)
                if h:
                    dve.wait_ge(s_aad, 16 * h)
                V.tensor_copy(TR[0:NT, :], PS[0:NT, 6, 0:T]).then_inc(s_alc, 1)

            def chain_max(h, js):
                if js[0] == 0:
                    dve.wait_ge(s_row, 16 * (h + 1))
                for j in js:
                    n = NT * h + j
                    dve.wait_ge(s_ml[j % 2], 16 * (n // 2 + 1))
                    V.tensor_tensor_reduce(MSK[:, j % 2, :], MSK[:, j % 2, :], ROW[:, 0, :], 1.0, 3.0 * NEG,
                                           ALU.add, ALU.max, MX[:, j:j + 1]).then_inc(s_mu, 1)

            def chain_shift(h):
                dve.wait_ge(s_mu, NT * (h + 1))
                aD = AL[:, 1, h, :]
                link(V.tensor_tensor(ZZ[:, :], MX[:, :], aD, ALU.add))
                link(V.scalar_tensor_tensor(MM[:, :], ZZ[:, :], SLOPE, ZZ[:, :], ALU.mult, ALU.max))
                link(V.tensor_tensor(AA[:, 0, :], aD, MM[:, :], ALU.subtract))
                V.scalar_tensor_tensor(AA[:, 1, :], aD, SLOPE, MM[:, :], ALU.mult, ALU.subtract).then_inc(s_aa, 1)
                V.tensor_scalar(ALF[:, h, :], AL[:, 0, h, :], SLOPE, None, ALU.mult).then_inc(s_al, 1)

            def chain_shift_rows(h):
                dve.wait_ge(s_aat, h + 1)
                dve.wait_ge(s_ald, 16 * (h + 1))
                V.tensor_copy(TR[:, :], PS[0:2 * NT, 6, 0:T]).then_inc(s_aac, 1)

            def p_leaky(h, i):
                q = NT * h + i
                dve.wait_ge(s_p1, q + 1)
                V.scalar_tensor_tensor(TMP[:, q % 3, :], ROW[:, 0, :], AL[:, 0, h, i:i + 1], TMP[:, q % 3, :],
                                       ALU.add, ALU.max).then_inc(s_p2, 1)

            def p_count(h, i):
                q = NT * h + i
                dve.wait_ge(s_p3, q + 1)
                V.scalar_tensor_tensor(TMP[:, q % 3, :], TMP[:, q % 3, :], 1.0, CT[:, i, :], ALU.min, ALU.mult
                                       ).then_inc(s_p4, 1)

            def p_step(h, i):
                if i < NT:
                    p_leaky(h, i)
                if 1 <= i <= NT:
                    p_count(h, i - 1)

            chain_row(0)
            chain_max(0, range(NT))
            chain_shift(0)
            chain_shift_rows(0)
            w1_lo(1)
            for i in range(NT + 1):
                if i < NT:
                    h_lo(1, i)
                p_step(0, i)

            def att_read(h, c):
                a = 5 * h + c + 1
                t = 3 * (a % 2)
                dve.wait_ge(s_att, a + 1)
                for b, (lo, n) in enumerate(BLK):
                    if c < 0:
                        ins = V.reciprocal(RDEN[:, lo:lo + n], PS[:, t + b, 0:n])
                        ins.then_inc(s_rd, 1)
                    else:
                        y = 3 * (CH * h + c) + b
                        if y >= 3:
                            dve.wait_ge(s_y6, y - 2)
                        V.tensor_tensor(YB[:, y % 3, 0:n], PS[:, t + b, 0:n], RDEN[:, lo:lo + n], ALU.mult
                                        ).then_inc(s_y1, 1)

            def y_elu(h, c, b):
                y = 3 * (CH * h + c) + b
                n = BLK[b][1]
                dve.wait_ge(s_y2, y + 1)
                V.scalar_tensor_tensor(YB[:, y % 3, 0:n], YB[:, y % 3, 0:n], 1.0, RB[:, y % 2, 0:n], ALU.min,
                                       ALU.add).then_inc(s_y3, 1)

            def a2_add(g):
                dve.wait_ge(s_a2, g + 1)
                if g:
                    dve.wait_ge(s_a2r, g)
                V.tensor_tensor(A2C[:, :], A2C[:, :], PS[0:T, 7, 0:2 * NT], ALU.add).then_inc(s_a2r, 1)

            for h in range(H):
                att_read(h, -1)
                if h + 1 < H:
                    chain_row(h + 1)
                for c in range(CH):
                    dve.wait_ge(s_rd, 3 * (h + 1))
                    att_read(h, c)
                    for b in range(3):
                        y_elu(h, c, b)
                    if c:
                        a2_add(CH * h + c - 1)
                    if h + 1 < H:
                        if c == 0:
                            chain_max(h + 1, range(NT // 2))
                        if c == 1:
                            chain_max(h + 1, range(NT // 2, NT))
                            chain_shift(h + 1)
                            if h + 2 < H:
                                w1_lo(h + 2)
                        if c == 2:
                            chain_shift_rows(h + 1)
                a2_add(CH * h + CH - 1)
                dve.wait_ge(s_a2r, CH * (h + 1))
                if h + 1 < H:
                    for i in range(NT + 1):
                        if i < NT and h + 2 < H:
                            h_lo(h + 2, i)
                        p_step(h + 1, i)

            link(V.tensor_scalar(AL[:, 0, H, :], A2C[:, 0:2 * NT:2], 1.0 / (SX * SW), None, ALU.mult))
            V.tensor_scalar(AL[:, 1, H, :], A2C[:, 1:2 * NT:2], 1.0 / (SX * SW), None, ALU.mult).then_inc(s_al4, 1)
            dve.wait_ge(s_al4, 1)
            for ch in range(NCH):
                dve.wait_ge(s_w2h, ch + 1)
                V.scalar_tensor_tensor(W2S[:, ch, 1, :], W2G[ch % 3][:, :], SW, W2S[:, ch, 0, :], ALU.mult,
                                       ALU.subtract).then_inc(s_w2l, 1)
            dve.wait_ge(s_att, 5 * H)
            V.memset(H2[:, :, 0, D:D + 1], 1.0).then_inc(s_h2o, 1)
            V.memset(H2[:, :, 1, D:D + 1], 0.0).then_inc(s_h2o, 1)
            chain_row(H)
            chain_max(H, range(NT))
            chain_shift(H)
            chain_shift_rows(H)

            def h2_lo(j):
                dve.wait_ge(s_h2h, j + 1)
                b = 2 * (j % 2)
                V.scalar_tensor_tensor(H2[:, j, 1, 0:D].rearrange("p (a n) -> p a n", a=2),
                                       PS[0:T, b:b + 2, 0:DH], 1.0 / SW,
                                       H2[:, j, 0, 0:D].rearrange("p (a n) -> p a n", a=2), ALU.mult,
                                       ALU.subtract).then_inc(s_h2l, 1)

            for i in range(NT + 1):
                p_step(H, i)
                if i < NT:
                    h2_lo(i)
            for j in range(NT):
                dve.wait_ge(s_at2, j + 1)
                b = 4 + 2 * (j % 2)
                link(V.reciprocal(ZZ[:, j:j + 1], PS[0:T, b + 1, DH - 1:DH]))
                link(V.tensor_scalar(ZZ[:, j:j + 1], ZZ[:, j:j + 1], 1.0 / SX, None, ALU.mult))
                dve.wait_ge(s_xb, NT)
                link(V.scalar_tensor_tensor(X2[:, j, 0:DH + 1], PS[0:T, b, 0:DH + 1], ZZ[:, j:j + 1],
                                            X2[:, j, 0:DH + 1], ALU.mult, ALU.add))
                V.scalar_tensor_tensor(X2[:, j, DH + 1:D], PS[0:T, b + 1, 0:DH - 1], ZZ[:, j:j + 1],
                                       X2[:, j, DH + 1:D], ALU.mult, ALU.add).then_inc(s_x2, 1)

            norm(X2, BS, MV, s_x2, 0, s_var2, s_sd2)
            for i in range(NT):
                V.tensor_scalar(XN2[:, i, :], X2[:, i, :], MV[:, i, 0:1], SD[:, i:i + 1], ALU.subtract, ALU.mult
                                ).then_inc(s_xn2, 1)
            dve.wait_ge(s_wrh, 1)
            V.scalar_tensor_tensor(WRS[:, :, 1, :], WRG[:, :, :], SW, WRS[:, :, 0, :], ALU.mult, ALU.subtract
                                   ).then_inc(s_wrs, 1)

            def ffn_lo(n):
                for q in range(3):
                    dve.wait_ge(s_wgh, 3 * n + q + 1)
                    V.scalar_tensor_tensor(WS[n % 2][:, 1, HALF * q:HALF * q + HALF],
                                           WG[:, HALF * q:HALF * q + HALF], SW,
                                           WS[n % 2][:, 0, HALF * q:HALF * q + HALF], ALU.mult, ALU.subtract
                                           ).then_inc(s_wgl, 1)

            ffn_lo(0)
            for i in range(NT):
                dve.wait_ge(s_x2h, i + 1)
                b = 2 * (i % 2)
                V.tensor_tensor(X2T[:, 1, :, T * i:T * i + T].rearrange("p (a k) n -> p a k n", a=2),
                                PS[:, b:b + 2, 0:375].rearrange("p a (k n) -> p a k n", n=T),
                                X2T[:, 0, :, T * i:T * i + T].rearrange("p (a k) n -> p a k n", a=2),
                                ALU.subtract).then_inc(s_x2lo, 1)
            dve.wait_ge(s_lg, 1)
            dve.wait_ge(s_const, 20)
            link(V.tensor_scalar(LG[:, :, :], PS[0:T, 7, 0:NT * E].rearrange("p (j e) -> p j e", e=E),
                                 1.0 / (SX * SW), None, ALU.mult))
            link(V.tensor_reduce(RK[:, 0, :], LG[:, :, :], AX.X, ALU.max))
            V.tensor_tensor(LG[:, :, :], LG[:, :, :], RK[:, 0, :].unsqueeze(2).to_broadcast([T, NT, E]),
                            ALU.subtract).then_inc(s_lgm, 1)

            def gate_up(n, w):
                dve.wait_ge(s_sg, n + 1)
                V.scalar_tensor_tensor(SG[:, n % 2, 0:w], PS[:, 2 * (n % 2) + 1, 0:w], SA / (SX * SW),
                                       SG[:, n % 2, 0:w], ALU.mult, ALU.mult).then_inc(s_gx, 1)

            ffn_lo(1)
            dve.wait_ge(s_pe, 1)
            link(V.tensor_reduce(RK[:, 0, :], LG[:, :, :], AX.X, ALU.add))
            link(V.reciprocal(RK[:, 1, :], RK[:, 0, :]))
            link(V.tensor_tensor(LG[:, :, :], LG[:, :, :], RK[:, 1, :].unsqueeze(2).to_broadcast([T, NT, E]),
                                 ALU.mult))
            for j in range(NT):
                link(V.max(M8[:, j, :], LG[:, j, :]))
                link(V.max_index(I8[:, j, :], M8[:, j, :], LG[:, j, :]))
            link(V.tensor_copy(IK[:, 0, :], I8[:, :, 0]))
            link(V.tensor_copy(IK[:, 1, :], I8[:, :, 1]))
            link(V.tensor_tensor(RK[:, 0, :], M8[:, :, 0], M8[:, :, 1], ALU.add))
            link(V.tensor_scalar(RK[:, 0, :], RK[:, 0, :], 1e-9, None, ALU.max))
            link(V.reciprocal(RK[:, 1, :], RK[:, 0, :]))
            for k in range(2):
                link(V.tensor_tensor(WK[:, k, :], M8[:, :, k], RK[:, 1, :], ALU.mult))
                link(V.tensor_tensor(OK[k][:, :, :], io8[:, :].unsqueeze(1).to_broadcast([T, NT, E]),
                                     IK[:, k, :].unsqueeze(2).to_broadcast([T, NT, E]), ALU.is_equal))
                link(V.tensor_tensor(OT[k][:, :, :], OK[k][:, :, :],
                                     tokid[:, :].unsqueeze(2).to_broadcast([T, NT, E]), ALU.mult))
                for r in range(3):
                    link(V.tensor_copy(O3[k][:, :, E * r:E * r + E], OK[k][:, :, :]))
            link(V.tensor_tensor(SS[:, :, :], OK[0][:, :, :], WK[:, 0, :].unsqueeze(2).to_broadcast([T, NT, E]),
                                 ALU.mult))
            link(V.tensor_tensor(LG[:, :, :], OK[1][:, :, :], WK[:, 1, :].unsqueeze(2).to_broadcast([T, NT, E]),
                                 ALU.mult))
            link(V.tensor_tensor(SS[:, :, :], SS[:, :, :], LG[:, :, :], ALU.add))
            link(V.tensor_tensor(LG[:, :, :], OK[0][:, :, :], OK[1][:, :, :], ALU.add))
            link(V.tensor_scalar(LG[:, :, :], LG[:, :, :], -1.0, None, ALU.add))
            link(V.tensor_tensor(SS[:, :, :], SS[:, :, :], LG[:, :, :], ALU.add))
            for r in range(2):
                link(V.tensor_copy(S3[:, :, E * r:E * r + E], SS[:, :, :]))
                link(V.tensor_tensor(SS[:, :, :], SS[:, :, :], S3[:, :, E * r:E * r + E], ALU.subtract))
            link(V.memset(CA[:, :, :, :], 0.0))
            V.tensor_copy(S3[:, :, 2 * E:3 * E], SS[:, :, :]).then_inc(s_s3, 1)
            for n in range(9):
                gate_up(n, BLK[n % 3][1])
            for n in range(3):
                dve.wait_ge(s_s3t, n + 1)
                dve.wait_ge(s_xns, 16 * NT)
                dve.wait_ge(s_x2t, NT)
                V.tensor_copy([S3T, O3T[0], O3T[1]][n][:, :].rearrange("p (a j n) -> p a j n", a=2, n=T),
                              blocks16(PB, 24, 2 * n)).then_inc(s_s3c, 1)

            def rank(r):
                j, k = divmod(r, 2)
                t = 3 * (r % 2)
                R = PSF[0:T, 512 * t:512 * t + N]
                own = WK[:, k, j:j + 1]
                dve.wait_ge(s_rr, r + 1)
                if r:
                    dve.wait_ge(s_rk, r)
                if j:
                    V.tensor_scalar(JN2[:, 0:T * j], R[:, 0:T * j], own, None, ALU.is_ge, ALU.add,
                                    accum_out=CA[:, 0, k, j:j + 1]).then_inc(s_dve, 1)
                    made[0] += 1
                    dve.wait_ge(s_dve, made[0])
                link(V.tensor_scalar(JN2[:, T * j:N], R[:, T * j:N], own, None, ALU.is_gt, ALU.add,
                                     accum_out=CA[:, 1, k, j:j + 1]))
                V.scalar_tensor_tensor(JN2[:, 0:T], R[:, T * j:T * j + T], own, TRI[:, :], ALU.is_equal, ALU.mult,
                                       accum_out=CA[:, 2, k, j:j + 1]).then_inc(s_rk, 1)

            def shared_add(j):
                dve.wait_ge(s_sd3, j + 1)
                V.scalar_tensor_tensor(X2[:, j, :].rearrange("p (a n) -> p a n", a=2), PS[0:T, 6:8, 0:DH],
                                       1.0 / (SA * SW), X2[:, j, :].rearrange("p (a n) -> p a n", a=2),
                                       ALU.mult, ALU.add).then_inc(s_sdr, 1)

            dve.wait_ge(s_gu2, 9)
            for j in range(NT):
                rank(2 * j)
                rank(2 * j + 1)
                shared_add(j)
            dve.wait_ge(s_rk, 2 * NT)
            link(V.tensor_tensor(RK[:, :, :], CA[:, 0, :, :], CA[:, 1, :, :], ALU.add))
            link(V.tensor_tensor(RK[:, :, :], RK[:, :, :], CA[:, 2, :, :], ALU.add))
            for k in range(2):
                for j in range(NT):
                    V.tensor_scalar(IND[:, k, j, :], io392[:, :], RK[:, k, j:j + 1], None, ALU.is_equal
                                    ).then_inc(s_ind, 1)
            link(V.tensor_scalar(CA[:, 0, :, :], RK[:, :, :], float(CAP), 1.0e6, ALU.is_ge, ALU.mult))
            link(V.tensor_tensor(RK[:, :, :], RK[:, :, :], CA[:, 0, :, :], ALU.add))
            link(V.scalar_tensor_tensor(CA[:, 1, :, :], IK[:, :, :], float(SLOTS), RK[:, :, :], ALU.mult, ALU.add))
            link(V.tensor_copy(IDX[:, :, :], CA[:, 1, :, :]))
            dve.wait_ge(s_tk, 1)
            V.tensor_copy(TOK[:, :, :], PS[0:SC, 7, 0:4 * E].rearrange("p (c e) -> p c e", e=E)).then_inc(s_tok, 1)

            def xg_lo(g):
                e, c = divmod(g, 4)
                dve.wait_ge(s_xgh, g + 1)
                b = 4 + 2 * (g % 2)
                for a in range(2):
                    ins = V.tensor_tensor(XGT[e % 2][:, 1, 3 * a:3 * a + 3, SC * c:SC * c + SC],
                                          PS[:, b + a, 0:3 * SC].rearrange("p (k n) -> p k n", n=SC),
                                          XGT[e % 2][:, 0, 3 * a:3 * a + 3, SC * c:SC * c + SC], ALU.subtract)
                    ins.then_inc(s_xgl, 1)

            for c in range(4):
                xg_lo(c)
            for e in range(E):
                if e + 2 <= E:
                    ffn_lo(e + 2)
                if e + 1 < E:
                    for c in range(4):
                        xg_lo(4 * (e + 1) + c)
                for m in range(KI):
                    gate_up(9 + KI * e + m, SLOTS)
            for n in range(2 * NT):
                j, k = divmod(n, 2)
                b = n % 4
                dve.wait_ge(s_gg[b], 16 * (n // 4 + 1))
                if n:
                    dve.wait_ge(s_g1, n)
                V.scalar_tensor_tensor(X2[:, j, :], GR[:, b, :], WK[:, k, j:j + 1], X2[:, j, :], ALU.mult, ALU.add
                                       ).then_inc(s_g1, 1)

        @block.tensor
        def _(pe):
            M = nc.tensor.matmul

            def mm3(out_, lhs, rhs, first, last):
                for a, b in ((0, 0), (0, 1), (1, 0)):
                    ins = M(out_, lhs(a), rhs(b), start=first and a + b == 0, stop=last and a == 1)
                return ins

            pe.wait_ge(s_const, 15)
            pe.wait_ge(s_keys, 1)
            for a in range(2):
                for q in range(2):
                    ins = nc.tensor.transpose(PS[0:T, 7, ET * a + 85 * q:ET * a + 85 * q + 85],
                                              EK[:, a, T * q:T * q + T], idf[0:85, 0:85])
            ins.then_inc(s_keyT, 1)
            for i in range(NT):
                pe.wait_ge(s_xn, i + 1)
                if i == 0:
                    pe.wait_ge(s_xn, NT)
                if i >= 2:
                    pe.wait_ge(s_xtl, i - 1)
                b = 6 - 2 * (i % 2)
                for k in range(KD):
                    ins = nc.tensor.transpose(PS[:, b + k // 3, T * (k % 3):T * (k % 3) + T],
                                              XA[:, i, 128 * k:128 * k + 128], idf[0:T, 0:T])
                ins.then_inc(s_xT, 1)

            def proj(h):
                pe.wait_ge(s_wl, w1_use(h, KD - 1) + 1)
                for i in range(NT):
                    v = NT + NT * h + i
                    pe.wait_ge(s_xts[v % 3], 16 * (v // 3 + 1))
                    if i == 0 and h == 0:
                        pe.wait_ge(s_xtl, NT)
                    if NT * h + i >= 2:
                        pe.wait_ge(s_hl, NT * h + i - 1)
                    if i < 2 and h:
                        pe.wait_ge(s_alc, h)
                        if h >= 2:
                            pe.wait_ge(s_a2r, CH * (h - 1))
                    for k in range(KD):
                        ins = mm3(PS[0:T, 6 + i % 2, :], lambda a: XTR[:, v % 3, a, k, :],
                                  lambda b: W1S[:, k, b, :], k == 0, k == KD - 1)
                    ins.then_inc(s_proj, 1)

            def chain_row(h):
                if h < H:
                    pe.wait_ge(s_hl, NT * (h + 1))
                else:
                    pe.wait_ge(s_al4, 1)
                nc.tensor.transpose(PS[0:NT, 6, 0:T], AL[:, 0, h, :], idf[0:T, 0:T]).then_inc(s_alt, 1)

            def chain_shift(h):
                pe.wait_ge(s_aa, h + 1)
                nc.tensor.transpose(PS[0:2 * NT, 6, 0:T], AA[:, :, :].rearrange("p a i -> p (a i)"),
                                    idf[0:T, 0:T]).then_inc(s_aat, 1)

            proj(0)
            pe.wait_ge(s_ol, KA)
            pe.sem_inc(s_cm, 1)
            pe.sem_inc(s_gu, 1)
            with pe.Fori(0, NC // GC) as g:
                n = 0
                for c in range(GC):
                    pe.wait_ge(s_ce, 1 + GC * g)
                    for q, (kind, t) in enumerate(jobs[c]):
                        col = (t + GT * g) if kind == "e" else (KT + t + 2 * g)
                        pe.wait_ge(s_or, g * NJ + n + 1)
                        ins = M(PS[0:T, c, 0:KC], OL[:, bass.ds(col, 1), :], OR[:, n % 4, :], start=q == 0,
                                stop=q == len(jobs[c]) - 1)
                        ins.then_inc(s_cm, 1)
                        n += 1
            pe.wait_ge(s_cs, 1)
            M(PS[:, 7, 0:1], onesf[:, :], MX[:, 0:1], start=True, stop=True).then_inc(s_ct1, 1)
            pe.wait_ge(s_flag, 1)
            total = pe.value_load(flag[0:1, 0:1])
            with pe.If(total != TOTAL):
                with pe.Fori(0, NC) as c:
                    pe.wait_ge(s_gk, 2 * c + 1)
                    M(PS[0:T, 5, 0:KC], OL[:, 0, :], iok[:, :], start=True, stop=False)
                    with pe.Fori(0, KA // 2) as t:
                        for u in range(2):
                            pe.wait_ge(s_go, c * KA + 2 * t + u + 1)
                            M(PS[0:T, 5, 0:KC], OL[:, bass.ds(2 * t + u, 1), :], OR[:, u, :], start=False,
                              stop=False).then_inc(s_gu, 1)
                    M(PS[0:T, 5, 0:KC], OL[:, 0, :], iok[:, :], start=False, stop=True).then_inc(s_gd, 1)
            pe.wait_ge(s_ctok, 1)
            for j in range(NT):
                if j >= 3:
                    pe.wait_ge(s_mm, j - 2)
                b = 2 * (j % 3)
                for i in range(NT):
                    ins = nc.tensor.transpose(PH[0:T, col16(b, i):col16(b, i) + T], CT[:, i, T * j:T * j + T], idh[0:T, 0:T])
                ins.then_inc(s_mt, 1)
            chain_row(0)
            chain_shift(0)
            pe.wait_ge(s_aac, 1)
            proj(1)

            def att(h, c):
                a_ = 5 * h + c + 1
                t = 3 * (a_ % 2)
                if a_ >= 2:
                    g2 = a_ - 2
                    h0, c0 = divmod(g2, 5)
                    if c0 == 0:
                        pe.wait_ge(s_rd, 3 * (h0 + 1))
                    else:
                        pe.wait_ge(s_y1, 3 * (CH * h0 + c0))
                else:
                    pe.wait_ge(s_mm, NT)
                for i in range(NT):
                    if c < 0:
                        pe.wait_ge(s_p6, NT * h + i + 1)
                        for b, (lo, n) in enumerate(BLK):
                            for part in range(2):
                                ins = M(PS[:, t + b, 0:n], ones[:, :], P[:, i, part, lo:lo + n],
                                        start=i == 0 and part == 0, stop=i == NT - 1 and part == 1)
                    else:
                        hb = HB[h % 2]
                        for pa, pb in ((0, 0), (0, 1), (1, 0)):
                            for b, (lo, n) in enumerate(BLK):
                                ins = M(PS[:, t + b, 0:n], hb[:, i, pa, 128 * c:128 * c + 128],
                                        P[:, i, pb, lo:lo + n], start=i == 0 and pa + pb == 0,
                                        stop=i == NT - 1 and pa == 1)
                ins.then_inc(s_att, 1)

            def al2(g):
                pe.wait_ge(s_y6, 3 * (g + 1))
                if g:
                    pe.wait_ge(s_a2r, g)
                else:
                    pe.wait_ge(s_hl, 2 * NT)
                for j in range(NT):
                    ins = mm3(PS[0:T, 7, 2 * j:2 * j + 2], lambda a: H1O[:, g % 2, a, T * j:T * j + T],
                              lambda b: V2S[:, g, b, :], True, True)
                ins.then_inc(s_a2, 1)

            for h in range(H):
                if h + 1 < H:
                    chain_row(h + 1)
                att(h, -1)
                for c in range(CH):
                    att(h, c)
                    if c:
                        al2(CH * h + c - 1)
                    if c == 2 and h + 1 < H:
                        chain_shift(h + 1)
                al2(CH * h + CH - 1)
                if h + 2 < H:
                    pe.wait_ge(s_aac, h + 2)
                    proj(h + 2)

            chain_row(H)
            for j in range(NT):
                pe.wait_ge(s_ht[j % 2], 16 * (j // 2 + 1))
                if j == 0:
                    pe.wait_ge(s_w2l, NCH)
                    pe.wait_ge(s_y1, 3 * NCH)
                if j >= 2:
                    pe.wait_ge(s_h2l, j - 1)
                b = 2 * (j % 2)
                for ch in range(NCH):
                    for q in range(2):
                        ins = mm3(PS[0:T, b + q, 0:DH], lambda a: HT[j % 2][:, a, ch, :],
                                  lambda r: W2S[:, ch, r, DH * q:DH * q + DH], ch == 0, ch == NCH - 1)
                ins.then_inc(s_pj2, 1)
                if j == 1:
                    chain_shift(H)
            pe.wait_ge(s_h2o, 2)
            pe.wait_ge(s_aac, H + 1)
            for j in range(NT):
                if j >= 2:
                    pe.wait_ge(s_x2, j - 1)
                b = 4 + 2 * (j % 2)
                for i in range(NT):
                    if j == 0:
                        pe.wait_ge(s_p6, NT * H + i + 1)
                        pe.wait_ge(s_h2l, i + 1)
                    for q, (lo, n) in enumerate(((0, DH + 1), (DH + 1, DH))):
                        ins = mm3(PS[0:T, b + q, 0:n], lambda a: P[:, i, a, T * j:T * j + T],
                                  lambda r: H2[:, i, r, lo:lo + n], i == 0, i == NT - 1)
                ins.then_inc(s_at2, 1)

            for i in range(NT):
                pe.wait_ge(s_xn2, i + 1)
                if i >= 2:
                    pe.wait_ge(s_x2lo, i - 1)
                b = 2 * (i % 2)
                for k in range(KD):
                    ins = nc.tensor.transpose(PS[:, b + k // 3, T * (k % 3):T * (k % 3) + T],
                                              XN2[:, i, 128 * k:128 * k + 128], idf[0:T, 0:T])
                ins.then_inc(s_x2t, 1)
            pe.wait_ge(s_x2lo, NT)
            pe.wait_ge(s_wrs, 1)
            for j in range(NT):
                for k in range(KD):
                    ins = mm3(PS[0:T, 7, E * j:E * j + E], lambda a: X2T[:, a, k, T * j:T * j + T],
                              lambda r: WRS[:, k, r, :], k == 0, k == KD - 1)
            ins.then_inc(s_lg, 1)

            def gate_up(n, wb, rhs, w, m):
                if n >= 2:
                    pe.wait_ge(s_gx, n - 1)
                for q in range(2):
                    for k in range(KD):
                        ins = mm3(PS[:, 2 * (n % 2) + q, 0:w],
                                  lambda a: wb[:, a, HALF * q + INNER * k + 128 * m:HALF * q + INNER * k + 128 * m + 128],
                                  lambda r: rhs(r, k), k == 0, k == KD - 1)
                ins.then_inc(s_gu2, 1)

            pe.wait_ge(s_wgl, 3)
            for m in range(KI):
                for b, (lo, w) in enumerate(BLK):
                    gate_up(3 * m + b, WS[0], lambda r, k: X2T[:, r, k, lo:lo + w], w, m)
            pe.wait_ge(s_s3, 1)
            pe.wait_ge(s_gx, 9)
            for n, S_ in enumerate((S3, O3[0], O3[1])):
                for j in range(NT):
                    ins = nc.tensor.transpose(PB[0:24, col16(2 * n, j):col16(2 * n, j) + T], S_[:, j, :], idb[0:T, 0:T])
                ins.then_inc(s_s3t, 1)

            def rank_rows(r):
                j, k = divmod(r, 2)
                t = 3 * (r % 2)
                if r >= 2:
                    pe.wait_ge(s_rk, r - 1)
                for lo in range(0, N, 512):
                    w = min(512, N - lo)
                    ins = M(PSF[0:T, 512 * t + lo:512 * t + lo + w], O3T[k][:, T * j:T * j + T],
                            S3T[:, lo:lo + w], start=True, stop=True)
                ins.then_inc(s_rr, 1)

            def down(lhs, wb, o_):
                for q in range(2):
                    for m in range(KI):
                        ins = mm3(o_(q), lambda a: lhs(a, m),
                                  lambda r: wb[:, r, 2 * HALF + D * m + DH * q:2 * HALF + D * m + DH * q + DH],
                                  m == 0, m == KI - 1)
                return ins

            pe.wait_ge(s_s3c, 3)
            rank_rows(0)
            rank_rows(1)
            pe.wait_ge(s_alo, 9)
            for j in range(NT):
                if j:
                    pe.wait_ge(s_sdr, j)
                down(lambda a, m: AB[:, a, m, T * j:T * j + T], WS[0], lambda q: PS[0:T, 6 + q, 0:DH]
                     ).then_inc(s_sd3, 1)
                if j + 1 < NT:
                    rank_rows(2 * j + 2)
                    rank_rows(2 * j + 3)
            pe.wait_ge(s_ind, 2 * NT)
            pe.wait_ge(s_sdr, NT)
            for c in range(4):
                for k in range(2):
                    for j in range(NT):
                        ins = M(PS[0:SC, 7, E * c:E * c + E], IND[:, k, j, SC * c:SC * c + SC], OT[k][:, j, :],
                                start=k + j == 0, stop=k == 1 and j == NT - 1)
            ins.then_inc(s_tk, 1)

            def rows_T(g):
                if g == 0:
                    pe.wait_ge(s_tok, 1)
                    pe.wait_ge(s_rk, 2 * NT)
                pe.wait_ge(s_xg[g % 2], 16 * (g // 2 + 1))
                if g >= 2:
                    pe.wait_ge(s_xgl, 2 * (g - 1))
                b = 4 + 2 * (g % 2)
                for k in range(KD):
                    ins = nc.tensor.transpose(PS[:, b + k // 3, SC * (k % 3):SC * (k % 3) + SC],
                                              XG[:, g % 2, 128 * k:128 * k + 128], idf[0:SC, 0:SC])
                ins.then_inc(s_xgt, 1)

            for c in range(4):
                rows_T(c)
            for e in range(E):
                if e + 1 < E:
                    for c in range(4):
                        rows_T(4 * (e + 1) + c)
                pe.wait_ge(s_xgl, 8 * (e + 1))
                pe.wait_ge(s_wgl, 3 * (e + 2))
                if e:
                    pe.wait_ge(s_yo, 4 * e)
                for m in range(KI):
                    gate_up(9 + KI * e + m, WS[(e + 1) % 2], lambda r, k: XGT[e % 2][:, r, k, :], SLOTS, m)
                pe.wait_ge(s_alo, 9 + KI * (e + 1))
                pe.wait_ge(s_gx, 9 + KI * (e + 1))
                for c in range(4):
                    g = 4 * e + c
                    b = 2 * (c % 2)
                    if c >= 2:
                        pe.wait_ge(s_yo, g - 1)
                    down(lambda a, m: AE[e % 2][:, a, m, SC * c:SC * c + SC], WS[(e + 1) % 2],
                         lambda q: PS[0:SC, b + q, 0:DH]).then_inc(s_ed, 1)


_INS = ['x', 'src', 'dst', 'L0_gnn_W1', 'L0_gnn_att_src1', 'L0_gnn_att_dst1', 'L0_gnn_b1', 'L0_gnn_W2',
        'L0_gnn_att_src2', 'L0_gnn_att_dst2', 'L0_gnn_b2', 'L0_ffn_Wr', 'L0_ffn_w1', 'L0_ffn_w3', 'L0_ffn_w2',
        'L0_ffn_s1', 'L0_ffn_s3', 'L0_ffn_s2']
_OUTS = [((1250, 768), 'float32')]


def kernel(**inputs):
    import numpy as _np
    import concourse.bacc as _bacc
    from concourse import mybir as _mybir
    from concourse.bass_utils import run_bass_kernel_spmd as _run

    nc = _bacc.Bacc("TRN2", target_bir_lowering=False, num_devices=1)
    arrays, args = {}, []
    for name in _INS:
        a = _np.ascontiguousarray(inputs[name])
        arrays[f"in_{name}_dram"] = a
        args.append(nc.dram_tensor(f"in_{name}_dram", a.shape, _mybir.dt.from_np(a.dtype), kind="ExternalInput").ap())
    for i, (shape, dtype) in enumerate(_OUTS):
        dt = _mybir.dt.from_np(_np.dtype(dtype))
        args.append(nc.dram_tensor(f"out_{i}_dram", shape, dt, kind="ExternalOutput").ap())
    build(nc, *args)
    r = _run(nc, [arrays], core_ids=[0])
    return r.results[0]["out_0_dram"]
```

```python
from contextlib import ExitStack

import numpy as np
import concourse.bass as bass
from concourse import mybir

ALU = mybir.AluOpType
ACT = mybir.ActivationFunctionType
AX = mybir.AxisListType
F32 = mybir.dt.float32
F16 = mybir.dt.float16
BF16 = mybir.dt.bfloat16
I32 = mybir.dt.int32
U32 = mybir.dt.uint32

SX = 64.0
SW = 1024.0
SA = 256.0
NEG = -1.0e30
EPS = 1e-5
SLOPE = 0.2


def build(nc, x, src, dst, W1, as1, ad1, b1, W2, as2, ad2, b2, Wr, w1, w3, w2, s1, s3, s2, out):
    N, D = x.shape
    NE = src.shape[0]
    H, C = as1.shape
    E, _, INNER = w1.shape
    T = 125
    NT = N // T
    KD = D // 128
    CH = C // 128
    NCH = H * CH
    KI = INNER // 128
    CAP = -(-N * 2 * 5 // (E * 4))
    SLOTS = CAP + CAP % 2
    SC = SLOTS // 4
    DH = D // 2
    GP = 112
    RANK_FROM = 4
    XGN, GRN = 8, 9
    BLK = [(0, 417), (417, 417), (834, 416)]
    assert NT * T == N and NE % T == 0 and SLOTS % 4 == 0

    ET = NE // T
    DC = 50
    NC = N // DC
    GC = 5
    GT = ET // (NC // GC)
    PADT = 4
    MARGIN = 250
    KC = NT * DC
    window = []
    for c in range(GC):
        lo = (c * DC * NE // N - MARGIN) // T
        hi = -(-((c + 1) * DC * NE // N + MARGIN) // T)
        window.append((lo + PADT, hi + PADT))
    assert window[0][0] >= 0 and window[-1][1] <= GT + 2 * PADT
    KT = ET + 2 * PADT
    selfs = [sorted({(c * DC) // T, (c * DC + DC - 1) // T}) for c in range(GC)]
    jobs = [[("e", t) for t in range(*window[c])] + [("s", t) for t in selfs[c]] for c in range(GC)]
    NJ = sum(len(j) for j in jobs)
    KA = KT + NT
    TOTAL = NE + N

    BASE = 16512
    names = [0]

    def at(off, shape, dt):
        names[0] += 1
        return nc.alloc_sbuf_tensor_at(f"sb{names[0]}", list(shape), dt, offset=BASE + off)

    o_ct, o_p, o_h, o_e = 0, 25024, 75040, 116000
    CT = at(o_ct, [T, NT, N], F16)
    P = at(o_p, [T, NT, 2, N], F16)
    OL = at(o_p, [T, KA, T], F16)
    XA = at(o_p, [T, NT, D], F32)
    HB = [at(o_h + b * 20480, [T, NT, 2, C], F16) for b in range(2)]
    ED = at(o_h + 20480, [85, 2, 2, T], I32)
    EF = at(o_h + 20480 + 2048, [85, 2, 2 * T], F32)
    EQ = at(o_h + 20480 + 4096, [85, 2, 2 * T], I32)
    EG = at(o_h + 20480 + 6144, [85, 2, 2 * T], F32)
    EK = at(o_h + 20480 + 8192, [85, 2, 2 * T], F32)
    OR = at(o_h + 20480 + 10240, [T, 4, KC], F16)
    o = o_e
    ROW = at(o, [T, 2, N], F32); o += 10016
    TMP = [at(o + 5000 // 32 * 32 * b + 32 * b, [T, N], F32) for b in range(3)]
    W2G = [at(o + 3072 * b, [128, D], F32) for b in range(3)]; o += 15072
    MSK = at(o, [T, 2, N], BF16); o += 5024
    o_w2s = o
    assert o_w2s == 146112
    XTR = at(o, [128, 3, 2, KD, T], F16); o += 9024
    W1S = at(o, [128, KD, 2, C], F16); o += 12288
    WST = at(o, [128, 2, D], F32); o += 6144
    YB = at(o, [128, 3, 417], F32)
    VJ = at(o, [128, D], F32); o += 5024
    RB = at(o, [128, 2, 417], F32); o += 3360
    H1O = at(o, [128, 2, 2, N], F16); o += 10016
    RDEN = at(o, [128, N], F32); o += 5024
    o_a = o
    AR1 = at(o, [T, 2, C], F32); o += 4096
    TMP.append(at(o, [T, N], F32)); o += 5024
    assert o <= 207008, o
    A2R = at(o_e + 10016, [128, 2, D], F32)
    W2S = [at(o_w2s + 3072 * i, [128, 2, D], F16) for i in range(8)]
    W2S += [at(o_h + 3072 * i, [128, 2, D], F16) for i in range(6)]
    W2S += [at(o_a + 3072 * i, [128, 2, D], F16) for i in range(2)]
    o_y = o_w2s + 9024 + 12288 + 6144
    HT = [at(o_y + 8000 * b, [128, 2, NCH, T], F16) for b in range(2)]
    H2 = [at(o_h + 6 * 3072 + 3104 * i, [T, 2, D + 2], F16) for i in range(7)]
    assert o_h + 6 * 3072 + 3104 * 7 <= o_e
    H2 += [at(o_y + 16000 + 3104 * i, [T, 2, D + 2], F16) for i in range(2)]
    assert o_y + 16000 + 2 * 3104 <= o_a
    H2.append(at(o_w2s + 30720 + 3072, [T, 2, D + 2], F16))
    X2 = at(o_w2s, [T, NT, D], F32)
    B2R = at(o_w2s + 30720, [T, D], F32)
    X2T = at(o_e, [128, 2, KD, N], F16)
    WG0 = at(0, [128, 2 * 2304], F32)
    XN2 = at(18432, [T, 2, D], F32)
    WG = at(30720, [128, 3 * 2304], F32)
    WS = [at(58368 + b * 27648, [128, 2, 3 * 2304], F16) for b in range(2)]
    o_f = 177792
    AB = at(o_f, [128, 2, KI, N], F16); o = o_f + 15008
    AE = [at(o_f + b * 4704, [128, 2, KI, SLOTS], F16) for b in range(2)]
    SG = at(o, [128, 2, 512], F32); o += 4096
    YO = at(o, [T, 2, D], F32); o += 6144
    assert o <= 203328 and o_w2s + 30720 <= o_f
    BS = at(183040, [T, NT, 2, 6], F32)
    IND = at(0, [T, 2, NT, SLOTS], F16)
    XG = at(0, [GP, XGN, D], F32)
    S3T = at(21824, [24, N], BF16)
    O3T = [at(24352 + k * 2528, [24, N], BF16) for k in range(2)]
    XGT = [at(o_e + b * 9408, [128, 2, KD, SLOTS], F16) for b in range(2)]
    JN2 = at(15680, [T, N], BF16)
    GRL = at(0, [128, NT, D], F32)
    GR = at(30720, [128, GRN, D], F32)

    o = 207008

    def small(shape, dt):
        nonlocal o
        size = int(np.prod(shape[1:])) * {F32: 4, I32: 4, U32: 4, F16: 2, BF16: 2}[dt]
        t = at(o, shape, dt)
        o += -(-size // 32) * 32
        assert BASE + o <= 229344, o
        return t

    idf = small([128, 128], F32)
    idh = small([128, 128], F16)
    idb = small([128, 128], BF16)
    ones = small([T, 128], F16)
    TRI = small([T, T], F16)
    io392 = small([T, SLOTS], F16)
    tokid = small([T, NT], F32)
    io8 = small([T, E], F32)
    LG = small([T, NT, E], F32)
    o_k = o_h + 20480 + 16000
    iok = at(o_k, [T, KC], F16)
    iot = at(o_k + 1024, [T, T], F16)
    KEY = at(o_k + 1280, [T, KA], F32)
    SLO = at(o_k + 2048, [T, KA], F32)
    onesf = at(o_k + 2816, [T, 128], F32)
    b1c = small([128, NCH], F32)
    V2F = small([128, NCH, 2], F32)
    V2S = small([128, NCH, 2, 2], F16)
    AL = small([T, 2, H + 1, NT], F32)
    ALF = small([T, H + 1, NT], F32)
    A2C = small([T, 2 * NT], F32)
    MX = small([T, NT], F32)
    ZZ = small([T, NT], F32)
    MM = small([T, NT], F32)
    AA = small([T, 2, NT], F32)
    TR = small([2 * NT, T], F32)
    CS = small([T, NC], F32)
    flag = small([128, 1], I32)
    QI = small([T, NT], I32)
    SD = small([T, NT], F32)
    def mid(shape, dt):
        nonlocal o
        size = int(np.prod(shape[1:])) * {F32: 4, I32: 4, U32: 4, F16: 2, BF16: 2}[dt]
        t = at(o, shape, dt)
        o += -(-size // 32) * 32
        return t

    o = 113664
    M8 = mid([T, NT, 8], F32)
    I8 = mid([T, NT, 8], U32)
    OK = [mid([T, NT, E], F32) for _ in range(2)]
    SS = mid([T, NT, E], F32)
    IK = mid([T, 2, NT], F32)
    WK = mid([T, 2, NT], F32)
    CA = mid([T, 3, 2, NT], F32)
    assert o <= o_e, (o, o_e)
    o = 203328
    OT = [mid([T, NT, E], F16) for _ in range(2)]
    RK = mid([T, 2, NT], F32)
    S3 = mid([T, NT, 24], BF16)
    O3 = [mid([T, NT, 24], BF16) for _ in range(2)]
    IDX = mid([128, 3, NT], U32)
    TOK = mid([GP, 4, E], U32)
    WL = mid([T, NT], F32)
    WRS = mid([128, KD, 2, E], F16)
    WRG = mid([128, KD, E], F32)
    MV = mid([T, NT, 2], F32)
    assert o <= 207008, o
    BS1 = at(o_h + 20480 + 14336, [T, NT, 2, 6], F32)
    MV1 = at(o_h + 20480 + 15360, [T, NT, 2], F32)

    def dram(name, shape, dt):
        return nc.dram_tensor(name, list(shape), dt, kind="Internal").ap()

    XTD = dram("xt_d", [NT, 128, 2 * KD * T], F16)
    MSKD = dram("mask_d", [NT, T, N], BF16)
    ALD = dram("al_d", [H + 1, NT, T], F32)
    AAD = dram("aa_d", [H + 1, 2 * NT, T], F32)
    H1D = dram("h1_d", [NT, 128, 2, NCH, T], F16)
    XND = dram("xn_d", [N, D], F32)
    YD = dram("y_d", [E * SLOTS, D], F32)

    ctx = ExitStack()
    with ctx:
        PS = ctx.enter_context(nc.psum_tensor("PS", [128, 8, 512], F32))
        PSF = PS[:, :, :].rearrange("p b n -> p (b n)")

        def ps16(dt):
            return PSF.bitcast(dt)

        PH, PB = ps16(F16), ps16(BF16)

        def col16(b, i):
            return 1024 * (b + i // 5) + (T + 1) * (i % 5)

        def blocks16(v, rows, b):
            return v[0:rows, 1024 * b:1024 * b + 2048].rearrange("p (a r) -> p a r", a=2)[
                :, :, 0:5 * (T + 1)].rearrange("p a (i n) -> p a i n", n=T + 1)[:, :, :, 0:T]

        def sem(name):
            return ctx.enter_context(nc.semaphore(name))

        s_const = sem("consts_made")
        s_edges = sem("edges_loaded")
        s_x = [sem(f"x_loaded{b}") for b in range(2)]
        s_bias = sem("biases_loaded")
        s_once = sem("keys_then_total_on_tensor_engine")
        s_a2v = sem("a2_loaded")
        s_dve = sem("dve_step")
        s_act = sem("act_step")
        s_keys = sem("keys_made")
        s_var = sem("variance_made")
        s_sd = sem("deviation_made")
        s_xn = sem("x_normalised")
        s_xT = sem("x_transposed")
        s_xth = sem("xT_hi_made")
        s_xtl = sem("xT_lo_made")
        s_xts = [sem(f"xT_slot{b}") for b in range(3)]
        s_wst = [sem(f"weights_in_slot{b}") for b in range(2)]
        s_wh = sem("weight_hi_made")
        s_wl = sem("weight_slot_used")
        s_arep = sem("attention_vectors_loaded")
        s_proj = sem("projection_done")
        s_hh = sem("h_hi_made")
        s_hl = sem("h_used")
        s_ol = sem("source_onehots_made")
        s_or = sem("pair_onehot_made")
        s_cm = sem("pair_onehot_used")
        s_k2 = sem("keys_advanced")
        s_ce = sem("chunk_kept")
        s_cs = sem("count_sum_steps")
        s_pf = sem("p_tile_free")
        s_go = sem("general_onehot_made")
        s_gu = sem("general_onehot_used")
        s_gd = sem("general_chunk_done")
        s_gk = sem("general_chunk_kept")
        s_ctok = sem("counts_final")
        s_mt = sem("mask_transposed")
        s_mm = sem("mask_made")
        s_ms = [sem(f"mask_stored{b}") for b in range(2)]
        s_ml = [sem(f"mask_loaded{b}") for b in range(2)]
        s_mu = sem("mask_used")
        s_v2 = sem("v2_made")
        s_alt = sem("al_transposed")
        s_alc = sem("al_row_made")
        s_ald = sem("al_row_stored")
        s_row = sem("al_row_broadcast")
        s_aa = sem("shifts_made")
        s_aat = sem("shifts_transposed")
        s_aac = sem("shift_rows_made")
        s_aad = sem("shift_rows_stored")
        s_rows = sem("shift_rows_broadcast")
        s_al = sem("al_complete")
        s_p1 = sem("p_second_branch")
        s_p2 = sem("p_leaky")
        s_p3 = sem("p_exp")
        s_p4 = sem("p_counted")
        s_p5 = sem("p_hi")
        s_p6 = sem("p_lo")
        s_att = sem("attention_group_done")
        s_atr = sem("attention_group_read")
        s_rd = sem("denominator_made")
        s_y1 = sem("y_divided")
        s_yr = sem("y_relu")
        s_y2 = sem("y_exp")
        s_y3 = sem("y_elu1")
        s_y4 = sem("y_scaled")
        s_y5 = sem("h1_hi")
        s_y6 = sem("h1_lo")
        s_h1s = [sem(f"h1_stored{b}") for b in range(2)]
        s_a2 = sem("al2_part_done")
        s_al4 = sem("al2_made")
        s_a2r = sem("al2_part_added")
        s_w2g = [sem(f"w2_in_slot{b}") for b in range(3)]
        s_w2h = sem("w2_hi")
        s_w2l = sem("w2_lo")
        s_ht = [sem(f"h1_loaded{b}") for b in range(2)]
        s_pj2 = sem("projection2_done")
        s_h2h = sem("h2_hi")
        s_h2l = sem("h2_lo")
        s_h2o = sem("h2_ones")
        s_xb = sem("x_plus_bias")
        s_at2 = sem("attention2_done")
        s_x2 = sem("x2_made")
        s_xn2 = sem("x2_normalised")
        s_xns = [sem(f"xn2_stored{b}") for b in range(2)]
        s_x2t = sem("x2_transposed")
        s_x2h = sem("x2T_hi")
        s_x2lo = sem("x2T_lo")
        s_wrl = sem("router_loaded")
        s_lg = sem("logits_done")
        s_lgm = sem("logits_shifted")
        s_pe = sem("probs_exp")
        s_wg = [sem(f"ffn_weights_loaded{q}") for q in range(3)]
        s_wgh = sem("ffn_weights_hi")
        s_wgl = sem("ffn_weights_lo")
        s_gdn = sem("gate_done")
        s_udn = sem("up_done")
        s_sg = sem("silu_made")
        s_gx = sem("gate_times_up")
        s_ah = sem("act_hi")
        s_alo = sem("act_lo")
        s_s3 = sem("scores_split")
        s_s3t = sem("scores_transposed")
        s_s3c = sem("scores_rows_made")
        s_sd3 = sem("shared_down_done")
        s_sdc = sem("shared_copied")
        s_sdr = sem("shared_added")
        s_rr = sem("rank_rows_done")
        s_rk = sem("rank_rows_used")
        s_ind = sem("slots_onehot_made")
        s_tk = sem("token_table_done")
        s_tok = sem("token_table_made")
        s_xg = [sem(f"rows_gathered{b}") for b in range(XGN)]
        s_xgt = sem("rows_transposed")
        s_xgh = sem("rows_hi")
        s_xgl = sem("rows_lo")
        s_ed = sem("expert_down_done")
        s_yo = sem("expert_rows_made")
        s_ys = [sem(f"expert_rows_stored{b}") for b in range(2)]
        s_gz = sem("return_slot_cleared")
        s_gzl = sem("return_places_cleared")
        s_gg = [sem(f"expert_rows_gathered{b}") for b in range(GRN)]
        s_ggl = [sem(f"last_rows_gathered{j}") for j in range(NT - XGN)]
        s_gl = sem("last_rows_added")
        s_g1 = sem("expert_rows_added")
        s_fin = sem("out_stored")

        block = ctx.enter_context(nc.Block())

        last_in = [(s_xg[j], 16 * (E * 4 // XGN + 1)) for j in range(XGN)]
        last_in += [(s_ggl[j], 16) for j in range(NT - XGN)]

        def w1_use(h, k):
            return k if h == 0 else KD + NCH + (h - 1) * KD + k

        def v2_use(ch):
            return KD + ch

        def tmp(h, i):
            q = NT * h + i
            if h < H:
                return TMP[q % 4], q - 3
            return TMP[i % 3], max(q - 2, NT * H)

        x2_in = [(s_xts[b], 16 * (len(range(b, NT + NT * H, 3)) + 1)) for b in range(3)]
        x2_in += [(s_wst[b], 16 * ((KD * H + NCH) // 2 + 1)) for b in range(2)]
        x2_in += [(s_w2g[b], 16 * (len(range(b, NCH, 3)) + 1)) for b in range(3)]
        x2_in += [(s_h1s[b], 16 * (NCH + 1)) for b in range(2)]
        NPRE = 4

        HALF = 2304

        def ffn_weights(n):
            if n == 0:
                return s1, s3, s2
            return w1[n - 1], w3[n - 1], w2[n - 1]

        @block.sync
        def _(sp):
            sp.dma_start(ED[:, 0], src.rearrange("(a q p) -> q a p", a=2, p=T)).then_inc(s_edges, 16)
            sp.dma_start(ED[:, 1], dst.rearrange("(a q p) -> q a p", a=2, p=T)).then_inc(s_edges, 16)
            for b in range(2):
                sp.dma_start(XA[:, 5 * b:5 * b + 5, :],
                             x[5 * T * b:5 * T * b + 5 * T, :].rearrange("(i p) d -> p i d", p=T)).then_inc(s_x[b], 16)
            with nc.allow_non_contiguous_dma(reason="one small column load"):
                sp.dma_start(b1c[:, :], b1.rearrange("(c p) -> p c", p=128)).then_inc(s_bias, 16)

            def load_w(u, view):
                if u >= 2:
                    sp.wait_ge(s_wl, u - 1)
                sp.dma_start(WST[:, u % 2, 0:view.shape[1]], view).then_inc(s_wst[u % 2], 16)

            def load_w1(h):
                load_al(h)
                load_w1_rows(h, range(KD))

            def load_al(h):
                if h:
                    sp.wait_ge(s_hl, NT * h)
                sp.dma_start(AR1[:, 0, :], as1[h:h + 1, :].to_broadcast([T, C])).then_inc(s_arep, 16)
                sp.dma_start(AR1[:, 1, :], ad1[h:h + 1, :].to_broadcast([T, C])).then_inc(s_arep, 16)

            def load_w1_rows(h, ks):
                for k in ks:
                    load_w(w1_use(h, k), W1[128 * k:128 * k + 128, C * h:C * h + C])

            def store_xt(i):
                sp.wait_ge(s_xtl, i + 1)
                sp.dma_start(XTD[i], XTR[:, i % 3].rearrange("p a k n -> p (a k n)")).then_inc(s_xts[i % 3], 16)

            def slot_uses(v):
                return 16 * (v // 3 + 1)

            def load_xt(h, i):
                v = NT + NT * h + i
                if v - 3 < NT:
                    sp.wait_ge(s_xts[v % 3], slot_uses(v - 3))
                else:
                    sp.wait_ge(s_proj, v - 3 - NT + 1)
                if h == 0:
                    sp.wait_ge(s_xts[i % 3], slot_uses(i))
                sp.dma_start(XTR[:, v % 3].rearrange("p a k n -> p (a k n)"), XTD[i]).then_inc(s_xts[v % 3], 16)

            load_al(0)
            load_w1_rows(0, range(2))
            for i in range(NT):
                store_xt(i)
            load_w1_rows(0, range(2, KD))
            for i in range(NT):
                load_xt(0, i)
            for j in range(NT):
                sp.wait_ge(s_mm, j + 1)
                sp.dma_start(MSKD[j], MSK[:, j % 2, :]).then_inc(s_ms[j % 2], 16)
            sp.wait_ge(s_xn, NT)
            sp.dma_start(A2R[:, 0, :], as2.to_broadcast([128, D])).then_inc(s_a2v, 16)
            sp.dma_start(A2R[:, 1, :], ad2.to_broadcast([128, D])).then_inc(s_a2v, 16)
            for ch in range(NCH):
                load_w(v2_use(ch), W2[128 * ch:128 * ch + 128, :])

            def chain_row(h):
                sp.wait_ge(s_alc, h + 1)
                sp.dma_start(ALD[h], TR[0:NT, :]).then_inc(s_ald, 16)
                sp.wait_ge(s_ald, 16 * (h + 1))
                if h:
                    sp.wait_ge(s_p1, NT * h)
                    sp.wait_ge(s_p2, NT * h)
                sp.dma_start(ROW[:, 0, :], ALD[h:h + 1].rearrange("o a n -> o (a n)").to_broadcast([T, N])
                             ).then_inc(s_row, 16)

            def chain_mask(h, js):
                for j in js:
                    n = NT * h + j
                    if n < 2:
                        sp.wait_ge(s_ms[0], 16 * (NT // 2))
                        sp.wait_ge(s_ms[1], 16 * (NT // 2))
                    else:
                        sp.wait_ge(s_mu, n - 1)
                    sp.dma_start(MSK[:, j % 2, :], MSKD[j]).then_inc(s_ml[j % 2], 16)

            def chain_shift(h):
                sp.wait_ge(s_aac, h + 1)
                sp.dma_start(AAD[h], TR[:, :]).then_inc(s_aad, 16)
                sp.wait_ge(s_aad, 16 * (h + 1))
                sp.dma_start(ROW[:, :, :].rearrange("p a n -> p (a n)"),
                             AAD[h:h + 1].rearrange("o a n -> o (a n)").to_broadcast([T, 2 * N])
                             ).then_inc(s_rows, 16)

            def store_h1(h, c):
                g = CH * h + c
                sp.wait_ge(s_y6, 3 * (g + 1))
                for part in range(2):
                    sp.dma_start(H1D[:, :, part, g, :].rearrange("j p n -> p j n"),
                                 H1O[:, g % 2, part, :].rearrange("p (j n) -> p j n", n=T)
                                 ).then_inc(s_h1s[g % 2], 16)

            chain_row(0)
            chain_mask(0, range(NT))
            chain_shift(0)
            load_w1(1)
            for i in range(NT):
                load_xt(1, i)
            def load_w2(ch):
                if ch >= 3:
                    sp.wait_ge(s_w2l, ch - 2)
                sp.dma_start(W2G[ch % 3][:, :], W2[128 * ch:128 * ch + 128, :]).then_inc(s_w2g[ch % 3], 16)

            for h in range(H):
                if h + 1 < H:
                    chain_row(h + 1)
                    chain_mask(h + 1, range(2))
                else:
                    sp.wait_ge(s_p6, NT * H)
                    for ch in range(3):
                        load_w2(ch)
                if h + 2 < H:
                    load_al(h + 2)
                    load_w1_rows(h + 2, range(2))
                store_h1(h, 0)
                if h + 1 < H:
                    chain_mask(h + 1, range(2, NT))
                    chain_shift(h + 1)
                else:
                    for ch in range(3, 7):
                        load_w2(ch)
                store_h1(h, 1)
                if h + 2 < H:
                    load_w1_rows(h + 2, range(2, KD))
                    for i in range(3):
                        load_xt(h + 2, i)
                if h + 1 == H:
                    for ch in range(7, 11):
                        load_w2(ch)
                store_h1(h, 2)
                if h + 1 == H:
                    for ch in range(11, NCH):
                        load_w2(ch)
                store_h1(h, 3)
                if h + 2 < H:
                    for i in range(3, NT):
                        load_xt(h + 2, i)

            def load_ht(j):
                if j == 0:
                    for b in range(2):
                        sp.wait_ge(s_h1s[b], 16 * NCH)
                if j == 1:
                    sp.wait_ge(s_a2, NCH)
                if j >= 2:
                    sp.wait_ge(s_pj2, j - 1)
                sp.dma_start(HT[j % 2][:, :, :, :].rearrange("p a c n -> p (a c n)"),
                             H1D[j].rearrange("p a c n -> p (a c n)")).then_inc(s_ht[j % 2], 16)

            load_ht(0)
            load_ht(1)
            chain_row(H)
            chain_mask(H, range(NT // 2))
            load_ht(2)
            chain_mask(H, range(NT // 2, NT))
            chain_shift(H)
            for j in range(3, NT):
                load_ht(j)
            sp.wait_ge(s_pj2, NT)
            sp.dma_start(B2R[:, :], b2.rearrange("(o d) -> o d", o=1).to_broadcast([T, D])).then_inc(s_bias, 16)
            for j in range(NT):
                sp.dma_start(X2[:, j, :], x[T * j:T * j + T, :]).then_inc(x2_in[j][0], 16)
            sp.dma_start(WRG[:, :, :], Wr.rearrange("(k p) e -> p k e", p=128)).then_inc(s_wrl, 16)
            sp.wait_ge(s_p4, NT * (H + 1))

            def weight_part(n, q):
                w = ffn_weights(n)[q]
                place = WG0 if n == 0 and q < 2 else WG
                sp.dma_start(place[:, HALF * q:HALF * q + HALF].rearrange("p (k i) -> p k i", i=w.shape[1]),
                             w.rearrange("(k p) i -> p k i", p=128)).then_inc(s_wg[q], 16)

            weight_part(0, 0)
            weight_part(0, 1)

            def store_xn(i):
                sp.wait_ge(s_xn2, i + 1)
                sp.dma_start(XND[T * i:T * i + T, :], XN2[:, i % 2, :]).then_inc(s_xns[i % 2], 16)

            for i in range(NT - 1):
                store_xn(i)
            sp.wait_ge(s_at2, NT)
            weight_part(0, 2)
            store_xn(NT - 1)

            def load_ffn(n):
                for q in range(3):
                    sp.wait_ge(s_wgh, 3 * (n - 1) + q + 1)
                    sp.wait_ge(s_wgl, 3 * (n - 1) + q + 1)
                    weight_part(n, q)

            load_ffn(1)
            for e in range(E):
                if e + 2 <= E:
                    load_ffn(e + 2)
                for c in range(4):
                    g = 4 * e + c
                    sp.wait_ge(s_yo, g + 1)
                    sp.dma_start(YD[SLOTS * e + SC * c:SLOTS * e + SC * c + SC, :], YO[0:SC, g % 2, :]
                                 ).then_inc(s_ys[g % 2], 16)
            for j in range(NT):
                sp.wait_ge(s_gl, j + 1)
                sp.dma_start(out[T * j:T * j + T, :], X2[:, j, :]).then_inc(s_fin, 16)
            sp.wait_ge(s_fin, 16 * NT)

        @block.gpsimd
        def _(pool):
            made = [0]

            def link(ins):
                made[0] += 1
                ins.then_inc(s_const, 1)
                pool.wait_ge(s_const, made[0])

            for t in (idf, idh, idb):
                link(nc.gpsimd.memset(t[:, :], 0.0))
                link(nc.gpsimd.affine_select(out=t[:, :], in_=t[:, :], compare_op=ALU.not_equal, fill=1.0,
                                             base=0, pattern=[[-1, 128]], channel_multiplier=1))
            link(nc.gpsimd.iota(iok[:, :], [[1, KC]], base=0, channel_multiplier=0,
                                allow_small_or_imprecise_dtypes=True))
            link(nc.gpsimd.iota(iot[:, :], [[1, T]], base=0, channel_multiplier=0,
                                allow_small_or_imprecise_dtypes=True))
            link(nc.gpsimd.memset(ones[:, :], 1.0))
            link(nc.gpsimd.memset(onesf[:, :], 1.0))
            link(nc.gpsimd.memset(KEY[:, 0:KT], -1.0))
            link(nc.gpsimd.memset(SLO[:, 0:KT], -1.0))
            link(nc.gpsimd.iota(SLO[:, KT:KA], [[0, NT]], base=0, channel_multiplier=1,
                                allow_small_or_imprecise_dtypes=True))
            link(nc.gpsimd.iota(MX[:, :], [[T, NT]], base=0, channel_multiplier=1,
                                allow_small_or_imprecise_dtypes=True))
            link(nc.gpsimd.iota(ZZ[:, :], [[T + DC, NT]], base=0, channel_multiplier=1,
                                allow_small_or_imprecise_dtypes=True))

            def p_lo(h, i):
                q = NT * h + i
                pool.wait_ge(s_p5, q + 1)
                nc.gpsimd.tensor_tensor(P[:, i, 1, :], tmp(h, i)[0][:, :], P[:, i, 0, :], ALU.subtract
                                        ).then_inc(s_p6, 1)

            def h1_lo(h, c, b):
                g = CH * h + c
                y = 3 * g + b
                lo, n = BLK[b]
                pool.wait_ge(s_y3, y + 1)
                nc.gpsimd.tensor_scalar(YB[:, y % 3, 0:n], YB[:, y % 3, 0:n], SX, -SX, ALU.mult, ALU.add
                                        ).then_inc(s_y4, 1)
                pool.wait_ge(s_y5, y + 1)
                nc.gpsimd.tensor_tensor(H1O[:, g % 2, 1, lo:lo + n], YB[:, y % 3, 0:n],
                                        H1O[:, g % 2, 0, lo:lo + n], ALU.subtract).then_inc(s_y6, 1)

            for i in range(NT):
                p_lo(0, i)
            for h in range(H):
                for c in range(CH):
                    if c == CH - 1 and h + 1 < H:
                        for i in range(NPRE - 2):
                            p_lo(h + 1, i)
                    for b in range(3):
                        h1_lo(h, c, b)
                if h + 1 < H:
                    for i in range(NPRE - 2, NT):
                        p_lo(h + 1, i)
            for i in range(NT):
                p_lo(H, i)
            pool.wait_ge(s_bias, 32)
            for j in range(NT):
                pool.wait_ge(*x2_in[j])
                nc.gpsimd.tensor_tensor(X2[:, j, :], X2[:, j, :], B2R[:, :], ALU.add).then_inc(s_xb, 1)

            pool.wait_ge(s_at2, NT)
            link(nc.gpsimd.memset(TRI[:, :], 1.0))
            link(nc.gpsimd.affine_select(out=TRI[:, :], in_=TRI[:, :], compare_op=ALU.is_gt, fill=0.0,
                                         base=0, pattern=[[-1, T]], channel_multiplier=1))
            link(nc.gpsimd.iota(io392[:, :], [[1, SLOTS]], base=0, channel_multiplier=0,
                                allow_small_or_imprecise_dtypes=True))
            link(nc.gpsimd.memset(IDX[:, :, :], 0.0))
            link(nc.gpsimd.memset(TOK[:, :, :], 0.0))
            link(nc.gpsimd.iota(tokid[:, :], [[T, NT]], base=0, channel_multiplier=1,
                                allow_small_or_imprecise_dtypes=True))
            link(nc.gpsimd.iota(io8[:, :], [[1, E]], base=0, channel_multiplier=0,
                                allow_small_or_imprecise_dtypes=True))

            def act_lo(n, dst, src_, hi):
                pool.wait_ge(s_ah, n + 1)
                nc.gpsimd.tensor_tensor(dst, src_, hi, ALU.subtract).then_inc(s_alo, 1)

            for m in range(KI):
                for b, (lo, w) in enumerate(BLK):
                    n = 3 * m + b
                    act_lo(n, AB[:, 1, m, lo:lo + w], SG[:, n % 2, 0:w], AB[:, 0, m, lo:lo + w])

            for j in range(NT):
                pool.wait_ge(s_sdc, j + 1)
                nc.gpsimd.tensor_tensor(X2[:, j, :], X2[:, j, :], YO[:, j % 2, :], ALU.add).then_inc(s_sdr, 1)

            def gather(g):
                e, c = divmod(g, 4)
                if g >= XGN:
                    pool.wait_ge(s_xgt, g - XGN + 1)
                nc.gpsimd.indirect_dma_start(
                    out=XG[:, g % XGN, :], out_offset=None, in_=XND[:, :],
                    in_offset=bass.IndirectOffsetOnAxis(ap=TOK[:, c, e:e + 1], axis=0),
                ).then_inc(s_xg[g % XGN], 16)

            def expert_lo(e, m):
                n = 9 + KI * e + m
                act_lo(n, AE[e % 2][:, 1, m, :], SG[:, n % 2, 0:SLOTS], AE[e % 2][:, 0, m, :])

            def gather_back(n):
                j, k = divmod(n, 2)
                if n >= GRN:
                    pool.wait_ge(s_gz, n - GRN + 1)
                nc.gpsimd.indirect_dma_start(
                    out=GR[:, n % GRN, :], out_offset=None, in_=YD[0:SLOTS * (E - 1), :],
                    in_offset=bass.IndirectOffsetOnAxis(ap=IDX[:, k, j:j + 1], axis=0),
                    bounds_check=(E - 1) * SLOTS - 1, oob_is_err=False,
                ).then_inc(s_gg[n % GRN], 16)

            pool.wait_ge(s_tok, 1)
            for b in range(2):
                pool.wait_ge(s_xns[b], 16 * NT // 2)
            for g in range(XGN):
                gather(g)
            for e in range(E - 1):
                for m in range(KI):
                    expert_lo(e, m)
                if e + 2 < E:
                    for c in range(4):
                        gather(4 * (e + 2) + c)
            pool.wait_ge(s_xgt, 4 * E)
            nc.gpsimd.memset(GRL[:, :, :], 0.0).then_inc(s_gzl, 1)
            for q in range(GRN // 3):
                pool.wait_ge(s_wgl, 3 * E + q + 1)
                nc.gpsimd.memset(GR[:, 3 * q:3 * q + 3, :], 0.0).then_inc(s_gzl, 1)
            pool.wait_ge(s_gzl, 1 + GRN // 3)
            for b in range(2):
                pool.wait_ge(s_ys[b], 16 * 2 * (E - 1))
            for n in range(2 * NT):
                if n in (3, 6, 9):
                    expert_lo(E - 1, n // 3 - 1)
                gather_back(n)
            for b in range(2):
                pool.wait_ge(s_ys[b], 16 * 2 * E)
            for j in range(NT):
                nc.gpsimd.indirect_dma_start(
                    out=GRL[:, j, :], out_offset=None, in_=YD[:, :],
                    in_offset=bass.IndirectOffsetOnAxis(ap=IDX[:, 2, j:j + 1], axis=0),
                    bounds_check=E * SLOTS - 1, oob_is_err=False,
                ).then_inc(last_in[j][0], 16)

        @block.scalar
        def _(act):
            A = nc.scalar.activation
            for b in range(2):
                act.wait_ge(s_var, b + 1)
                A(SD[:, 5 * b:5 * b + 5], MV1[:, 5 * b:5 * b + 5, 1], ACT.Sqrt).then_inc(s_sd, 1)
            for i in range(NT):
                act.wait_ge(s_xT, i + 1)
                if i >= 3:
                    act.wait_ge(s_xts[i % 3], 16 * (i // 3))
                b = 6 - 2 * (i % 2)
                A(XTR[:, i % 3, 0].rearrange("p (a k) n -> p a (k n)", a=2), PS[:, b:b + 2, 0:375],
                  ACT.Copy).then_inc(s_xth, 1)

            def w1_hi(h):
                if h:
                    act.wait_ge(s_proj, NT * h)
                for k in range(KD):
                    u = w1_use(h, k)
                    act.wait_ge(s_wst[u % 2], 16 * (u // 2 + 1))
                    A(W1S[:, k, 0, :], WST[:, u % 2, 0:C], ACT.Copy, scale=SW).then_inc(s_wh, 1)

            def h_hi(h, i):
                act.wait_ge(s_proj, NT * h + i + 1)
                if h >= 2 and i == 0:
                    act.wait_ge(s_att, 5 * (h - 1))
                A(HB[h % 2][:, i, 0, :], PS[0:T, 6 + i % 2, :], ACT.Copy, scale=1.0 / SW).then_inc(s_hh, 1)

            w1_hi(0)
            for i in range(NT):
                h_hi(0, i)
            act.sem_inc(s_ce, 1)
            with act.Fori(0, NC // GC) as g:
                for c in range(GC):
                    act.wait_ge(s_cm, 1 + g * NJ + sum(len(j) for j in jobs[:c + 1]))
                    A(CT[:, :, bass.ds((GC * g + c) * DC, DC)],
                      PS[0:T, c, 0:KC].rearrange("p (i n) -> p i n", n=DC), ACT.Copy,
                      accum_out=CS[:, bass.ds(GC * g + c, 1)]).then_inc(s_ce, 1)

            def p_branch(h, i):
                q = NT * h + i
                if i == 0:
                    act.wait_ge(s_rows, 16 * (h + 1))
                    act.wait_ge(s_al, h + 1)
                if q >= 4:
                    act.wait_ge(s_p6, tmp(h, i)[1])
                A(tmp(h, i)[0][:, :], ROW[:, 1, :], ACT.Identity, bias=ALF[:, h, i:i + 1]).then_inc(s_p1, 1)

            def p_exp(h, i):
                q = NT * h + i
                act.wait_ge(s_p2, q + 1)
                A(tmp(h, i)[0][:, :], tmp(h, i)[0][:, :], ACT.Exp).then_inc(s_p3, 1)

            def p_hi(h, i):
                q = NT * h + i
                act.wait_ge(s_p4, q + 1)
                if h and i < NT - 1:
                    act.wait_ge(s_pf, (NT - 1) * (h - 1) + i + 1)
                elif h:
                    act.wait_ge(s_att, 5 * h)
                if q == 0:
                    act.wait_ge(s_ctok, 1)
                A(P[:, i, 0, :], tmp(h, i)[0][:, :], ACT.Copy).then_inc(s_p5, 1)

            def p_step(h, i):
                if i < NT:
                    p_branch(h, i)
                if 1 <= i <= NT:
                    p_exp(h, i - 1)
                if 2 <= i:
                    p_hi(h, i - 2)

            def y_step(h, c, b):
                g = CH * h + c
                y = 3 * g + b
                lo, n = BLK[b]
                act.wait_ge(s_y1, y + 1)
                if y >= 2:
                    act.wait_ge(s_y3, y - 1)
                if y == 0:
                    act.wait_ge(s_bias, 16)
                A(RB[:, y % 2, 0:n], YB[:, y % 3, 0:n], ACT.Relu, bias=b1c[:, g:g + 1], scale=1.0 / SX
                  ).then_inc(s_yr, 1)
                A(YB[:, y % 3, 0:n], YB[:, y % 3, 0:n], ACT.Exp, bias=b1c[:, g:g + 1], scale=1.0 / SX
                  ).then_inc(s_y2, 1)

            def y_hi(h, c, b):
                g = CH * h + c
                y = 3 * g + b
                lo, n = BLK[b]
                act.wait_ge(s_y4, y + 1)
                if b == 0 and g >= 2:
                    act.wait_ge(s_h1s[g % 2], 32 * (g // 2))
                    act.wait_ge(s_a2, g - 1)
                A(H1O[:, g % 2, 0, lo:lo + n], YB[:, y % 3, 0:n], ACT.Copy).then_inc(s_y5, 1)

            def w2_hi(ch):
                if ch == 0:
                    act.wait_ge(s_p6, NT * H)
                act.wait_ge(s_w2g[ch % 3], 16 * (ch // 3 + 1))
                A(W2S[ch][:, 0, :], W2G[ch % 3][:, :], ACT.Copy, scale=SW).then_inc(s_w2h, 1)

            w1_hi(1)
            for i in range(NT + 2):
                if i < NT:
                    h_hi(1, i)
                p_step(0, i)
            for h in range(H):
                for c in range(CH):
                    for b in range(4):
                        if b < 3:
                            y_step(h, c, b)
                        if b:
                            y_hi(h, c, b - 1)
                    if c == 2 and h + 2 < H:
                        w1_hi(h + 2)
                    if h + 1 == H:
                        for ch in range(4 * c, 4 * c + 4):
                            w2_hi(ch)
                    if c == 2 and h + 1 < H:
                        for i in range(NPRE):
                            p_step(h + 1, i)
                if h + 1 < H:
                    for i in range(NPRE, NT + NPRE):
                        if h + 2 < H:
                            h_hi(h + 2, i - NPRE)
                        if i < NT + 2:
                            p_step(h + 1, i)
            def h2_hi(j):
                act.wait_ge(s_pj2, j + 1)
                b = 2 * (j % 2)
                A(H2[j][:, 0, 0:D].rearrange("p (a n) -> p a n", a=2), PS[0:T, b:b + 2, 0:DH], ACT.Copy,
                  scale=1.0 / SW).then_inc(s_h2h, 1)

            act.wait_ge(s_w2l, NCH)
            for i in range(NT + 2):
                p_step(H, i)
                if i < NT:
                    h2_hi(i)

            def x2t_hi(i):
                act.wait_ge(s_x2t, i + 1)
                b = 2 * (i % 2)
                A(X2T[:, 0, :, T * i:T * i + T].rearrange("p (a k) n -> p a k n", a=2),
                  PS[:, b:b + 2, 0:375].rearrange("p a (k n) -> p a k n", n=T), ACT.Copy).then_inc(s_x2h, 1)

            act.wait_ge(s_wrl, 16)
            A(WRS[:, :, 0, :], WRG[:, :, :], ACT.Copy, scale=SW).then_inc(s_wh, 1)
            for j in range(NT):
                act.wait_ge(s_var, 3 + j)
                A(SD[:, j:j + 1], MV[:, j, 1:2], ACT.Sqrt).then_inc(s_sd, 1)
                if j:
                    x2t_hi(j - 1)

            def ffn_hi(n, q):
                act.wait_ge(s_wg[q], 16 * (n + 1))
                if n == 0:
                    act.wait_ge(s_at2, NT)
                if n >= 2 and q == 0:
                    if n == 2:
                        act.wait_ge(s_sd3, NT)
                    else:
                        act.wait_ge(s_ed, 4 * (n - 2))
                A(WS[n % 2][:, 0, HALF * q:HALF * q + HALF], (WG0 if n == 0 and q < 2 else WG)[:, HALF * q:HALF * q + HALF], ACT.Copy,
                  scale=SW).then_inc(s_wgh, 1)

            ffn_hi(0, 0)
            x2t_hi(NT - 1)
            ffn_hi(0, 1)
            ffn_hi(0, 2)
            act.wait_ge(s_lgm, 1)
            A(LG[:, :, :], LG[:, :, :], ACT.Exp).then_inc(s_pe, 1)

            def silu(n, w):
                act.wait_ge(s_gdn, n + 1)
                if n >= 2:
                    act.wait_ge(s_alo, n - 1)
                A(SG[:, n % 2, 0:w], PS[:, 6, 0:w], ACT.Silu, scale=1.0 / (SX * SW)).then_inc(s_sg, 1)

            def act_hi(n, dst_, w):
                act.wait_ge(s_gx, n + 1)
                A(dst_, SG[:, n % 2, 0:w], ACT.Copy).then_inc(s_ah, 1)

            for n in range(9):
                lo, w = BLK[n % 3]
                silu(n, w)
                act_hi(n, AB[:, 0, n // 3, lo:lo + w], w)
                if 1 <= n <= 3:
                    ffn_hi(1, n - 1)
            for j in range(NT):
                act.wait_ge(s_sd3, j + 1)
                if j >= 2:
                    act.wait_ge(s_sdr, j - 1)
                A(YO[:, j % 2, :].rearrange("p (a n) -> p a n", a=2), PS[0:T, 6:8, 0:DH], ACT.Copy,
                  scale=1.0 / (SA * SW)).then_inc(s_sdc, 1)

            def xg_hi(g):
                e, c = divmod(g, 4)
                act.wait_ge(s_xgt, g + 1)
                if c == 0 and e >= 2:
                    act.wait_ge(s_udn, 9 + KI * (e - 1))
                b = 2 + 2 * (g % 2)
                A(XGT[e % 2][:, 0, :, SC * c:SC * c + SC].rearrange("p (a k) n -> p a k n", a=2),
                  PS[:, b:b + 2, 0:3 * SC].rearrange("p a (k n) -> p a k n", n=SC), ACT.Copy).then_inc(s_xgh, 1)

            def y_out(g):
                c = g % 4
                act.wait_ge(s_ed, g + 1)
                if g >= 2:
                    act.wait_ge(s_ys[g % 2], 16 * (g // 2))
                else:
                    act.wait_ge(s_sdr, NT)
                b = 6 if c % 2 == 0 else 0
                A(YO[0:SC, g % 2, :].rearrange("p (a n) -> p a n", a=2), PS[0:SC, b:b + 2, 0:DH], ACT.Copy,
                  scale=1.0 / (SA * SW)).then_inc(s_yo, 1)

            for c in range(4):
                xg_hi(c)
            for e in range(E):
                for m in range(KI):
                    n = 9 + KI * e + m
                    silu(n, SLOTS)
                    if m == 0 and e >= 2:
                        act.wait_ge(s_ed, 4 * (e - 1))
                    act_hi(n, AE[e % 2][:, 0, m, :], SLOTS)
                    if m < 2 and e + 2 <= E:
                        ffn_hi(e + 2, m)
                for c in range(5):
                    if c < 4 and e + 1 < E:
                        xg_hi(4 * (e + 1) + c)
                    if c:
                        y_out(4 * e + c - 1)
                if e + 2 <= E:
                    ffn_hi(e + 2, 2)

        @block.vector
        def _(dve):
            V = nc.vector
            made = [0]

            def link(ins):
                made[0] += 1
                ins.then_inc(s_dve, 1)
                dve.wait_ge(s_dve, made[0])

            dve.wait_ge(s_edges, 32)
            link(V.tensor_copy(EF[:, :, :], ED[:, :, :, :].rearrange("q s a p -> q s (a p)")))
            link(V.tensor_scalar(EQ[:, 0, :], EF[:, 0, :], 1.0 / T, 0.5 / T - 0.5, ALU.mult, ALU.add))
            link(V.tensor_scalar(EQ[:, 1, :], EF[:, 1, :], 1.0 / DC, 0.5 / DC - 0.5, ALU.mult, ALU.add))
            link(V.tensor_copy(EG[:, :, :], EQ[:, :, :]))
            link(V.scalar_tensor_tensor(EK[:, 1, :], EG[:, 0, :], -float(T), EF[:, 0, :], ALU.mult, ALU.add))
            link(V.scalar_tensor_tensor(EK[:, 0, :], EG[:, 1, :], 1000.0 - DC, EF[:, 1, :], ALU.mult, ALU.add))
            V.scalar_tensor_tensor(EK[:, 0, :], EG[:, 0, :], float(DC), EK[:, 0, :], ALU.mult, ALU.add
                                   ).then_inc(s_keys, 1)
            dve.wait_ge(s_const, 15)
            link(V.tensor_scalar(QI[:, :], MX[:, :], 1.0 / DC, 0.5 / DC - 0.5, ALU.mult, ALU.add))
            link(V.tensor_copy(MM[:, :], QI[:, :]))
            link(V.scalar_tensor_tensor(KEY[:, KT:KA], MM[:, :], 1000.0 - DC, ZZ[:, :], ALU.mult, ALU.add))
            dve.wait_ge(s_once, 1)
            link(V.tensor_copy(KEY[:, PADT:PADT + ET], PS[0:T, 7, 0:ET]))
            link(V.tensor_copy(SLO[:, PADT:PADT + ET], PS[0:T, 7, ET:2 * ET]))

            def norm(X, BSt, MVt, tiles, turn):
                for i in tiles:
                    for a in range(2):
                        V.bn_stats(BSt[:, i, a, :], X[:, i, DH * a:DH * a + DH]).then_inc(s_dve, 1)
                        made[0] += 1
                dve.wait_ge(s_dve, made[0])
                for i in tiles:
                    V.bn_aggr(MVt[:, i, :], BSt[:, i, :, :].rearrange("p a s -> p (a s)")).then_inc(s_dve, 1)
                    made[0] += 1
                dve.wait_ge(s_dve, made[0])
                a, b = tiles[0], tiles[-1] + 1
                V.tensor_scalar(MVt[:, a:b, 1], MVt[:, a:b, 1], EPS, None, ALU.add).then_inc(s_var, 1)
                dve.wait_ge(s_sd, turn)
                link(V.reciprocal(SD[:, a:b], SD[:, a:b]))
                link(V.tensor_scalar(SD[:, a:b], SD[:, a:b], SX, None, ALU.mult))

            for b in range(2):
                dve.wait_ge(s_x[b], 16)
                norm(XA, BS1, MV1, range(5 * b, 5 * b + 5), b + 1)
                for i in range(5 * b, 5 * b + 5):
                    V.tensor_scalar(XA[:, i, :], XA[:, i, :], MV1[:, i, 0:1], SD[:, i:i + 1], ALU.subtract,
                                    ALU.mult).then_inc(s_xn, 1)
            for i in range(NT):
                dve.wait_ge(s_xth, i + 1)
                b = 6 - 2 * (i % 2)
                V.tensor_tensor(XTR[:, i % 3, 1].rearrange("p (a k) n -> p a (k n)", a=2), PS[:, b:b + 2, 0:375],
                                XTR[:, i % 3, 0].rearrange("p (a k) n -> p a (k n)", a=2), ALU.subtract
                                ).then_inc(s_xtl, 1)

            def w1_lo(h):
                for k in range(KD):
                    u = w1_use(h, k)
                    dve.wait_ge(s_wh, KD * h + k + 1)
                    V.scalar_tensor_tensor(W1S[:, k, 1, :], WST[:, u % 2, 0:C], SW, W1S[:, k, 0, :], ALU.mult,
                                           ALU.subtract).then_inc(s_wl, 1)

            def h_lo(h, i):
                q = NT * h + i
                if i == 0:
                    dve.wait_ge(s_arep, 32 * (h + 1))
                dve.wait_ge(s_hh, q + 1)
                for a in range(2):
                    V.tensor_tensor_reduce(HB[h % 2][:, i, 1, :], PS[0:T, 6 + i % 2, :], AR1[:, a, :],
                                           1.0 / (SX * SW), 0.0, ALU.mult, ALU.add, AL[:, a, h, i:i + 1]
                                           ).then_inc(s_dve, 1)
                    made[0] += 1
                    dve.wait_ge(s_dve, made[0])
                V.scalar_tensor_tensor(HB[h % 2][:, i, 1, :], PS[0:T, 6 + i % 2, :], 1.0 / SW,
                                       HB[h % 2][:, i, 0, :], ALU.mult, ALU.subtract).then_inc(s_hl, 1)

            w1_lo(0)
            for i in range(NT):
                h_lo(0, i)

            dve.wait_ge(s_xT, NT)
            with dve.Fori(0, KA // 4) as t:
                for u in range(4):
                    V.tensor_scalar(OL[:, bass.ds(4 * t + u, 1), :], iot[:, :].rearrange("p (o n) -> p o n", o=1),
                                    SLO[:, bass.ds(4 * t + u, 1)], None, ALU.is_equal).then_inc(s_ol, 1)
            with dve.Fori(0, NC // GC) as g:
                n = 0
                for c in range(GC):
                    for kind, t in jobs[c]:
                        col = (t + GT * g) if kind == "e" else (KT + t + 2 * g)
                        if n >= 4:
                            dve.wait_ge(s_cm, g * NJ + n - 2)
                        else:
                            dve.wait_ge(s_cm, g * NJ + 1)
                        V.tensor_scalar(OR[:, n % 4, :], iok[:, :], 1000.0 * c, KEY[:, bass.ds(col, 1)],
                                        ALU.add, ALU.is_equal).then_inc(s_or, 1)
                        n += 1
                dve.wait_ge(s_or, (g + 1) * NJ)
                V.tensor_scalar(KEY[:, :], KEY[:, :], -1000.0 * GC, None, ALU.add).then_inc(s_k2, 1)
                dve.wait_ge(s_k2, g + 1)
            dve.wait_ge(s_ce, 1 + NC)
            V.tensor_reduce(MX[:, 0:1], CS[:, :], AX.X, ALU.add).then_inc(s_cs, 1)
            dve.wait_ge(s_once, 2)
            V.tensor_copy(flag[:, :], PS[:, 7, 0:1]).then_inc(s_cs, 1)
            dve.wait_ge(s_cs, 2)
            total = dve.value_load(flag[0:1, 0:1])
            with dve.If(total != TOTAL):
                V.tensor_scalar(KEY[:, :], KEY[:, :], 1000.0 * NC, None, ALU.add).then_inc(s_gk, 1)
                dve.wait_ge(s_gk, 1)
                with dve.Fori(0, NC) as c:
                    with dve.Fori(0, KA // 2) as t:
                        for u in range(2):
                            dve.wait_ge(s_gu, 1 + c * KA + 2 * t + u)
                            V.tensor_scalar(OR[:, u, :], iok[:, :], 0.0, KEY[:, bass.ds(2 * t + u, 1)],
                                            ALU.add, ALU.is_equal).then_inc(s_go, 1)
                    dve.wait_ge(s_gd, c + 1)
                    V.tensor_copy(CT[:, :, bass.ds(c * DC, DC)],
                                  PS[0:T, 5, 0:KC].rearrange("p (i n) -> p i n", n=DC)).then_inc(s_gk, 1)
                    V.tensor_scalar(KEY[:, :], KEY[:, :], -1000.0, None, ALU.add).then_inc(s_gk, 1)
                    dve.wait_ge(s_gk, 2 * c + 3)
            V.tensor_copy(MX[:, 0:1], CS[:, 0:1]).then_inc(s_ctok, 1)

            for j in range(NT):
                dve.wait_ge(s_mt, j + 1)
                if j >= 2:
                    dve.wait_ge(s_ms[j % 2], 16 * (j // 2))
                b = 2 * (j % 3)
                V.tensor_scalar(MSK[:, j % 2, :].rearrange("p (a i n) -> p a i n", a=2, n=T),
                                blocks16(PH, T, b), 0.0, NEG, ALU.is_equal, ALU.mult).then_inc(s_mm, 1)

            dve.wait_ge(s_a2v, 32)
            for ch in range(NCH):
                u = v2_use(ch)
                dve.wait_ge(s_wst[u % 2], 16 * (u // 2 + 1))
                dve.wait_ge(s_wl, u)
                for a in range(2):
                    ins = V.tensor_tensor_reduce(VJ[:, :], WST[:, u % 2, :], A2R[:, a, :], SW, 0.0, ALU.mult,
                                                 ALU.add, V2F[:, ch, a:a + 1])
                    if a == 0:
                        link(ins)
                ins.then_inc(s_wl, 1)
            dve.wait_ge(s_wl, KD + NCH)
            link(V.tensor_copy(V2S[:, :, 0, :], V2F[:, :, :]))
            link(V.tensor_tensor(V2S[:, :, 1, :], V2F[:, :, :], V2S[:, :, 0, :], ALU.subtract))
            link(V.memset(A2C[:, :], 0.0))

            def chain_row(h):
                dve.wait_ge(s_alt, h + 1)
                if h:
                    dve.wait_ge(s_aad, 16 * h)
                V.tensor_copy(TR[0:NT, :], PS[0:NT, 6, 0:T]).then_inc(s_alc, 1)

            def chain_max(h, js):
                if js[0] == 0:
                    dve.wait_ge(s_row, 16 * (h + 1))
                for j in js:
                    n = NT * h + j
                    dve.wait_ge(s_ml[j % 2], 16 * (n // 2 + 1))
                    V.tensor_tensor_reduce(MSK[:, j % 2, :], MSK[:, j % 2, :], ROW[:, 0, :], 1.0, 3.0 * NEG,
                                           ALU.add, ALU.max, MX[:, j:j + 1]).then_inc(s_mu, 1)

            def chain_shift(h):
                dve.wait_ge(s_mu, NT * (h + 1))
                aD = AL[:, 1, h, :]
                link(V.tensor_tensor(ZZ[:, :], MX[:, :], aD, ALU.add))
                link(V.scalar_tensor_tensor(MM[:, :], ZZ[:, :], SLOPE, ZZ[:, :], ALU.mult, ALU.max))
                link(V.tensor_tensor(AA[:, 0, :], aD, MM[:, :], ALU.subtract))
                V.scalar_tensor_tensor(AA[:, 1, :], aD, SLOPE, MM[:, :], ALU.mult, ALU.subtract).then_inc(s_aa, 1)
                V.tensor_scalar(ALF[:, h, :], AL[:, 0, h, :], SLOPE, None, ALU.mult).then_inc(s_al, 1)

            def chain_shift_rows(h):
                dve.wait_ge(s_aat, h + 1)
                dve.wait_ge(s_ald, 16 * (h + 1))
                V.tensor_copy(TR[:, :], PS[0:2 * NT, 6, 0:T]).then_inc(s_aac, 1)

            def p_leaky(h, i):
                q = NT * h + i
                dve.wait_ge(s_p1, q + 1)
                V.scalar_tensor_tensor(tmp(h, i)[0][:, :], ROW[:, 0, :], AL[:, 0, h, i:i + 1], tmp(h, i)[0][:, :],
                                       ALU.add, ALU.max).then_inc(s_p2, 1)

            def p_count(h, i):
                q = NT * h + i
                dve.wait_ge(s_p3, q + 1)
                V.scalar_tensor_tensor(tmp(h, i)[0][:, :], tmp(h, i)[0][:, :], 1.0, CT[:, i, :], ALU.min, ALU.mult
                                       ).then_inc(s_p4, 1)

            def p_step(h, i):
                if i < NT:
                    p_leaky(h, i)
                if 1 <= i <= NT:
                    p_count(h, i - 1)

            chain_row(0)
            chain_max(0, range(NT))
            chain_shift(0)
            chain_shift_rows(0)
            w1_lo(1)
            for i in range(NT + 1):
                if i < NT:
                    h_lo(1, i)
                p_step(0, i)

            def att_read(h, c):
                a = 5 * h + c + 1
                t = 3 * (a % 2)
                dve.wait_ge(s_att, a + 1)
                for b, (lo, n) in enumerate(BLK):
                    if c < 0:
                        ins = V.reciprocal(RDEN[:, lo:lo + n], PS[:, t + b, 0:n])
                        ins.then_inc(s_rd, 1)
                    else:
                        y = 3 * (CH * h + c) + b
                        if y >= 3:
                            dve.wait_ge(s_y6, y - 2)
                        V.tensor_tensor(YB[:, y % 3, 0:n], PS[:, t + b, 0:n], RDEN[:, lo:lo + n], ALU.mult
                                        ).then_inc(s_y1, 1)

            def y_elu(h, c, b):
                y = 3 * (CH * h + c) + b
                n = BLK[b][1]
                dve.wait_ge(s_y2, y + 1)
                V.scalar_tensor_tensor(YB[:, y % 3, 0:n], YB[:, y % 3, 0:n], 1.0, RB[:, y % 2, 0:n], ALU.min,
                                       ALU.add).then_inc(s_y3, 1)

            def a2_add(g):
                dve.wait_ge(s_a2, g + 1)
                if g:
                    dve.wait_ge(s_a2r, g)
                V.tensor_tensor(A2C[:, :], A2C[:, :], PS[0:T, 7, 0:2 * NT], ALU.add).then_inc(s_a2r, 1)

            def w2_lo(ch):
                dve.wait_ge(s_w2h, ch + 1)
                V.scalar_tensor_tensor(W2S[ch][:, 1, :], W2G[ch % 3][:, :], SW, W2S[ch][:, 0, :], ALU.mult,
                                       ALU.subtract).then_inc(s_w2l, 1)

            for h in range(H):
                att_read(h, -1)
                if h + 1 < H:
                    chain_row(h + 1)
                if h:
                    a2_add(CH * h - 1)
                dve.wait_ge(s_rd, 3 * (h + 1))
                for c in range(CH):
                    if c == CH - 1 and h + 1 < H:
                        for i in range(NPRE):
                            p_step(h + 1, i)
                    att_read(h, c)
                    for b in range(3):
                        y_elu(h, c, b)
                    if c == 1 and h + 1 < H:
                        chain_shift_rows(h + 1)
                    if c:
                        a2_add(CH * h + c - 1)
                    if c == 0 and h + 1 < H:
                        chain_max(h + 1, range(NT))
                        chain_shift(h + 1)
                    if c == 2 and h + 2 < H:
                        w1_lo(h + 2)
                    if h + 1 == H:
                        for ch in range(4 * c, 4 * c + 4):
                            w2_lo(ch)
                if h + 1 < H:
                    for i in range(NPRE, NT + NPRE):
                        if h + 2 < H:
                            h_lo(h + 2, i - NPRE)
                        if i < NT + 1:
                            p_step(h + 1, i)
            a2_add(NCH - 1)
            dve.wait_ge(s_a2r, NCH)

            link(V.tensor_scalar(AL[:, 0, H, :], A2C[:, 0:2 * NT:2], 1.0 / (SX * SW), None, ALU.mult))
            V.tensor_scalar(AL[:, 1, H, :], A2C[:, 1:2 * NT:2], 1.0 / (SX * SW), None, ALU.mult).then_inc(s_al4, 1)
            dve.wait_ge(s_al4, 1)
            chain_row(H)
            chain_max(H, range(NT))
            chain_shift(H)
            chain_shift_rows(H)

            def h2_lo(j):
                dve.wait_ge(s_h2h, j + 1)
                b = 2 * (j % 2)
                V.memset(H2[j][:, 0, D:D + 1], 1.0).then_inc(s_h2o, 1)
                V.memset(H2[j][:, 1, D:D + 1], 0.0).then_inc(s_h2o, 1)
                V.scalar_tensor_tensor(H2[j][:, 1, 0:D].rearrange("p (a n) -> p a n", a=2),
                                       PS[0:T, b:b + 2, 0:DH], 1.0 / SW,
                                       H2[j][:, 0, 0:D].rearrange("p (a n) -> p a n", a=2), ALU.mult,
                                       ALU.subtract).then_inc(s_h2l, 1)

            for i in range(NT + 1):
                p_step(H, i)
                if i < NT:
                    h2_lo(i)
            def x2t_lo(i):
                dve.wait_ge(s_x2h, i + 1)
                b = 2 * (i % 2)
                V.tensor_tensor(X2T[:, 1, :, T * i:T * i + T].rearrange("p (a k) n -> p a k n", a=2),
                                PS[:, b:b + 2, 0:375].rearrange("p a (k n) -> p a k n", n=T),
                                X2T[:, 0, :, T * i:T * i + T].rearrange("p (a k) n -> p a k n", a=2),
                                ALU.subtract).then_inc(s_x2lo, 1)

            dve.wait_ge(s_wh, KD * H + 1)
            V.scalar_tensor_tensor(WRS[:, :, 1, :], WRG[:, :, :], SW, WRS[:, :, 0, :], ALU.mult, ALU.subtract
                                   ).then_inc(s_wl, 1)
            for j in range(NT):
                dve.wait_ge(s_at2, j + 1)
                b = 4 + 2 * (j % 2)
                link(V.reciprocal(ZZ[:, j:j + 1], PS[0:T, b + 1, DH - 1:DH]))
                link(V.tensor_scalar(ZZ[:, j:j + 1], ZZ[:, j:j + 1], 1.0 / SX, None, ALU.mult))
                dve.wait_ge(s_xb, j + 1)
                link(V.scalar_tensor_tensor(X2[:, j, 0:DH + 1], PS[0:T, b, 0:DH + 1], ZZ[:, j:j + 1],
                                            X2[:, j, 0:DH + 1], ALU.mult, ALU.add))
                V.scalar_tensor_tensor(X2[:, j, DH + 1:D], PS[0:T, b + 1, 0:DH - 1], ZZ[:, j:j + 1],
                                       X2[:, j, DH + 1:D], ALU.mult, ALU.add).then_inc(s_x2, 1)

                dve.wait_ge(s_x2, j + 1)
                norm(X2, BS, MV, (j,), 3 + j)
                if j >= 2:
                    dve.wait_ge(s_x2t, j - 1)
                    dve.wait_ge(s_xns[j % 2], 16 * (j // 2))
                V.tensor_scalar(XN2[:, j % 2, :], X2[:, j, :], MV[:, j, 0:1], SD[:, j:j + 1], ALU.subtract,
                                ALU.mult).then_inc(s_xn2, 1)
                if j:
                    x2t_lo(j - 1)


            def ffn_lo(n, q):
                dve.wait_ge(s_wgh, 3 * n + q + 1)
                V.scalar_tensor_tensor(WS[n % 2][:, 1, HALF * q:HALF * q + HALF],
                                       (WG0 if n == 0 and q < 2 else WG)[:, HALF * q:HALF * q + HALF], SW,
                                       WS[n % 2][:, 0, HALF * q:HALF * q + HALF], ALU.mult, ALU.subtract
                                       ).then_inc(s_wgl, 1)

            ffn_lo(0, 0)
            x2t_lo(NT - 1)
            ffn_lo(0, 1)
            ffn_lo(0, 2)
            dve.wait_ge(s_lg, 1)
            dve.wait_ge(s_const, 22)
            link(V.tensor_scalar(LG[:, :, :], PS[0:T, 7, 0:NT * E].rearrange("p (j e) -> p j e", e=E),
                                 1.0 / (SX * SW), None, ALU.mult))
            link(V.tensor_reduce(RK[:, 0, :], LG[:, :, :], AX.X, ALU.max))
            V.tensor_tensor(LG[:, :, :], LG[:, :, :], RK[:, 0, :].unsqueeze(2).to_broadcast([T, NT, E]),
                            ALU.subtract).then_inc(s_lgm, 1)

            def gate_up(n, w):
                dve.wait_ge(s_sg, n + 1)
                dve.wait_ge(s_udn, n + 1)
                V.scalar_tensor_tensor(SG[:, n % 2, 0:w], PS[:, 7, 0:w], SA / (SX * SW),
                                       SG[:, n % 2, 0:w], ALU.mult, ALU.mult).then_inc(s_gx, 1)

            dve.wait_ge(s_pe, 1)
            link(V.tensor_reduce(RK[:, 0, :], LG[:, :, :], AX.X, ALU.add))
            link(V.reciprocal(RK[:, 1, :], RK[:, 0, :]))
            link(V.tensor_tensor(LG[:, :, :], LG[:, :, :], RK[:, 1, :].unsqueeze(2).to_broadcast([T, NT, E]),
                                 ALU.mult))
            for j in range(NT):
                link(V.max(M8[:, j, :], LG[:, j, :]))
                link(V.max_index(I8[:, j, :], M8[:, j, :], LG[:, j, :]))
            gate_up(0, BLK[0][1])
            link(V.tensor_copy(IK[:, 0, :], I8[:, :, 0]))
            link(V.tensor_copy(IK[:, 1, :], I8[:, :, 1]))
            link(V.tensor_tensor(RK[:, 0, :], M8[:, :, 0], M8[:, :, 1], ALU.add))
            link(V.tensor_scalar(RK[:, 0, :], RK[:, 0, :], 1e-9, None, ALU.max))
            link(V.reciprocal(RK[:, 1, :], RK[:, 0, :]))
            for k in range(2):
                link(V.tensor_tensor(WK[:, k, :], M8[:, :, k], RK[:, 1, :], ALU.mult))
                link(V.tensor_tensor(OK[k][:, :, :], io8[:, :].unsqueeze(1).to_broadcast([T, NT, E]),
                                     IK[:, k, :].unsqueeze(2).to_broadcast([T, NT, E]), ALU.is_equal))
                link(V.tensor_tensor(OT[k][:, :, :], OK[k][:, :, :],
                                     tokid[:, :].unsqueeze(2).to_broadcast([T, NT, E]), ALU.mult))
                for r in range(3):
                    link(V.tensor_copy(O3[k][:, :, E * r:E * r + E], OK[k][:, :, :]))
            gate_up(1, BLK[1][1])
            link(V.tensor_tensor(SS[:, :, :], OK[0][:, :, :], WK[:, 0, :].unsqueeze(2).to_broadcast([T, NT, E]),
                                 ALU.mult))
            link(V.tensor_tensor(LG[:, :, :], OK[1][:, :, :], WK[:, 1, :].unsqueeze(2).to_broadcast([T, NT, E]),
                                 ALU.mult))
            link(V.tensor_tensor(SS[:, :, :], SS[:, :, :], LG[:, :, :], ALU.add))
            link(V.tensor_tensor(LG[:, :, :], OK[0][:, :, :], OK[1][:, :, :], ALU.add))
            link(V.tensor_scalar(LG[:, :, :], LG[:, :, :], -1.0, None, ALU.add))
            link(V.tensor_tensor(SS[:, :, :], SS[:, :, :], LG[:, :, :], ALU.add))
            for r in range(2):
                link(V.tensor_copy(S3[:, :, E * r:E * r + E], SS[:, :, :]))
                link(V.tensor_tensor(SS[:, :, :], SS[:, :, :], S3[:, :, E * r:E * r + E], ALU.subtract))
            link(V.memset(CA[:, :, :, :], 0.0))
            V.tensor_copy(S3[:, :, 2 * E:3 * E], SS[:, :, :]).then_inc(s_s3, 1)
            ffn_lo(1, 0)
            gate_up(2, BLK[2][1])
            ffn_lo(1, 1)
            for n in range(3):
                dve.wait_ge(s_s3t, n + 1)
                for b in range(2):
                    dve.wait_ge(s_xns[b], 16 * NT // 2)
                dve.wait_ge(s_x2t, NT)
                V.tensor_copy([S3T, O3T[0], O3T[1]][n][:, :].rearrange("p (a j n) -> p a j n", a=2, n=T),
                              blocks16(PB, 24, 2 * n)).then_inc(s_s3c, 1)

            def rank(r):
                j, k = divmod(r, 2)
                t = 3 * (r % 2)
                R = PSF[0:T, 512 * t:512 * t + N]
                own = WK[:, k, j:j + 1]
                dve.wait_ge(s_rr, r + 1)
                if r:
                    dve.wait_ge(s_rk, r)
                if j:
                    V.tensor_scalar(JN2[:, 0:T * j], R[:, 0:T * j], own, None, ALU.is_ge, ALU.add,
                                    accum_out=CA[:, 0, k, j:j + 1]).then_inc(s_dve, 1)
                    made[0] += 1
                    dve.wait_ge(s_dve, made[0])
                link(V.tensor_scalar(JN2[:, T * j:N], R[:, T * j:N], own, None, ALU.is_gt, ALU.add,
                                     accum_out=CA[:, 1, k, j:j + 1]))
                V.scalar_tensor_tensor(JN2[:, 0:T], R[:, T * j:T * j + T], own, TRI[:, :], ALU.is_equal, ALU.mult,
                                       accum_out=CA[:, 2, k, j:j + 1]).then_inc(s_rk, 1)

            for n in range(3, 9):
                if n >= RANK_FROM:
                    rank(3 * (n - RANK_FROM))
                gate_up(n, BLK[n % 3][1])
                if n == 3:
                    ffn_lo(1, 2)
                if n >= RANK_FROM:
                    rank(3 * (n - RANK_FROM) + 1)
                    rank(3 * (n - RANK_FROM) + 2)
            for r in range(3 * (9 - RANK_FROM), 2 * NT):
                rank(r)
            dve.wait_ge(s_rk, 2 * NT)
            link(V.tensor_tensor(RK[:, :, :], CA[:, 0, :, :], CA[:, 1, :, :], ALU.add))
            link(V.tensor_tensor(RK[:, :, :], RK[:, :, :], CA[:, 2, :, :], ALU.add))
            for k in range(2):
                for j in range(NT):
                    V.tensor_scalar(IND[:, k, j, :], io392[:, :], RK[:, k, j:j + 1], None, ALU.is_equal
                                    ).then_inc(s_ind, 1)
            link(V.tensor_scalar(CA[:, 0, :, :], RK[:, :, :], float(CAP), 1.0e6, ALU.is_ge, ALU.mult))
            link(V.tensor_tensor(RK[:, :, :], RK[:, :, :], CA[:, 0, :, :], ALU.add))
            link(V.tensor_scalar(CA[:, 0, :, :], IK[:, :, :], E - 1.0, None, ALU.is_equal))
            link(V.scalar_tensor_tensor(CA[:, 1, :, :], IK[:, :, :], float(SLOTS), RK[:, :, :], ALU.mult, ALU.add))
            link(V.tensor_scalar(CA[:, 2, :, :], CA[:, 1, :, :], -2.0e6, None, ALU.add))
            link(V.tensor_tensor(CA[:, 2, :, :], CA[:, 2, :, :], CA[:, 0, :, :], ALU.mult))
            link(V.tensor_tensor(RK[:, 0, :], CA[:, 2, 0, :], CA[:, 2, 1, :], ALU.add))
            link(V.tensor_scalar(RK[:, 0, :], RK[:, 0, :], 2.0e6, None, ALU.add))
            link(V.tensor_copy(IDX[0:T, 2, :], RK[:, 0, :]))
            link(V.scalar_tensor_tensor(CA[:, 1, :, :], CA[:, 0, :, :], 2.0e6, CA[:, 1, :, :], ALU.mult, ALU.add))
            link(V.tensor_copy(IDX[0:T, 0:2, :], CA[:, 1, :, :]))
            link(V.tensor_tensor(CA[:, 2, :, :], CA[:, 0, :, :], WK[:, :, :], ALU.mult))
            link(V.tensor_tensor(WL[:, :], CA[:, 2, 0, :], CA[:, 2, 1, :], ALU.add))
            dve.wait_ge(s_tk, 1)
            V.tensor_copy(TOK[0:SC, :, :], PS[0:SC, 0, 0:4 * E].rearrange("p (c e) -> p c e", e=E)).then_inc(s_tok, 1)

            def xg_lo(g):
                e, c = divmod(g, 4)
                dve.wait_ge(s_xgh, g + 1)
                b = 2 + 2 * (g % 2)
                V.tensor_tensor(XGT[e % 2][:, 1, :, SC * c:SC * c + SC].rearrange("p (a k) n -> p a k n", a=2),
                                PS[:, b:b + 2, 0:3 * SC].rearrange("p a (k n) -> p a k n", n=SC),
                                XGT[e % 2][:, 0, :, SC * c:SC * c + SC].rearrange("p (a k) n -> p a k n", a=2),
                                ALU.subtract).then_inc(s_xgl, 1)

            def add_back(n):
                j, k = divmod(n, 2)
                b = n % GRN
                if n == 0:
                    dve.wait_ge(s_sdr, NT)
                dve.wait_ge(s_gg[b], 16 * (n // GRN + 1))
                if n:
                    dve.wait_ge(s_g1, n)
                V.scalar_tensor_tensor(X2[:, j, :], GR[0:T, b, :], WK[:, k, j:j + 1], X2[:, j, :], ALU.mult,
                                       ALU.add).then_inc(s_g1, 1)
                if n + GRN < 2 * NT:
                    dve.wait_ge(s_g1, n + 1)
                    V.memset(GR[:, b, :], 0.0).then_inc(s_gz, 1)

            for c in range(4):
                xg_lo(c)
            for e in range(E):
                for m in range(KI):
                    gate_up(9 + KI * e + m, SLOTS)
                    if m < 2 and e + 2 <= E:
                        ffn_lo(e + 2, m)
                    if m == 1 and e == E - 1:
                        add_back(0)
                        add_back(1)
                if e + 1 < E:
                    for c in range(4):
                        xg_lo(4 * (e + 1) + c)
                if e + 2 <= E:
                    ffn_lo(e + 2, 2)
            for n in range(2, 2 * NT):
                add_back(n)
            dve.wait_ge(s_g1, 2 * NT)
            for j in range(NT):
                dve.wait_ge(*last_in[j])
                V.scalar_tensor_tensor(X2[:, j, :], GRL[0:T, j, :], WL[:, j:j + 1], X2[:, j, :], ALU.mult, ALU.add
                                       ).then_inc(s_gl, 1)

        @block.tensor
        def _(pe):
            M = nc.tensor.matmul

            def mm3(out_, lhs, rhs, first, last):
                for a, b in ((0, 0), (0, 1), (1, 0)):
                    ins = M(out_, lhs(a), rhs(b), start=first and a + b == 0, stop=last and a == 1)
                return ins

            pe.wait_ge(s_const, 15)
            pe.wait_ge(s_keys, 1)
            for a in range(2):
                for q in range(2):
                    ins = nc.tensor.transpose(PS[0:T, 7, ET * a + 85 * q:ET * a + 85 * q + 85],
                                              EK[:, a, T * q:T * q + T], idf[0:85, 0:85])
            ins.then_inc(s_once, 1)
            for i in range(NT):
                pe.wait_ge(s_xn, i + 1)
                if i == 0:
                    pe.wait_ge(s_xn, NT)
                if i >= 2:
                    pe.wait_ge(s_xtl, i - 1)
                b = 6 - 2 * (i % 2)
                for k in range(KD):
                    ins = nc.tensor.transpose(PS[:, b + k // 3, T * (k % 3):T * (k % 3) + T],
                                              XA[:, i, 128 * k:128 * k + 128], idf[0:T, 0:T])
                ins.then_inc(s_xT, 1)

            def proj(h):
                pe.wait_ge(s_wl, w1_use(h, KD - 1) + 1)
                for i in range(NT):
                    v = NT + NT * h + i
                    pe.wait_ge(s_xts[v % 3], 16 * (v // 3 + 1))
                    if i == 0 and h == 0:
                        pe.wait_ge(s_xtl, NT)
                    if NT * h + i >= 2:
                        pe.wait_ge(s_hl, NT * h + i - 1)
                    if i < 2 and h:
                        pe.wait_ge(s_alc, h)
                        if h >= 2:
                            pe.wait_ge(s_a2r, CH * (h - 1) - 1)
                    for k in range(KD):
                        ins = mm3(PS[0:T, 6 + i % 2, :], lambda a: XTR[:, v % 3, a, k, :],
                                  lambda b: W1S[:, k, b, :], k == 0, k == KD - 1)
                    ins.then_inc(s_proj, 1)

            def chain_row(h):
                if h < H:
                    pe.wait_ge(s_hl, NT * (h + 1))
                else:
                    pe.wait_ge(s_al4, 1)
                nc.tensor.transpose(PS[0:NT, 6, 0:T], AL[:, 0, h, :], idf[0:T, 0:T]).then_inc(s_alt, 1)

            def chain_shift(h):
                pe.wait_ge(s_aa, h + 1)
                nc.tensor.transpose(PS[0:2 * NT, 6, 0:T], AA[:, :, :].rearrange("p a i -> p (a i)"),
                                    idf[0:T, 0:T]).then_inc(s_aat, 1)

            proj(0)
            pe.wait_ge(s_ol, KA)
            pe.sem_inc(s_cm, 1)
            pe.sem_inc(s_gu, 1)
            with pe.Fori(0, NC // GC) as g:
                n = 0
                for c in range(GC):
                    pe.wait_ge(s_ce, 1 + GC * g)
                    for q, (kind, t) in enumerate(jobs[c]):
                        col = (t + GT * g) if kind == "e" else (KT + t + 2 * g)
                        pe.wait_ge(s_or, g * NJ + n + 1)
                        ins = M(PS[0:T, c, 0:KC], OL[:, bass.ds(col, 1), :], OR[:, n % 4, :], start=q == 0,
                                stop=q == len(jobs[c]) - 1)
                        ins.then_inc(s_cm, 1)
                        n += 1
            pe.wait_ge(s_cs, 1)
            M(PS[:, 7, 0:1], onesf[:, :], MX[:, 0:1], start=True, stop=True).then_inc(s_once, 1)
            pe.wait_ge(s_cs, 2)
            total = pe.value_load(flag[0:1, 0:1])
            with pe.If(total != TOTAL):
                with pe.Fori(0, NC) as c:
                    pe.wait_ge(s_gk, 2 * c + 1)
                    M(PS[0:T, 5, 0:KC], OL[:, 0, :], iok[:, :], start=True, stop=False)
                    with pe.Fori(0, KA // 2) as t:
                        for u in range(2):
                            pe.wait_ge(s_go, c * KA + 2 * t + u + 1)
                            M(PS[0:T, 5, 0:KC], OL[:, bass.ds(2 * t + u, 1), :], OR[:, u, :], start=False,
                              stop=False).then_inc(s_gu, 1)
                    M(PS[0:T, 5, 0:KC], OL[:, 0, :], iok[:, :], start=False, stop=True).then_inc(s_gd, 1)
            pe.wait_ge(s_ctok, 1)
            for j in range(NT):
                if j >= 3:
                    pe.wait_ge(s_mm, j - 2)
                b = 2 * (j % 3)
                for i in range(NT):
                    ins = nc.tensor.transpose(PH[0:T, col16(b, i):col16(b, i) + T], CT[:, i, T * j:T * j + T], idh[0:T, 0:T])
                ins.then_inc(s_mt, 1)
            chain_row(0)
            chain_shift(0)
            pe.wait_ge(s_aac, 1)
            proj(1)

            def att(h, c):
                a_ = 5 * h + c + 1
                t = 3 * (a_ % 2)
                if a_ >= 2:
                    g2 = a_ - 2
                    h0, c0 = divmod(g2, 5)
                    if c0 == 0:
                        pe.wait_ge(s_rd, 3 * (h0 + 1))
                    else:
                        pe.wait_ge(s_y1, 3 * (CH * h0 + c0))
                else:
                    pe.wait_ge(s_mm, NT)
                for i in range(NT):
                    if c < 0:
                        pe.wait_ge(s_p6, NT * h + i + 1)
                        for b, (lo, n) in enumerate(BLK):
                            for part in range(2):
                                ins = M(PS[:, t + b, 0:n], ones[:, :], P[:, i, part, lo:lo + n],
                                        start=i == 0 and part == 0, stop=i == NT - 1 and part == 1)
                    else:
                        hb = HB[h % 2]
                        if c == 2 and i == 5 and h + 1 < H:
                            chain_shift(h + 1)
                        for pa, pb in ((0, 0), (0, 1), (1, 0)):
                            for b, (lo, n) in enumerate(BLK):
                                ins = M(PS[:, t + b, 0:n], hb[:, i, pa, 128 * c:128 * c + 128],
                                        P[:, i, pb, lo:lo + n], start=i == 0 and pa + pb == 0,
                                        stop=i == NT - 1 and pa == 1)
                        if c == CH - 1 and i < NT - 1:
                            ins.then_inc(s_pf, 1)
                ins.then_inc(s_att, 1)

            def al2(g):
                pe.wait_ge(s_y6, 3 * (g + 1))
                if g:
                    pe.wait_ge(s_a2r, g)
                if g % CH == CH - 1 or g == 0:
                    pe.wait_ge(s_hl, NT * min(H, g // CH + (3 if g else 2)))
                for j in range(NT):
                    ins = mm3(PS[0:T, 7, 2 * j:2 * j + 2], lambda a: H1O[:, g % 2, a, T * j:T * j + T],
                              lambda b: V2S[:, g, b, :], True, True)
                ins.then_inc(s_a2, 1)

            for h in range(H):
                att(h, -1)
                if h + 1 < H:
                    chain_row(h + 1)
                if h:
                    al2(CH * h - 1)
                for c in range(CH):
                    att(h, c)
                    if c:
                        al2(CH * h + c - 1)
                if h + 2 < H:
                    pe.wait_ge(s_aac, h + 2)
                    proj(h + 2)
            al2(NCH - 1)

            chain_row(H)
            for j in range(NT):
                pe.wait_ge(s_ht[j % 2], 16 * (j // 2 + 1))
                if j == 0:
                    pe.wait_ge(s_y1, 3 * NCH)
                if j >= 2:
                    pe.wait_ge(s_h2l, j - 1)
                b = 2 * (j % 2)
                for ch in range(NCH):
                    if j == 0:
                        pe.wait_ge(s_w2l, ch + 1)
                    for q in range(2):
                        ins = mm3(PS[0:T, b + q, 0:DH], lambda a: HT[j % 2][:, a, ch, :],
                                  lambda r: W2S[ch][:, r, DH * q:DH * q + DH], ch == 0, ch == NCH - 1)
                ins.then_inc(s_pj2, 1)
                if j == 1:
                    chain_shift(H)
            def x2_T(i):
                pe.wait_ge(s_xn2, i + 1)
                if i >= 2:
                    pe.wait_ge(s_x2lo, i - 1)
                b = 2 * (i % 2)
                for k in range(KD):
                    ins = nc.tensor.transpose(PS[:, b + k // 3, T * (k % 3):T * (k % 3) + T],
                                              XN2[:, i % 2, 128 * k:128 * k + 128], idf[0:T, 0:T])
                ins.then_inc(s_x2t, 1)

            pe.wait_ge(s_aac, H + 1)
            for j in range(NT):
                if j >= 2:
                    pe.wait_ge(s_x2, j - 1)
                b = 4 + 2 * (j % 2)
                for i in range(NT):
                    if j == 0:
                        pe.wait_ge(s_p6, NT * H + i + 1)
                        pe.wait_ge(s_h2l, i + 1)
                        pe.wait_ge(s_h2o, 2 * (i + 1))
                    for q, (lo, n) in enumerate(((0, DH + 1), (DH + 1, DH))):
                        ins = mm3(PS[0:T, b + q, 0:n], lambda a: P[:, i, a, T * j:T * j + T],
                                  lambda r: H2[i][:, r, lo:lo + n], i == 0, i == NT - 1)
                ins.then_inc(s_at2, 1)
                if j:
                    x2_T(j - 1)

            x2_T(NT - 1)
            pe.wait_ge(s_x2lo, NT)
            pe.wait_ge(s_wl, KD * H + NCH + 1)
            for j in range(NT):
                for k in range(KD):
                    ins = mm3(PS[0:T, 7, E * j:E * j + E], lambda a: X2T[:, a, k, T * j:T * j + T],
                              lambda r: WRS[:, k, r, :], k == 0, k == KD - 1)
            ins.then_inc(s_lg, 1)

            def gate_or_up(n, q, wb, rhs, w, m):
                if n:
                    pe.wait_ge((s_sg, s_gx)[q], n)
                for k in range(KD):
                    ins = mm3(PS[:, 6 + q, 0:w],
                              lambda a: wb[:, a, HALF * q + INNER * k + 128 * m:HALF * q + INNER * k + 128 * m + 128],
                              lambda r: rhs(r, k), k == 0, k == KD - 1)
                ins.then_inc((s_gdn, s_udn)[q], 1)

            def rank_rows(r):
                j, k = divmod(r, 2)
                t = 3 * (r % 2)
                if r >= 2:
                    pe.wait_ge(s_rk, r - 1)
                else:
                    pe.wait_ge(s_s3c, 3)
                for lo in range(0, N, 512):
                    w = min(512, N - lo)
                    ins = M(PSF[0:T, 512 * t + lo:512 * t + lo + w], O3T[k][:, T * j:T * j + T],
                            S3T[:, lo:lo + w], start=True, stop=True)
                ins.then_inc(s_rr, 1)

            def down(lhs, wb, o_):
                for q in range(2):
                    for m in range(KI):
                        ins = mm3(o_(q), lambda a: lhs(a, m),
                                  lambda r: wb[:, r, 2 * HALF + D * m + DH * q:2 * HALF + D * m + DH * q + DH],
                                  m == 0, m == KI - 1)
                return ins

            pe.wait_ge(s_wgl, 3)
            for n in range(9):
                m, b = divmod(n, 3)
                lo, w = BLK[b]
                for q in range(2):
                    if n == 0 and q == 1:
                        pe.wait_ge(s_lgm, 1)
                    gate_or_up(n, q, WS[0], lambda r, k: X2T[:, r, k, lo:lo + w], w, m)
                    if n >= RANK_FROM:
                        for r in ((0,), (1, 2))[q]:
                            rank_rows(3 * (n - RANK_FROM) + r)
                if n == 2:
                    pe.wait_ge(s_s3, 1)
                    for v, S_ in enumerate((S3, O3[0], O3[1])):
                        for j in range(NT):
                            ins = nc.tensor.transpose(PB[0:24, col16(2 * v, j):col16(2 * v, j) + T], S_[:, j, :],
                                                      idb[0:T, 0:T])
                        ins.then_inc(s_s3t, 1)
            pe.wait_ge(s_alo, 9)
            pe.wait_ge(s_gx, 9)
            for j in range(NT):
                if j:
                    pe.wait_ge(s_sdc, j)
                down(lambda a, m: AB[:, a, m, T * j:T * j + T], WS[0], lambda q: PS[0:T, 6 + q, 0:DH]
                     ).then_inc(s_sd3, 1)
                if 3 * (9 - RANK_FROM) + j < 2 * NT:
                    rank_rows(3 * (9 - RANK_FROM) + j)
                if j == 7:
                    pe.wait_ge(s_ind, 2 * NT)
                    pe.wait_ge(s_rk, 2 * NT)
                    for c in range(4):
                        for k in range(2):
                            for i in range(NT):
                                ins = M(PS[0:SC, 0, E * c:E * c + E], IND[:, k, i, SC * c:SC * c + SC],
                                        OT[k][:, i, :], start=k + i == 0, stop=k == 1 and i == NT - 1)
                    ins.then_inc(s_tk, 1)

            def rows_T(g):
                if g == 0:
                    pe.wait_ge(s_tok, 1)
                pe.wait_ge(s_xg[g % XGN], 16 * (g // XGN + 1))
                if g >= 2:
                    pe.wait_ge(s_xgl, g - 1)
                b = 2 + 2 * (g % 2)
                for k in range(KD):
                    ins = nc.tensor.transpose(PS[:, b + k // 3, SC * (k % 3):SC * (k % 3) + SC],
                                              XG[0:SC, g % XGN, 128 * k:128 * k + 128], idf[0:SC, 0:SC])
                ins.then_inc(s_xgt, 1)

            for c in range(4):
                rows_T(c)
            for e in range(E):
                wb = WS[(e + 1) % 2]
                pe.wait_ge(s_xgl, 4 * (e + 1))
                pe.wait_ge(s_wgl, 3 * (e + 2) - 1)
                if e == 0:
                    pe.wait_ge(s_sdc, NT)
                else:
                    pe.wait_ge(s_yo, 4 * e - 1)
                for m in range(KI):
                    for q in range(2):
                        gate_or_up(9 + KI * e + m, q, wb, lambda r, k: XGT[e % 2][:, r, k, :], SLOTS, m)
                for c in range(4):
                    g = 4 * e + c
                    if e + 1 < E:
                        for r in ((0, 1), (2,), (3,), ())[c]:
                            rows_T(4 * (e + 1) + r)
                    if c == 0:
                        pe.wait_ge(s_alo, 9 + KI * (e + 1))
                        pe.wait_ge(s_gx, 9 + KI * (e + 1))
                        pe.wait_ge(s_wgl, 3 * (e + 2))
                    if g >= 2:
                        pe.wait_ge(s_yo, g - 1)
                    b = 6 if c % 2 == 0 else 0
                    down(lambda a, m: AE[e % 2][:, a, m, SC * c:SC * c + SC], wb,
                         lambda q: PS[0:SC, b + q, 0:DH]).then_inc(s_ed, 1)


_INS = ['x', 'src', 'dst', 'L0_gnn_W1', 'L0_gnn_att_src1', 'L0_gnn_att_dst1', 'L0_gnn_b1', 'L0_gnn_W2',
        'L0_gnn_att_src2', 'L0_gnn_att_dst2', 'L0_gnn_b2', 'L0_ffn_Wr', 'L0_ffn_w1', 'L0_ffn_w3', 'L0_ffn_w2',
        'L0_ffn_s1', 'L0_ffn_s3', 'L0_ffn_s2']
_OUTS = [((1250, 768), 'float32')]


def kernel(**inputs):
    import numpy as _np
    import concourse.bacc as _bacc
    from concourse import mybir as _mybir
    from concourse.bass_utils import run_bass_kernel_spmd as _run

    nc = _bacc.Bacc("TRN2", target_bir_lowering=False, num_devices=1)
    arrays, args = {}, []
    for name in _INS:
        a = _np.ascontiguousarray(inputs[name])
        arrays[f"in_{name}_dram"] = a
        args.append(nc.dram_tensor(f"in_{name}_dram", a.shape, _mybir.dt.from_np(a.dtype), kind="ExternalInput").ap())
    for i, (shape, dtype) in enumerate(_OUTS):
        dt = _mybir.dt.from_np(_np.dtype(dtype))
        args.append(nc.dram_tensor(f"out_{i}_dram", shape, dt, kind="ExternalOutput").ap())
    build(nc, *args)
    r = _run(nc, [arrays], core_ids=[0])
    return r.results[0]["out_0_dram"]
```

```python
from contextlib import ExitStack

import numpy as np
import concourse.bass as bass
from concourse import mybir

ALU = mybir.AluOpType
ACT = mybir.ActivationFunctionType
AX = mybir.AxisListType
F32 = mybir.dt.float32
F16 = mybir.dt.float16
BF16 = mybir.dt.bfloat16
I32 = mybir.dt.int32
U32 = mybir.dt.uint32

SX = 64.0
SW = 1024.0
SA = 256.0
NEG = -1.0e30
EPS = 1e-5
SLOPE = 0.2


def build(nc, x, src, dst, W1, as1, ad1, b1, W2, as2, ad2, b2, Wr, w1, w3, w2, s1, s3, s2, out):
    N, D = x.shape
    NE = src.shape[0]
    H, C = as1.shape
    E, _, INNER = w1.shape
    T = 125
    NT = N // T
    KD = D // 128
    CH = C // 128
    NCH = H * CH
    KI = INNER // 128
    CAP = -(-N * 2 * 5 // (E * 4))
    SLOTS = CAP + CAP % 2
    SC = SLOTS // 4
    DH = D // 2
    RO, RG, PG = 12, 4, 2
    GP = 112
    RANK_FROM = 4
    XGN, GRN = 8, 9
    BLK = [(0, 417), (417, 417), (834, 416)]
    assert NT * T == N and NE % T == 0 and SLOTS % 4 == 0

    ET = NE // T
    DC = 50
    NC = N // DC
    GC = 5
    GT = ET // (NC // GC)
    PADT = 4
    MARGIN = 250
    KC = NT * DC
    window = []
    for c in range(GC):
        lo = (c * DC * NE // N - MARGIN) // T
        hi = -(-((c + 1) * DC * NE // N + MARGIN) // T)
        window.append((lo + PADT, hi + PADT))
    assert window[0][0] >= 0 and window[-1][1] <= GT + 2 * PADT
    KT = ET + 2 * PADT
    selfs = [sorted({(c * DC) // T, (c * DC + DC - 1) // T}) for c in range(GC)]
    jobs = [[("e", t) for t in range(*window[c])] + [("s", t) for t in selfs[c]] for c in range(GC)]
    NJ = sum(len(j) for j in jobs)
    KA = KT + NT
    TOTAL = NE + N
    PIECES = [(0, 2), (2, 5), (5, NT)]
    OLP = -(-KA // NT)

    BASE = 16512
    names = [0]

    def at(off, shape, dt):
        names[0] += 1
        return nc.alloc_sbuf_tensor_at(f"sb{names[0]}", list(shape), dt, offset=BASE + off)

    o_ct, o_p, o_h, o_e = 0, 25024, 75040, 116000
    CT = at(o_ct, [T, NT, N], F16)
    P = at(o_p, [T, NT, 2, N], F16)
    OL = at(o_p, [T, KA, T], F16)
    XA = at(o_p, [T, NT, D], F32)
    W1F = at(o_p + 30720, [128, KD, C], F32)
    HB = [at(o_h + b * 20480, [T, NT, 2, C], F16) for b in range(2)]
    ED = at(o_h + 20480, [85, 2, 2, T], I32)
    EF = at(o_h + 20480 + 2048, [85, 2, 2 * T], F32)
    EQ = at(o_h + 20480 + 4096, [85, 2, 2 * T], I32)
    EG = at(o_h + 20480 + 6144, [85, 2, 2 * T], F32)
    EK = at(o_h + 20480 + 8192, [85, 2, 2 * T], F32)
    OR = at(o_h + 20480, [T, RO, KC], F16)
    o = o_e
    ROW = at(o, [T, 2, N], F32); o += 10016
    TMP = [at(o + 5000 // 32 * 32 * b + 32 * b, [T, N], F32) for b in range(3)]
    W2G = [at(o + 3072 * b, [128, D], F32) for b in range(3)]; o += 15072
    MSK = at(o, [T, 2, N], BF16); o += 5024
    o_w2s = o
    XTR = at(o, [128, 3, 2, KD, T], F16); o += 9024
    W1S = at(o, [128, KD, 2, C], F16); o += 12288
    WST = at(o, [128, 2, D], F32); o += 6144
    YB = at(o, [128, 3, 417], F32)
    o += 5024
    RB = at(o, [128, 2, 417], F32); o += 3360
    H1O = at(o, [128, 2, 2, N], F16); o += 10016
    RDEN = at(o, [128, N], F32); o += 5024
    o_a = o
    AR1 = at(o, [T, 2, C], F32); o += 4096
    TMP.append(at(o, [T, N], F32)); o += 5024
    assert o <= 207008, o
    WV = [at(o_e + 3072 * b, [128, D], F32) for b in range(3)]
    A2R = at(o_e + 10016, [128, 2, D], F32)
    VP = [at(o_e + 10016 + 6144 + 3072 * b, [128, D], F32) for b in range(2)]
    MSKT = [MSK] + [at(o_e + 10016 + 5024 * b, [T, 2, N], BF16) for b in range(3)]
    MSKT.append(at(o_a + 4096, [T, 2, N], BF16))
    W2S = [at(o_w2s + 3072 * i, [128, 2, D], F16) for i in range(8)]
    W2S += [at(o_h + 3072 * i, [128, 2, D], F16) for i in range(6)]
    W2S += [at(o_a + 3072 * i, [128, 2, D], F16) for i in range(2)]
    o_y = o_w2s + 9024 + 12288 + 6144
    HT0 = at(o_e, [128, 2, NCH, T], F16)
    HT = [at(o_y + 8000 * b, [128, 2, NCH, T], F16) for b in range(2)]
    H2 = [at(o_h + 6 * 3072 + 3104 * i, [T, 2, D + 2], F16) for i in range(7)]
    assert o_h + 6 * 3072 + 3104 * 7 <= o_e
    H2 += [at(o_y + 16000 + 3104 * i, [T, 2, D + 2], F16) for i in range(2)]
    assert o_y + 16000 + 2 * 3104 <= o_a
    H2.append(at(o_w2s + 30720 + 3072, [T, 2, D + 2], F16))
    X2 = at(o_w2s, [T, NT, D], F32)
    B2R = at(o_w2s + 30720, [T, D], F32)
    X2T = at(o_e, [128, 2, KD, N], F16)
    WG0 = at(0, [128, 2 * 2304], F32)
    XN2 = at(18432, [T, 2, D], F32)
    WG = at(30720, [128, 3 * 2304], F32)
    WS = [at(58368 + b * 27648, [128, 2, 3 * 2304], F16) for b in range(2)]
    o_f = 177792
    AB = at(o_f, [128, 2, KI, N], F16); o = o_f + 15008
    AE = [at(o_f + b * 4704, [128, 2, KI, SLOTS], F16) for b in range(2)]
    SG = at(o, [128, 2, 512], F32); o += 4096
    YO = at(o, [T, 2, D], F32); o += 6144
    assert o <= 203328 and o_w2s + 30720 <= o_f
    BS = at(183040, [T, NT, 2, 6], F32)
    IND = at(0, [T, 2, NT, SLOTS], F16)
    XG = at(0, [GP, XGN, D], F32)
    S3T = at(21824, [24, N], BF16)
    O3T = [at(24352 + k * 2528, [24, N], BF16) for k in range(2)]
    XGT = [at(o_e + b * 9408, [128, 2, KD, SLOTS], F16) for b in range(2)]
    JN2 = at(15680, [T, N], BF16)
    GRL = at(0, [128, NT, D], F32)
    GR = at(30720, [128, GRN, D], F32)

    o = 207008

    def small(shape, dt):
        nonlocal o
        size = int(np.prod(shape[1:])) * {F32: 4, I32: 4, U32: 4, F16: 2, BF16: 2}[dt]
        t = at(o, shape, dt)
        o += -(-size // 32) * 32
        assert BASE + o <= 229344, o
        return t

    idf = small([128, 128], F32)
    idh = small([128, 128], F16)
    idb = small([128, 128], BF16)
    ones = small([T, 128], F16)
    TRI = small([T, T], F16)
    io392 = small([T, SLOTS], F16)
    tokid = small([T, NT], F32)
    io8 = small([T, E], F32)
    LG = small([T, NT, E], F32)
    o_k = o_h + 20480 + 16000
    iok = at(o_k, [T, KC], F16)
    iot = at(o_k + 1024, [T, T], F16)
    KEY = at(o_k + 1280, [T, KA], F32)
    SLO = at(o_k + 2048, [T, KA], F32)
    onesf = at(o_k + 2816, [T, 128], F32)
    b1c = small([128, NCH], F32)
    V2F = small([128, NCH, 2], F32)
    V2S = small([128, NCH, 2, 2], F16)
    AL = small([T, 2, H + 1, NT], F32)
    ALF = small([T, H + 1, NT], F32)
    A2C = small([T, 2 * NT], F32)
    MX = small([T, NT], F32)
    ZZ = small([T, NT], F32)
    MM = small([T, NT], F32)
    AA = small([T, 2, NT], F32)
    TR = small([2 * NT, T], F32)
    CS = small([T, NC], F32)
    flag = small([128, 1], I32)
    QI = small([T, NT], I32)
    SD = small([T, NT], F32)
    def mid(shape, dt):
        nonlocal o
        size = int(np.prod(shape[1:])) * {F32: 4, I32: 4, U32: 4, F16: 2, BF16: 2}[dt]
        t = at(o, shape, dt)
        o += -(-size // 32) * 32
        return t

    o = 113664
    M8 = mid([T, NT, 8], F32)
    I8 = mid([T, NT, 8], U32)
    OK = [mid([T, NT, E], F32) for _ in range(2)]
    SS = mid([T, NT, E], F32)
    IK = mid([T, 2, NT], F32)
    WK = mid([T, 2, NT], F32)
    CA = mid([T, 3, 2, NT], F32)
    assert o <= o_e, (o, o_e)
    o = 203328
    OT = [mid([T, NT, E], F16) for _ in range(2)]
    RK = mid([T, 2, NT], F32)
    S3 = mid([T, NT, 24], BF16)
    O3 = [mid([T, NT, 24], BF16) for _ in range(2)]
    IDX = mid([128, 3, NT], U32)
    TOK = mid([GP, 4, E], U32)
    WL = mid([T, NT], F32)
    WRS = mid([128, KD, 2, E], F16)
    WRG = mid([128, KD, E], F32)
    MV = mid([T, NT, 2], F32)
    assert o <= 207008, o
    BS1 = at(o_h + 20480 + 14336, [T, NT, 2, 6], F32)
    MV1 = at(o_h + 20480 + 15360, [T, NT, 2], F32)

    def dram(name, shape, dt):
        return nc.dram_tensor(name, list(shape), dt, kind="Internal").ap()

    XTD = dram("xt_d", [NT, 128, 2 * KD * T], F16)
    MSKD = dram("mask_d", [NT, T, N], BF16)
    ALD = dram("al_d", [H + 1, NT, T], F32)
    AAD = dram("aa_d", [H + 1, 2 * NT, T], F32)
    H1D = dram("h1_d", [NT, 128, 2, NCH, T], F16)
    XND = dram("xn_d", [N, D], F32)
    YD = dram("y_d", [E * SLOTS, D], F32)

    ctx = ExitStack()
    with ctx:
        PS = ctx.enter_context(nc.psum_tensor("PS", [128, 8, 512], F32))
        PSF = PS[:, :, :].rearrange("p b n -> p (b n)")

        def ps16(dt):
            return PSF.bitcast(dt)

        PH, PB = ps16(F16), ps16(BF16)

        def col16(b, i):
            return 1024 * (b + i // 5) + (T + 1) * (i % 5)

        def blocks16(v, rows, b):
            return v[0:rows, 1024 * b:1024 * b + 2048].rearrange("p (a r) -> p a r", a=2)[
                :, :, 0:5 * (T + 1)].rearrange("p a (i n) -> p a i n", n=T + 1)[:, :, :, 0:T]

        def sem(name):
            return ctx.enter_context(nc.semaphore(name))

        s_const = sem("consts_made")
        s_edges = sem("edges_loaded")
        s_x = [sem(f"x_loaded{b}") for b in range(3)]
        s_bias = sem("biases_loaded")
        s_once = sem("keys_then_total_on_tensor_engine")
        s_a2v = sem("a2_loaded")
        s_dve = sem("dve_step")
        s_act = sem("act_step")
        s_keys = sem("keys_made")
        s_var = sem("variance_made")
        s_sd = sem("deviation_made")
        s_xn = sem("x_normalised")
        s_xT = sem("x_transposed")
        s_xth = sem("xT_hi_made")
        s_xtl = sem("xT_lo_made")
        s_xts = [sem(f"xT_slot{b}") for b in range(3)]
        s_wst = [sem(f"weights_in_slot{b}") for b in range(2)]
        s_wh = sem("weight_hi_made")
        s_wl = sem("weight_slot_used")
        s_arep = sem("attention_vectors_loaded")
        s_proj = sem("projection_done")
        s_hh = sem("h_hi_made")
        s_hl = sem("h_used")
        s_ol = sem("source_onehots_made")
        s_or = sem("pair_onehot_made")
        s_cm = sem("pair_onehot_used")
        s_k2 = sem("keys_advanced")
        s_ce = sem("chunk_kept")
        s_cs = sem("count_sum_steps")
        s_pf = sem("p_tile_free")
        s_go = sem("general_onehot_made")
        s_gu = sem("general_onehot_used")
        s_gd = sem("general_chunk_done")
        s_gk = sem("general_chunk_kept")
        s_ctok = sem("counts_final")
        s_mt = sem("mask_transposed")
        s_mm = sem("mask_made")
        s_ms = [sem(f"mask_stored{b}") for b in range(2)]
        s_ml = sem("masks_loaded")
        s_vp = sem("v2_product_made")
        s_va = sem("v2_sum_made")
        s_mu = sem("mask_used")
        s_alt = sem("al_transposed")
        s_alc = sem("al_row_made")
        s_ald = sem("al_row_stored")
        s_row = sem("al_row_broadcast")
        s_aa = sem("shifts_made")
        s_aat = sem("shifts_transposed")
        s_aac = sem("shift_rows_made")
        s_aad = sem("shift_rows_stored")
        s_rows = sem("shift_rows_broadcast")
        s_al = sem("al_complete")
        s_p1 = sem("p_second_branch")
        s_p2 = sem("p_leaky")
        s_p3 = sem("p_exp")
        s_p4 = sem("p_counted")
        s_p5 = sem("p_hi")
        s_p6 = sem("p_lo")
        s_att = sem("attention_group_done")
        s_rd = sem("denominator_made")
        s_y1 = sem("y_divided")
        s_yr = sem("y_relu")
        s_y2 = sem("y_exp")
        s_y3 = sem("y_elu1")
        s_y4 = sem("y_scaled")
        s_y5 = sem("h1_hi")
        s_y6 = sem("h1_lo")
        s_h1s = [sem(f"h1_stored{b}") for b in range(2)]
        s_a2 = sem("al2_part_done")
        s_a2r = sem("al2_part_added")
        s_w2g = [sem(f"w2_in_slot{b}") for b in range(3)]
        s_w2h = sem("w2_hi")
        s_w2l = sem("w2_lo")
        s_h0 = sem("h1_last_head_loaded")
        s_ht = [sem(f"h1_loaded{b}") for b in range(2)]
        s_pj2 = sem("projection2_done")
        s_h2h = sem("h2_hi")
        s_h2l = sem("h2_lo")
        s_xb = sem("x_plus_bias")
        s_at2 = sem("attention2_done")
        s_x2 = sem("x2_made")
        s_xn2 = sem("x2_normalised")
        s_xns = [sem(f"xn2_stored{b}") for b in range(2)]
        s_x2t = sem("x2_transposed")
        s_x2h = sem("x2T_hi")
        s_x2lo = sem("x2T_lo")
        s_wrl = sem("router_loaded")
        s_lg = sem("logits_done")
        s_lgm = sem("logits_shifted")
        s_pe = sem("probs_exp")
        s_wg = [sem(f"ffn_weights_loaded{q}") for q in range(3)]
        s_wgh = sem("ffn_weights_hi")
        s_wgl = sem("ffn_weights_lo")
        s_gdn = sem("gate_done")
        s_udn = sem("up_done")
        s_sg = sem("silu_made")
        s_gx = sem("gate_times_up")
        s_ah = sem("act_hi")
        s_alo = sem("act_lo")
        s_s3 = sem("scores_split")
        s_s3t = sem("scores_transposed")
        s_s3c = sem("scores_rows_made")
        s_sd3 = sem("shared_down_done")
        s_sdc = sem("shared_copied")
        s_sdr = sem("shared_added")
        s_rr = sem("rank_rows_done")
        s_rk = sem("rank_rows_used")
        s_ind = sem("slots_onehot_made")
        s_tk = sem("token_table_done")
        s_tok = sem("token_table_made")
        s_xg = [sem(f"rows_gathered{b}") for b in range(XGN)]
        s_xgt = sem("rows_transposed")
        s_xgh = sem("rows_hi")
        s_xgl = sem("rows_lo")
        s_ed = sem("expert_down_done")
        s_yo = sem("expert_rows_made")
        s_ys = [sem(f"expert_rows_stored{b}") for b in range(2)]
        s_gz = sem("return_slot_cleared")
        s_gzl = sem("return_places_cleared")
        s_gg = [sem(f"expert_rows_gathered{b}") for b in range(GRN)]
        s_ggl = [sem(f"last_rows_gathered{j}") for j in range(NT - XGN)]
        s_gl = sem("last_rows_added")
        s_g1 = sem("expert_rows_added")
        s_fin = sem("out_stored")

        block = ctx.enter_context(nc.Block())

        last_in = [(s_xg[j], 16 * (E * 4 // XGN + 1)) for j in range(XGN)]
        last_in += [(s_ggl[j], 16) for j in range(NT - XGN)]

        def w1_use(h, k):
            return KD * (h - 1) + k

        def w1_in(h, k):
            if h == 0:
                return W1F[:, k, :], s_wst[0], 16
            u = w1_use(h, k)
            return WST[:, u % 2, 0:C], s_wst[u % 2], 16 * (u // 2 + 1 + (1 - u % 2))

        def tmp(h, i):
            q = NT * h + i
            if h < H:
                return TMP[q % 4], q - 3
            return TMP[i % 3], max(q - 2, NT * H)

        x2_in = [(s_xts[b], 16 * (len(range(b, NT + NT * H, 3)) + 1)) for b in range(3)]
        x2_in += [(s_wst[b], 16 * (KD * (H - 1) // 2 + 2 - b)) for b in range(2)]
        x2_in += [(s_w2g[b], 16 * (len(range(b, 2 * NCH, 3)) + 1)) for b in range(3)]
        x2_in += [(s_h1s[b], 16 * (NCH + 1)) for b in range(2)]
        NPRE = 4

        HALF = 2304

        def ffn_weights(n):
            if n == 0:
                return s1, s3, s2
            return w1[n - 1], w3[n - 1], w2[n - 1]

        @block.sync
        def _(sp):
            sp.dma_start(ED[:, 0], src.rearrange("(a q p) -> q a p", a=2, p=T)).then_inc(s_edges, 16)
            sp.dma_start(ED[:, 1], dst.rearrange("(a q p) -> q a p", a=2, p=T)).then_inc(s_edges, 16)
            for n, (a, b) in enumerate(PIECES):
                sp.dma_start(XA[:, a:b, :], x[T * a:T * b, :].rearrange("(i p) d -> p i d", p=T)
                             ).then_inc(s_x[n], 16)
            sp.dma_start(W1F[:, :, :], W1[:, 0:C].rearrange("(k p) c -> p k c", p=128)).then_inc(s_wst[0], 16)
            with nc.allow_non_contiguous_dma(reason="one small column load"):
                sp.dma_start(b1c[:, :], b1.rearrange("(c p) -> p c", p=128)).then_inc(s_bias, 16)

            def load_w(u, view):
                sp.wait_ge(s_wl, KD + max(u - 1, 0))
                sp.dma_start(WST[:, u % 2, 0:view.shape[1]], view).then_inc(s_wst[u % 2], 16)

            def load_w1(h):
                load_al(h)
                load_w1_rows(h, range(KD))

            def load_al(h):
                if h:
                    sp.wait_ge(s_hl, NT * h)
                sp.dma_start(AR1[:, 0, :], as1[h:h + 1, :].to_broadcast([T, C])).then_inc(s_arep, 16)
                sp.dma_start(AR1[:, 1, :], ad1[h:h + 1, :].to_broadcast([T, C])).then_inc(s_arep, 16)

            def load_w1_rows(h, ks):
                for k in ks:
                    load_w(w1_use(h, k), W1[128 * k:128 * k + 128, C * h:C * h + C])

            def store_xt(i):
                sp.wait_ge(s_xtl, i + 1)
                sp.dma_start(XTD[i], XTR[:, i % 3].rearrange("p a k n -> p (a k n)")).then_inc(s_xts[i % 3], 16)

            def slot_uses(v):
                return 16 * (v // 3 + 1)

            def load_xt(h, i):
                v = NT + NT * h + i
                if v - 3 < NT:
                    sp.wait_ge(s_xts[v % 3], slot_uses(v - 3))
                else:
                    sp.wait_ge(s_proj, v - 3 - NT + 1)
                if h == 0:
                    sp.wait_ge(s_xts[i % 3], slot_uses(i))
                sp.dma_start(XTR[:, v % 3].rearrange("p a k n -> p (a k n)"), XTD[i]).then_inc(s_xts[v % 3], 16)

            def load_v2(ch):
                if ch >= 3:
                    sp.wait_ge(s_vp, 2 * (ch - 2))
                sp.dma_start(WV[ch % 3][:, :], W2[128 * ch:128 * ch + 128, :]).then_inc(s_w2g[ch % 3], 16)

            load_al(0)
            sp.dma_start(A2R[:, 0, :], as2.to_broadcast([128, D])).then_inc(s_a2v, 16)
            sp.dma_start(A2R[:, 1, :], ad2.to_broadcast([128, D])).then_inc(s_a2v, 16)
            for i in range(NT):
                store_xt(i)
            for ch in range(3):
                load_v2(ch)
            for i in range(NT):
                load_xt(0, i)
                load_v2(3 + i)
            for ch in range(3 + NT, NCH):
                load_v2(ch)

            def chain_row(h):
                sp.wait_ge(s_alc, h + 1)
                sp.dma_start(ALD[h], TR[0:NT, :]).then_inc(s_ald, 16)
                sp.wait_ge(s_ald, 16 * (h + 1))
                if h:
                    sp.wait_ge(s_p1, NT * h)
                    sp.wait_ge(s_p2, NT * h)
                sp.dma_start(ROW[:, 0, :], ALD[h:h + 1].rearrange("o a n -> o (a n)").to_broadcast([T, N])
                             ).then_inc(s_row, 16)

            def load_masks(h, t):
                sp.dma_start(MSKT[t if h < H else t % 4][:, :, :], MSKD[2 * t:2 * t + 2].rearrange("j p n -> p j n")
                             ).then_inc(s_ml, 16)

            def chain_shift(h):
                sp.wait_ge(s_aac, h + 1)
                sp.dma_start(AAD[h], TR[:, :]).then_inc(s_aad, 16)
                sp.wait_ge(s_aad, 16 * (h + 1))
                sp.dma_start(ROW[:, :, :].rearrange("p a n -> p (a n)"),
                             AAD[h:h + 1].rearrange("o a n -> o (a n)").to_broadcast([T, 2 * N])
                             ).then_inc(s_rows, 16)

            def store_h1(h, c):
                g = CH * h + c
                sp.wait_ge(s_y6, 3 * (g + 1))
                for part in range(2):
                    sp.dma_start(H1D[:, :, part, g, :].rearrange("j p n -> p j n"),
                                 H1O[:, g % 2, part, :].rearrange("p (j n) -> p j n", n=T)
                                 ).then_inc(s_h1s[g % 2], 16)

            load_w1(1)
            sp.wait_ge(s_vp, 2 * NCH)
            chain_row(0)
            for i in range(3):
                load_xt(1, i)
            for j in range(NT):
                sp.wait_ge(s_mm, j + 1)
                sp.dma_start(MSKD[j], MSK[:, j % 2, :]).then_inc(s_ms[j % 2], 16)
            for i in range(3, 6):
                load_xt(1, i)
            chain_shift(0)
            for i in range(6, NT):
                load_xt(1, i)

            def load_w2(ch):
                if ch >= 3:
                    sp.wait_ge(s_w2l, ch - 2)
                u = NCH + ch
                sp.dma_start(W2G[u % 3][:, :], W2[128 * ch:128 * ch + 128, :]).then_inc(s_w2g[u % 3], 16)

            for h in range(H):
                sp.wait_ge(s_p6, NT * (h + 1))
                if h + 1 < H:
                    if h == 0:
                        for b in range(2):
                            sp.wait_ge(s_ms[b], 16 * (NT // 2))
                    for t in range(NT // 2):
                        load_masks(h + 1, t)
                    chain_row(h + 1)
                else:
                    for ch in range(3):
                        load_w2(ch)
                if h + 2 < H:
                    load_al(h + 2)
                    load_w1_rows(h + 2, range(2))
                if h + 1 == H:
                    sp.wait_ge(s_h1s[0], 32 * CH * (H - 1) // 2)
                    sp.wait_ge(s_h1s[1], 32 * CH * (H - 1) // 2)
                    sp.dma_start(HT0[:, :, 0:NCH - CH, :], H1D[0, :, :, 0:NCH - CH, :]).then_inc(s_a2v, 16)
                store_h1(h, 0)
                if h + 2 < H:
                    load_w1_rows(h + 2, range(2, 4))
                if h + 1 < H:
                    chain_shift(h + 1)
                else:
                    for ch in range(3, 7):
                        load_w2(ch)
                store_h1(h, 1)
                if h + 2 < H:
                    load_w1_rows(h + 2, range(4, KD))
                    for i in range(3):
                        load_xt(h + 2, i)
                if h + 1 == H:
                    for ch in range(7, 11):
                        load_w2(ch)
                store_h1(h, 2)
                if h + 1 == H:
                    for ch in range(11, NCH):
                        load_w2(ch)
                store_h1(h, 3)
                if h + 2 < H:
                    for i in range(3, NT):
                        load_xt(h + 2, i)

            def load_ht(j):
                if j == 0:
                    for b in range(2):
                        sp.wait_ge(s_h1s[b], 16 * NCH)
                    sp.dma_start(HT0[:, :, NCH - CH:NCH, :], H1D[0, :, :, NCH - CH:NCH, :]).then_inc(s_h0, 16)
                    return
                if j == 1:
                    sp.wait_ge(s_a2, NCH)
                if j >= 3:
                    sp.wait_ge(s_pj2, j - 1)
                sp.dma_start(HT[j % 2][:, :, :, :].rearrange("p a c n -> p (a c n)"),
                             H1D[j].rearrange("p a c n -> p (a c n)")).then_inc(s_ht[j % 2], 16)

            load_ht(0)
            load_ht(1)
            load_ht(2)
            sp.wait_ge(s_w2l, NCH)
            for t in range(4):
                load_masks(H, t)
            sp.wait_ge(s_pj2, 1)
            chain_row(H)
            load_ht(3)
            sp.wait_ge(s_mu, NT * H + 2)
            load_masks(H, 4)
            chain_shift(H)
            for j in range(4, NT):
                load_ht(j)
            sp.wait_ge(s_pj2, NT)
            sp.dma_start(B2R[:, :], b2.rearrange("(o d) -> o d", o=1).to_broadcast([T, D])).then_inc(s_bias, 16)
            for j in range(NT):
                sp.dma_start(X2[:, j, :], x[T * j:T * j + T, :]).then_inc(x2_in[j][0], 16)
            sp.dma_start(WRG[:, :, :], Wr.rearrange("(k p) e -> p k e", p=128)).then_inc(s_wrl, 16)
            sp.wait_ge(s_p4, NT * (H + 1))

            def weight_part(n, q):
                w = ffn_weights(n)[q]
                place = WG0 if n == 0 and q < 2 else WG
                sp.dma_start(place[:, HALF * q:HALF * q + HALF].rearrange("p (k i) -> p k i", i=w.shape[1]),
                             w.rearrange("(k p) i -> p k i", p=128)).then_inc(s_wg[q], 16)

            weight_part(0, 0)
            weight_part(0, 1)

            def store_xn(i):
                sp.wait_ge(s_xn2, i + 1)
                sp.dma_start(XND[T * i:T * i + T, :], XN2[:, i % 2, :]).then_inc(s_xns[i % 2], 16)

            for i in range(NT - 1):
                store_xn(i)
            sp.wait_ge(s_at2, NT)
            weight_part(0, 2)
            store_xn(NT - 1)

            def load_ffn(n):
                for q in range(3):
                    sp.wait_ge(s_wgh, 3 * (n - 1) + q + 1)
                    sp.wait_ge(s_wgl, 3 * (n - 1) + q + 1)
                    weight_part(n, q)

            load_ffn(1)
            for e in range(E):
                if e + 2 <= E:
                    load_ffn(e + 2)
                for c in range(4):
                    g = 4 * e + c
                    sp.wait_ge(s_yo, g + 1)
                    sp.dma_start(YD[SLOTS * e + SC * c:SLOTS * e + SC * c + SC, :], YO[0:SC, g % 2, :]
                                 ).then_inc(s_ys[g % 2], 16)
            for j in range(NT):
                sp.wait_ge(s_gl, j + 1)
                sp.dma_start(out[T * j:T * j + T, :], X2[:, j, :]).then_inc(s_fin, 16)
            sp.wait_ge(s_fin, 16 * NT)

        @block.gpsimd
        def _(pool):
            made = [0]

            def link(ins):
                made[0] += 1
                ins.then_inc(s_const, 1)
                pool.wait_ge(s_const, made[0])

            for t in (idf, idh, idb):
                link(nc.gpsimd.memset(t[:, :], 0.0))
                link(nc.gpsimd.affine_select(out=t[:, :], in_=t[:, :], compare_op=ALU.not_equal, fill=1.0,
                                             base=0, pattern=[[-1, 128]], channel_multiplier=1))
            link(nc.gpsimd.iota(iok[:, :], [[1, KC]], base=0, channel_multiplier=0,
                                allow_small_or_imprecise_dtypes=True))
            link(nc.gpsimd.iota(iot[:, :], [[1, T]], base=0, channel_multiplier=0,
                                allow_small_or_imprecise_dtypes=True))
            link(nc.gpsimd.memset(ones[:, :], 1.0))
            link(nc.gpsimd.memset(onesf[:, :], 1.0))
            link(nc.gpsimd.memset(KEY[:, 0:KT], -1.0))
            link(nc.gpsimd.memset(SLO[:, 0:KT], -1.0))
            link(nc.gpsimd.iota(SLO[:, KT:KA], [[0, NT]], base=0, channel_multiplier=1,
                                allow_small_or_imprecise_dtypes=True))
            link(nc.gpsimd.iota(MX[:, :], [[T, NT]], base=0, channel_multiplier=1,
                                allow_small_or_imprecise_dtypes=True))
            link(nc.gpsimd.iota(ZZ[:, :], [[T + DC, NT]], base=0, channel_multiplier=1,
                                allow_small_or_imprecise_dtypes=True))

            def p_lo(h, i):
                q = NT * h + i
                pool.wait_ge(s_p5, q + 1)
                nc.gpsimd.tensor_tensor(P[:, i, 1, :], tmp(h, i)[0][:, :], P[:, i, 0, :], ALU.subtract
                                        ).then_inc(s_p6, 1)

            def h1_lo(h, c, b):
                g = CH * h + c
                y = 3 * g + b
                lo, n = BLK[b]
                pool.wait_ge(s_y3, y + 1)
                nc.gpsimd.tensor_scalar(YB[:, y % 3, 0:n], YB[:, y % 3, 0:n], SX, -SX, ALU.mult, ALU.add
                                        ).then_inc(s_y4, 1)
                pool.wait_ge(s_y5, y + 1)
                nc.gpsimd.tensor_tensor(H1O[:, g % 2, 1, lo:lo + n], YB[:, y % 3, 0:n],
                                        H1O[:, g % 2, 0, lo:lo + n], ALU.subtract).then_inc(s_y6, 1)

            pool.wait_ge(s_a2v, 32)
            for ch in range(NCH):
                pool.wait_ge(s_w2g[ch % 3], 16 * (ch // 3 + 1))
                for a in range(2):
                    k = 2 * ch + a
                    if k >= 2:
                        pool.wait_ge(s_va, k - 1)
                    nc.gpsimd.tensor_tensor(VP[a][:, :], WV[ch % 3][:, :], A2R[:, a, :], ALU.mult).then_inc(s_vp, 1)

            for k in range(KD):
                w = w1_in(1, k)[0]
                pool.wait_ge(s_wh, KD + k + 1)
                link(nc.gpsimd.tensor_scalar(w, w, SW, None, ALU.mult))
                nc.gpsimd.tensor_tensor(W1S[:, k, 1, :], w, W1S[:, k, 0, :], ALU.subtract).then_inc(s_wl, 1)

            for i in range(NT):
                p_lo(0, i)
            for h in range(H):
                for c in range(CH):
                    if c == CH - 1 and h + 1 < H:
                        for i in range(NPRE - 2):
                            p_lo(h + 1, i)
                    for b in range(3):
                        h1_lo(h, c, b)
                if h + 1 < H:
                    for i in range(NPRE - 2, NT):
                        p_lo(h + 1, i)
            for i in range(NT):
                p_lo(H, i)
            pool.wait_ge(s_bias, 32)
            for j in range(NT):
                pool.wait_ge(*x2_in[j])
                nc.gpsimd.tensor_tensor(X2[:, j, :], X2[:, j, :], B2R[:, :], ALU.add).then_inc(s_xb, 1)

            pool.wait_ge(s_at2, NT)
            link(nc.gpsimd.memset(TRI[:, :], 1.0))
            link(nc.gpsimd.affine_select(out=TRI[:, :], in_=TRI[:, :], compare_op=ALU.is_gt, fill=0.0,
                                         base=0, pattern=[[-1, T]], channel_multiplier=1))
            link(nc.gpsimd.iota(io392[:, :], [[1, SLOTS]], base=0, channel_multiplier=0,
                                allow_small_or_imprecise_dtypes=True))
            link(nc.gpsimd.memset(IDX[:, :, :], 0.0))
            link(nc.gpsimd.memset(TOK[:, :, :], 0.0))
            link(nc.gpsimd.iota(tokid[:, :], [[T, NT]], base=0, channel_multiplier=1,
                                allow_small_or_imprecise_dtypes=True))
            link(nc.gpsimd.iota(io8[:, :], [[1, E]], base=0, channel_multiplier=0,
                                allow_small_or_imprecise_dtypes=True))

            def act_lo(n, dst, src_, hi):
                pool.wait_ge(s_ah, n + 1)
                nc.gpsimd.tensor_tensor(dst, src_, hi, ALU.subtract).then_inc(s_alo, 1)

            for m in range(KI):
                for b, (lo, w) in enumerate(BLK):
                    n = 3 * m + b
                    act_lo(n, AB[:, 1, m, lo:lo + w], SG[:, n % 2, 0:w], AB[:, 0, m, lo:lo + w])

            for j in range(NT):
                pool.wait_ge(s_sdc, j + 1)
                nc.gpsimd.tensor_tensor(X2[:, j, :], X2[:, j, :], YO[:, j % 2, :], ALU.add).then_inc(s_sdr, 1)

            def gather(g):
                e, c = divmod(g, 4)
                if g >= XGN:
                    pool.wait_ge(s_xgt, g - XGN + 1)
                nc.gpsimd.indirect_dma_start(
                    out=XG[:, g % XGN, :], out_offset=None, in_=XND[:, :],
                    in_offset=bass.IndirectOffsetOnAxis(ap=TOK[:, c, e:e + 1], axis=0),
                ).then_inc(s_xg[g % XGN], 16)

            def expert_lo(e, m):
                n = 9 + KI * e + m
                act_lo(n, AE[e % 2][:, 1, m, :], SG[:, n % 2, 0:SLOTS], AE[e % 2][:, 0, m, :])

            def gather_back(n):
                j, k = divmod(n, 2)
                if n >= GRN:
                    pool.wait_ge(s_gz, n - GRN + 1)
                nc.gpsimd.indirect_dma_start(
                    out=GR[:, n % GRN, :], out_offset=None, in_=YD[0:SLOTS * (E - 1), :],
                    in_offset=bass.IndirectOffsetOnAxis(ap=IDX[:, k, j:j + 1], axis=0),
                    bounds_check=(E - 1) * SLOTS - 1, oob_is_err=False,
                ).then_inc(s_gg[n % GRN], 16)

            pool.wait_ge(s_tok, 1)
            for b in range(2):
                pool.wait_ge(s_xns[b], 16 * NT // 2)
            for g in range(XGN):
                gather(g)
            for e in range(E - 1):
                for m in range(KI):
                    expert_lo(e, m)
                if e + 2 < E:
                    for c in range(4):
                        gather(4 * (e + 2) + c)
            pool.wait_ge(s_xgt, 4 * E)
            nc.gpsimd.memset(GRL[:, :, :], 0.0).then_inc(s_gzl, 1)
            for q in range(GRN // 3):
                pool.wait_ge(s_wgl, 3 * E + q + 1)
                nc.gpsimd.memset(GR[:, 3 * q:3 * q + 3, :], 0.0).then_inc(s_gzl, 1)
            pool.wait_ge(s_gzl, 1 + GRN // 3)
            for b in range(2):
                pool.wait_ge(s_ys[b], 16 * 2 * (E - 1))
            for n in range(2 * NT):
                if n in (3, 6, 9):
                    expert_lo(E - 1, n // 3 - 1)
                gather_back(n)
            for b in range(2):
                pool.wait_ge(s_ys[b], 16 * 2 * E)
            for j in range(NT):
                nc.gpsimd.indirect_dma_start(
                    out=GRL[:, j, :], out_offset=None, in_=YD[:, :],
                    in_offset=bass.IndirectOffsetOnAxis(ap=IDX[:, 2, j:j + 1], axis=0),
                    bounds_check=E * SLOTS - 1, oob_is_err=False,
                ).then_inc(last_in[j][0], 16)

        @block.scalar
        def _(act):
            A = nc.scalar.activation
            for n, (a, b) in enumerate(PIECES):
                act.wait_ge(s_var, n + 1)
                A(SD[:, a:b], MV1[:, a:b, 1], ACT.Sqrt).then_inc(s_sd, 1)
            def w1_hi(h, ks):
                for k in ks:
                    if h and k == 0:
                        act.wait_ge(s_proj, NT * h)
                    w, arrived, value = w1_in(h, k)
                    act.wait_ge(arrived, value)
                    A(W1S[:, k, 0, :], w, ACT.Copy, scale=SW).then_inc(s_wh, 1)

            def h_hi(h, i):
                act.wait_ge(s_proj, NT * h + i + 1)
                if h >= 2 and i == 0:
                    act.wait_ge(s_att, 5 * (h - 1))
                A(HB[h % 2][:, i, 0, :], PS[0:T, 6 + i % 2, :], ACT.Copy, scale=1.0 / SW).then_inc(s_hh, 1)

            def v2_sum(k):
                act.wait_ge(s_vp, k + 1)
                A(VP[k % 2][:, :], VP[k % 2][:, :], ACT.Copy, scale=SW, accum_out=V2F[:, k // 2, k % 2:k % 2 + 1]
                  ).then_inc(s_va, 1)

            for i in range(NT):
                act.wait_ge(s_xT, i + 1)
                if i >= 3:
                    act.wait_ge(s_xts[i % 3], 16 * (i // 3))
                b = 6 - 2 * (i % 2)
                A(XTR[:, i % 3, 0].rearrange("p (a k) n -> p a (k n)", a=2), PS[:, b:b + 2, 0:375],
                  ACT.Copy).then_inc(s_xth, 1)
                if 4 <= i < 4 + KD:
                    w1_hi(0, (i - 4,))
            k = 0
            for i in range(NT):
                h_hi(0, i)
                while k * NT < 2 * NCH * (i + 1):
                    v2_sum(k)
                    k += 1
            act.sem_inc(s_ce, 1)
            w1_hi(1, range(KD))
            with act.Fori(0, NC // GC) as g:
                for c in range(GC):
                    act.wait_ge(s_cm, 1 + g * NJ + sum(len(j) for j in jobs[:c + 1]))
                    A(CT[:, :, bass.ds((GC * g + c) * DC, DC)],
                      PS[0:T, c, 0:KC].rearrange("p (i n) -> p i n", n=DC), ACT.Copy,
                      accum_out=CS[:, bass.ds(GC * g + c, 1)]).then_inc(s_ce, 1)

            def p_branch(h, i):
                q = NT * h + i
                if i == 0:
                    act.wait_ge(s_rows, 16 * (h + 1))
                    act.wait_ge(s_al, h + 1)
                if q >= 4:
                    act.wait_ge(s_p6, tmp(h, i)[1])
                A(tmp(h, i)[0][:, :], ROW[:, 1, :], ACT.Identity, bias=ALF[:, h, i:i + 1]).then_inc(s_p1, 1)

            def p_exp(h, i):
                q = NT * h + i
                act.wait_ge(s_p2, q + 1)
                A(tmp(h, i)[0][:, :], tmp(h, i)[0][:, :], ACT.Exp).then_inc(s_p3, 1)

            def p_hi(h, i):
                q = NT * h + i
                act.wait_ge(s_p4, q + 1)
                if h and i < NT - 1:
                    act.wait_ge(s_pf, (NT - 1) * (h - 1) + i + 1)
                elif h:
                    act.wait_ge(s_att, 5 * h)
                if q == 0:
                    act.wait_ge(s_ctok, 1)
                A(P[:, i, 0, :], tmp(h, i)[0][:, :], ACT.Copy).then_inc(s_p5, 1)

            def p_step(h, i):
                if i < NT:
                    p_branch(h, i)
                if 1 <= i <= NT:
                    p_exp(h, i - 1)
                if 2 <= i:
                    p_hi(h, i - 2)

            def y_step(h, c, b):
                g = CH * h + c
                y = 3 * g + b
                lo, n = BLK[b]
                act.wait_ge(s_y1, y + 1)
                if y >= 2:
                    act.wait_ge(s_y3, y - 1)
                if y == 0:
                    act.wait_ge(s_bias, 16)
                A(RB[:, y % 2, 0:n], YB[:, y % 3, 0:n], ACT.Relu, bias=b1c[:, g:g + 1], scale=1.0 / SX
                  ).then_inc(s_yr, 1)
                A(YB[:, y % 3, 0:n], YB[:, y % 3, 0:n], ACT.Exp, bias=b1c[:, g:g + 1], scale=1.0 / SX
                  ).then_inc(s_y2, 1)

            def y_hi(h, c, b):
                g = CH * h + c
                y = 3 * g + b
                lo, n = BLK[b]
                act.wait_ge(s_y4, y + 1)
                if b == 0 and g >= 2:
                    act.wait_ge(s_h1s[g % 2], 32 * (g // 2))
                    act.wait_ge(s_a2, g - 1)
                A(H1O[:, g % 2, 0, lo:lo + n], YB[:, y % 3, 0:n], ACT.Copy).then_inc(s_y5, 1)

            def w2_hi(ch):
                if ch == 0:
                    act.wait_ge(s_p6, NT * H)
                u = NCH + ch
                act.wait_ge(s_w2g[u % 3], 16 * (u // 3 + 1))
                A(W2S[ch][:, 0, :], W2G[u % 3][:, :], ACT.Copy, scale=SW).then_inc(s_w2h, 1)

            for j in range(NT):
                act.wait_ge(s_mt, j + 1)
                if j >= 2:
                    act.wait_ge(s_ms[j % 2], 16 * (j // 2))
                    act.wait_ge(s_mu, j - 1)
                A(MSK[:, j % 2, :].rearrange("p (a i n) -> p a i n", a=2, n=T), blocks16(PH, T, 2 * (j % 3)),
                  ACT.Relu, bias=1.0, scale=-1.0).then_inc(s_act, 1)
                act.wait_ge(s_act, j + 1)
                A(MSK[:, j % 2, :], MSK[:, j % 2, :], ACT.Copy, scale=NEG).then_inc(s_mm, 1)
                if j % 3 == 2:
                    h_hi(1, j // 3)
            for i in range(NT + 2):
                if NT // 3 + i < NT:
                    h_hi(1, NT // 3 + i)
                p_step(0, i)
            for h in range(H):
                for c in range(CH):
                    for b in range(4):
                        if b < 3:
                            y_step(h, c, b)
                        if b:
                            y_hi(h, c, b - 1)
                    if c < 3 and h + 2 < H:
                        w1_hi(h + 2, range(2 * c, 2 * c + 2))
                    if h + 1 == H:
                        for ch in range(4 * c, 4 * c + 4):
                            w2_hi(ch)
                    if c == 2 and h + 1 < H:
                        for i in range(NPRE):
                            p_step(h + 1, i)
                if h + 1 < H:
                    for i in range(NPRE, NT + NPRE):
                        if h + 2 < H:
                            h_hi(h + 2, i - NPRE)
                        if i < NT + 2:
                            p_step(h + 1, i)
            def h2_hi(j):
                act.wait_ge(s_pj2, j + 1)
                b = 2 * (j % 3)
                A(H2[j][:, 0, 0:D].rearrange("p (a n) -> p a n", a=2), PS[0:T, b:b + 2, 0:DH], ACT.Copy,
                  scale=1.0 / SW).then_inc(s_h2h, 1)

            act.wait_ge(s_w2l, NCH)
            for i in range(NT + 2):
                p_step(H, i)
                if i < NT:
                    h2_hi(i)

            def x2t_hi(i):
                act.wait_ge(s_x2t, i + 1)
                b = 2 * (i % 2)
                A(X2T[:, 0, :, T * i:T * i + T].rearrange("p (a k) n -> p a k n", a=2),
                  PS[:, b:b + 2, 0:375].rearrange("p a (k n) -> p a k n", n=T), ACT.Copy).then_inc(s_x2h, 1)

            act.wait_ge(s_wrl, 16)
            A(WRS[:, :, 0, :], WRG[:, :, :], ACT.Copy, scale=SW).then_inc(s_wh, 1)
            for j in range(NT):
                act.wait_ge(s_var, len(PIECES) + 1 + j)
                A(SD[:, j:j + 1], MV[:, j, 1:2], ACT.Sqrt).then_inc(s_sd, 1)
                if j:
                    x2t_hi(j - 1)

            def ffn_hi(n, q):
                act.wait_ge(s_wg[q], 16 * (n + 1))
                if n == 0:
                    act.wait_ge(s_at2, NT)
                if n >= 2 and q == 0:
                    if n == 2:
                        act.wait_ge(s_sd3, NT)
                    else:
                        act.wait_ge(s_ed, 4 * (n - 2))
                A(WS[n % 2][:, 0, HALF * q:HALF * q + HALF], (WG0 if n == 0 and q < 2 else WG)[:, HALF * q:HALF * q + HALF], ACT.Copy,
                  scale=SW).then_inc(s_wgh, 1)

            ffn_hi(0, 0)
            x2t_hi(NT - 1)
            ffn_hi(0, 1)
            ffn_hi(0, 2)
            act.wait_ge(s_lgm, 1)
            A(LG[:, :, :], LG[:, :, :], ACT.Exp).then_inc(s_pe, 1)

            def silu(n, w):
                act.wait_ge(s_gdn, n + 1)
                if n >= 2:
                    act.wait_ge(s_alo, n - 1)
                A(SG[:, n % 2, 0:w], PS[:, 6, 0:w], ACT.Silu, scale=1.0 / (SX * SW)).then_inc(s_sg, 1)

            def act_hi(n, dst_, w):
                act.wait_ge(s_gx, n + 1)
                A(dst_, SG[:, n % 2, 0:w], ACT.Copy).then_inc(s_ah, 1)

            for n in range(9):
                lo, w = BLK[n % 3]
                silu(n, w)
                act_hi(n, AB[:, 0, n // 3, lo:lo + w], w)
                if 1 <= n <= 3:
                    ffn_hi(1, n - 1)
            for j in range(NT):
                act.wait_ge(s_sd3, j + 1)
                if j >= 2:
                    act.wait_ge(s_sdr, j - 1)
                A(YO[:, j % 2, :].rearrange("p (a n) -> p a n", a=2), PS[0:T, 6:8, 0:DH], ACT.Copy,
                  scale=1.0 / (SA * SW)).then_inc(s_sdc, 1)

            def xg_hi(g):
                e, c = divmod(g, 4)
                act.wait_ge(s_xgt, g + 1)
                if c == 0 and e >= 2:
                    act.wait_ge(s_udn, 9 + KI * (e - 1))
                b = 2 + 2 * (g % 2)
                A(XGT[e % 2][:, 0, :, SC * c:SC * c + SC].rearrange("p (a k) n -> p a k n", a=2),
                  PS[:, b:b + 2, 0:3 * SC].rearrange("p a (k n) -> p a k n", n=SC), ACT.Copy).then_inc(s_xgh, 1)

            def y_out(g):
                c = g % 4
                act.wait_ge(s_ed, g + 1)
                if g >= 2:
                    act.wait_ge(s_ys[g % 2], 16 * (g // 2))
                else:
                    act.wait_ge(s_sdr, NT)
                b = 6 if c % 2 == 0 else 0
                A(YO[0:SC, g % 2, :].rearrange("p (a n) -> p a n", a=2), PS[0:SC, b:b + 2, 0:DH], ACT.Copy,
                  scale=1.0 / (SA * SW)).then_inc(s_yo, 1)

            for c in range(4):
                xg_hi(c)
            for e in range(E):
                for m in range(KI):
                    n = 9 + KI * e + m
                    silu(n, SLOTS)
                    if m == 0 and e >= 2:
                        act.wait_ge(s_ed, 4 * (e - 1))
                    act_hi(n, AE[e % 2][:, 0, m, :], SLOTS)
                    if m < 2 and e + 2 <= E:
                        ffn_hi(e + 2, m)
                for c in range(5):
                    if c < 4 and e + 1 < E:
                        xg_hi(4 * (e + 1) + c)
                    if c:
                        y_out(4 * e + c - 1)
                if e + 2 <= E:
                    ffn_hi(e + 2, 2)

        @block.vector
        def _(dve):
            V = nc.vector
            made = [0]

            def link(ins):
                made[0] += 1
                ins.then_inc(s_dve, 1)
                dve.wait_ge(s_dve, made[0])

            dve.wait_ge(s_edges, 32)
            link(V.tensor_copy(EF[:, :, :], ED[:, :, :, :].rearrange("q s a p -> q s (a p)")))
            link(V.tensor_scalar(EQ[:, 0, :], EF[:, 0, :], 1.0 / T, 0.5 / T - 0.5, ALU.mult, ALU.add))
            link(V.tensor_scalar(EQ[:, 1, :], EF[:, 1, :], 1.0 / DC, 0.5 / DC - 0.5, ALU.mult, ALU.add))
            link(V.tensor_copy(EG[:, :, :], EQ[:, :, :]))
            link(V.scalar_tensor_tensor(EK[:, 1, :], EG[:, 0, :], -float(T), EF[:, 0, :], ALU.mult, ALU.add))
            link(V.scalar_tensor_tensor(EK[:, 0, :], EG[:, 1, :], 1000.0 - DC, EF[:, 1, :], ALU.mult, ALU.add))
            V.scalar_tensor_tensor(EK[:, 0, :], EG[:, 0, :], float(DC), EK[:, 0, :], ALU.mult, ALU.add
                                   ).then_inc(s_keys, 1)
            dve.wait_ge(s_const, 15)
            link(V.tensor_scalar(QI[:, :], MX[:, :], 1.0 / DC, 0.5 / DC - 0.5, ALU.mult, ALU.add))
            link(V.tensor_copy(MM[:, :], QI[:, :]))
            link(V.scalar_tensor_tensor(KEY[:, KT:KA], MM[:, :], 1000.0 - DC, ZZ[:, :], ALU.mult, ALU.add))
            dve.wait_ge(s_once, 1)
            link(V.tensor_copy(KEY[:, PADT:PADT + ET], PS[0:T, 7, 0:ET]))
            link(V.tensor_copy(SLO[:, PADT:PADT + ET], PS[0:T, 7, ET:2 * ET]))

            def norm(X, BSt, MVt, tiles, turn):
                for i in tiles:
                    for a in range(2):
                        V.bn_stats(BSt[:, i, a, :], X[:, i, DH * a:DH * a + DH]).then_inc(s_dve, 1)
                        made[0] += 1
                dve.wait_ge(s_dve, made[0])
                for i in tiles:
                    V.bn_aggr(MVt[:, i, :], BSt[:, i, :, :].rearrange("p a s -> p (a s)")).then_inc(s_dve, 1)
                    made[0] += 1
                dve.wait_ge(s_dve, made[0])
                a, b = tiles[0], tiles[-1] + 1
                V.tensor_scalar(MVt[:, a:b, 1], MVt[:, a:b, 1], EPS, None, ALU.add).then_inc(s_var, 1)
                dve.wait_ge(s_sd, turn)
                link(V.reciprocal(SD[:, a:b], SD[:, a:b]))
                link(V.tensor_scalar(SD[:, a:b], SD[:, a:b], SX, None, ALU.mult))

            for n, (a, b) in enumerate(PIECES):
                dve.wait_ge(s_x[n], 16)
                norm(XA, BS1, MV1, range(a, b), n + 1)
                for i in range(a, b):
                    V.tensor_scalar(XA[:, i, :], XA[:, i, :], MV1[:, i, 0:1], SD[:, i:i + 1], ALU.subtract,
                                    ALU.mult).then_inc(s_xn, 1)

            def w1_lo(h, ks):
                for k in ks:
                    dve.wait_ge(s_wh, KD * h + k + 1)
                    V.scalar_tensor_tensor(W1S[:, k, 1, :], w1_in(h, k)[0], SW, W1S[:, k, 0, :], ALU.mult,
                                           ALU.subtract).then_inc(s_wl, 1)

            def h_lo(h, i):
                q = NT * h + i
                if i == 0:
                    dve.wait_ge(s_arep, 32 * (h + 1))
                dve.wait_ge(s_hh, q + 1)
                for a in range(2):
                    V.tensor_tensor_reduce(HB[h % 2][:, i, 1, :], PS[0:T, 6 + i % 2, :], AR1[:, a, :],
                                           1.0 / (SX * SW), 0.0, ALU.mult, ALU.add, AL[:, a, h, i:i + 1]
                                           ).then_inc(s_dve, 1)
                    made[0] += 1
                    dve.wait_ge(s_dve, made[0])
                V.scalar_tensor_tensor(HB[h % 2][:, i, 1, :], PS[0:T, 6 + i % 2, :], 1.0 / SW,
                                       HB[h % 2][:, i, 0, :], ALU.mult, ALU.subtract).then_inc(s_hl, 1)

            for i in range(NT):
                dve.wait_ge(s_xth, i + 1)
                b = 6 - 2 * (i % 2)
                V.tensor_tensor(XTR[:, i % 3, 1].rearrange("p (a k) n -> p a (k n)", a=2), PS[:, b:b + 2, 0:375],
                                XTR[:, i % 3, 0].rearrange("p (a k) n -> p a (k n)", a=2), ALU.subtract
                                ).then_inc(s_xtl, 1)
                if 4 <= i < 4 + KD:
                    w1_lo(0, (i - 4,))
            dve.wait_ge(s_xT, NT)
            for i in range(NT):
                a, b = OLP * i, min(OLP * (i + 1), KA)
                V.tensor_tensor(OL[:, a:b, :], iot[:, :].unsqueeze(1).to_broadcast([T, b - a, T]),
                                SLO[:, a:b].unsqueeze(2).to_broadcast([T, b - a, T]), ALU.is_equal
                                ).then_inc(s_ol, 1)
                h_lo(0, i)

            def chain_row(h):
                dve.wait_ge(s_alt, h + 1)
                if h:
                    dve.wait_ge(s_aad, 16 * h)
                V.tensor_copy(TR[0:NT, :], PS[0:NT, 6, 0:T]).then_inc(s_alc, 1)

            chain_row(0)
            with dve.Fori(0, NC // GC) as g:
                n = 0
                for c in range(GC):
                    for kind, t in jobs[c]:
                        col = (t + GT * g) if kind == "e" else (KT + t + 2 * g)
                        if n == 0:
                            dve.wait_ge(s_cm, g * NJ + 1)
                        elif n >= RO and n % RG == 0:
                            dve.wait_ge(s_cm, g * NJ + n - RO + RG + 1)
                        V.tensor_scalar(OR[:, n % RO, :], iok[:, :], 1000.0 * c, KEY[:, bass.ds(col, 1)],
                                        ALU.add, ALU.is_equal).then_inc(s_or, 1)
                        n += 1
                dve.wait_ge(s_or, (g + 1) * NJ)
                V.tensor_scalar(KEY[:, :], KEY[:, :], -1000.0 * GC, None, ALU.add).then_inc(s_k2, 1)
                dve.wait_ge(s_k2, g + 1)
            dve.wait_ge(s_ce, 1 + NC)
            V.tensor_reduce(MX[:, 0:1], CS[:, :], AX.X, ALU.add).then_inc(s_cs, 1)
            dve.wait_ge(s_once, 2)
            V.tensor_copy(flag[:, :], PS[:, 7, 0:1]).then_inc(s_cs, 1)
            dve.wait_ge(s_cs, 2)
            total = dve.value_load(flag[0:1, 0:1])
            with dve.If(total != TOTAL):
                V.tensor_scalar(KEY[:, :], KEY[:, :], 1000.0 * NC, None, ALU.add).then_inc(s_gk, 1)
                dve.wait_ge(s_gk, 1)
                with dve.Fori(0, NC) as c:
                    with dve.Fori(0, KA // 2) as t:
                        for u in range(2):
                            dve.wait_ge(s_gu, 1 + c * KA + 2 * t + u)
                            V.tensor_scalar(OR[:, u, :], iok[:, :], 0.0, KEY[:, bass.ds(2 * t + u, 1)],
                                            ALU.add, ALU.is_equal).then_inc(s_go, 1)
                    dve.wait_ge(s_gd, c + 1)
                    V.tensor_copy(CT[:, :, bass.ds(c * DC, DC)],
                                  PS[0:T, 5, 0:KC].rearrange("p (i n) -> p i n", n=DC)).then_inc(s_gk, 1)
                    V.tensor_scalar(KEY[:, :], KEY[:, :], -1000.0, None, ALU.add).then_inc(s_gk, 1)
                    dve.wait_ge(s_gk, 2 * c + 3)
            V.tensor_copy(MX[:, 0:1], CS[:, 0:1]).then_inc(s_ctok, 1)

            dve.wait_ge(s_va, 2 * NCH)
            link(V.tensor_copy(V2S[:, :, 0, :], V2F[:, :, :]))
            link(V.tensor_tensor(V2S[:, :, 1, :], V2F[:, :, :], V2S[:, :, 0, :], ALU.subtract))
            link(V.memset(A2C[:, :], 0.0))

            def chain_max(h, j):
                if j == 0:
                    dve.wait_ge(s_row, 16 * (h + 1))
                if h == 0:
                    dve.wait_ge(s_mm, j + 1)
                    mask, junk = MSK[:, j % 2, :], MSKT[1][:, 0, :]
                    if j:
                        dve.wait_ge(s_mu, j)
                else:
                    if h < H:
                        dve.wait_ge(s_ml, 16 * (NT // 2) * h)
                    else:
                        dve.wait_ge(s_ml, 16 * ((NT // 2) * h - (1 if j < 8 else 0)))
                    mask = junk = MSKT[j // 2 if h < H else j // 2 % 4][:, j % 2, :]
                V.tensor_tensor_reduce(junk, mask, ROW[:, 0, :], 1.0, 3.0 * NEG, ALU.add, ALU.max,
                                       MX[:, j:j + 1]).then_inc(s_mu, 1)

            def chain_shift(h):
                dve.wait_ge(s_mu, NT * (h + 1))
                aD = AL[:, 1, h, :]
                link(V.tensor_tensor(ZZ[:, :], MX[:, :], aD, ALU.add))
                link(V.scalar_tensor_tensor(MM[:, :], ZZ[:, :], SLOPE, ZZ[:, :], ALU.mult, ALU.max))
                link(V.tensor_tensor(AA[:, 0, :], aD, MM[:, :], ALU.subtract))
                V.scalar_tensor_tensor(AA[:, 1, :], aD, SLOPE, MM[:, :], ALU.mult, ALU.subtract).then_inc(s_aa, 1)
                V.tensor_scalar(ALF[:, h, :], AL[:, 0, h, :], SLOPE, None, ALU.mult).then_inc(s_al, 1)

            def chain_shift_rows(h):
                dve.wait_ge(s_aat, h + 1)
                dve.wait_ge(s_ald, 16 * (h + 1))
                V.tensor_copy(TR[:, :], PS[0:2 * NT, 6, 0:T]).then_inc(s_aac, 1)

            def p_leaky(h, i):
                q = NT * h + i
                dve.wait_ge(s_p1, q + 1)
                V.scalar_tensor_tensor(tmp(h, i)[0][:, :], ROW[:, 0, :], AL[:, 0, h, i:i + 1], tmp(h, i)[0][:, :],
                                       ALU.add, ALU.max).then_inc(s_p2, 1)

            def p_count(h, i):
                q = NT * h + i
                dve.wait_ge(s_p3, q + 1)
                V.scalar_tensor_tensor(tmp(h, i)[0][:, :], tmp(h, i)[0][:, :], 1.0, CT[:, i, :], ALU.min, ALU.mult
                                       ).then_inc(s_p4, 1)

            def p_step(h, i):
                if i < NT:
                    p_leaky(h, i)
                if 1 <= i <= NT:
                    p_count(h, i - 1)

            for j in range(NT):
                chain_max(0, j)
                if j % 3 == 2:
                    h_lo(1, j // 3)
            chain_shift(0)
            chain_shift_rows(0)
            for i in range(NT + 1):
                if NT // 3 + i < NT:
                    h_lo(1, NT // 3 + i)
                p_step(0, i)

            def att_read(h, c):
                a = 5 * h + c + 1
                t = 3 * (a % 2)
                dve.wait_ge(s_att, a + 1)
                for b, (lo, n) in enumerate(BLK):
                    if c < 0:
                        ins = V.reciprocal(RDEN[:, lo:lo + n], PS[:, t + b, 0:n])
                        ins.then_inc(s_rd, 1)
                    else:
                        y = 3 * (CH * h + c) + b
                        if y >= 3:
                            dve.wait_ge(s_y6, y - 2)
                        V.tensor_tensor(YB[:, y % 3, 0:n], PS[:, t + b, 0:n], RDEN[:, lo:lo + n], ALU.mult
                                        ).then_inc(s_y1, 1)

            def y_elu(h, c, b):
                y = 3 * (CH * h + c) + b
                n = BLK[b][1]
                dve.wait_ge(s_y2, y + 1)
                V.scalar_tensor_tensor(YB[:, y % 3, 0:n], YB[:, y % 3, 0:n], 1.0, RB[:, y % 2, 0:n], ALU.min,
                                       ALU.add).then_inc(s_y3, 1)

            def a2_add(g):
                dve.wait_ge(s_a2, g + 1)
                if g:
                    dve.wait_ge(s_a2r, g)
                V.tensor_tensor(A2C[:, :], A2C[:, :], PS[0:T, 7, 0:2 * NT], ALU.add).then_inc(s_a2r, 1)

            def w2_lo(ch):
                dve.wait_ge(s_w2h, ch + 1)
                V.scalar_tensor_tensor(W2S[ch][:, 1, :], W2G[(NCH + ch) % 3][:, :], SW, W2S[ch][:, 0, :], ALU.mult,
                                       ALU.subtract).then_inc(s_w2l, 1)

            for h in range(H):
                att_read(h, -1)
                if h + 1 < H:
                    chain_row(h + 1)
                if h:
                    a2_add(CH * h - 1)
                dve.wait_ge(s_rd, 3 * (h + 1))
                for c in range(CH):
                    if c == CH - 1 and h + 1 < H:
                        for i in range(NPRE):
                            p_step(h + 1, i)
                    if c == CH - 1:
                        a2_add(CH * h + c - 1)
                    att_read(h, c)
                    for b in range(3):
                        y_elu(h, c, b)
                    if c == 1 and h + 1 < H:
                        chain_shift_rows(h + 1)
                    if 0 < c < CH - 1:
                        a2_add(CH * h + c - 1)
                    if c < 3 and h + 2 < H:
                        w1_lo(h + 2, range(2 * c, 2 * c + 2))
                    if c == 0 and h + 1 < H:
                        for j in range(NT):
                            chain_max(h + 1, j)
                        chain_shift(h + 1)
                    if h + 1 == H:
                        for ch in range(4 * c, 4 * c + 4):
                            w2_lo(ch)
                if h + 1 < H:
                    for i in range(NPRE, NT + NPRE):
                        if h + 2 < H:
                            h_lo(h + 2, i - NPRE)
                        if i < NT + 1:
                            p_step(h + 1, i)
            a2_add(NCH - 1)
            dve.wait_ge(s_a2r, NCH)

            link(V.tensor_scalar(AL[:, 0, H, :], A2C[:, 0:2 * NT:2], 1.0 / (SX * SW), None, ALU.mult))
            V.tensor_scalar(AL[:, 1, H, :], A2C[:, 1:2 * NT:2], 1.0 / (SX * SW), None, ALU.mult).then_inc(s_a2r, 1)
            dve.wait_ge(s_a2r, NCH + 1)
            chain_row(H)
            for j in range(NT):
                chain_max(H, j)
            chain_shift(H)
            chain_shift_rows(H)

            def h2_lo(j):
                dve.wait_ge(s_h2h, j + 1)
                b = 2 * (j % 3)
                V.memset(H2[j][:, 0, D:D + 1], 1.0).then_inc(s_h2l, 1)
                V.memset(H2[j][:, 1, D:D + 1], 0.0).then_inc(s_h2l, 1)
                V.scalar_tensor_tensor(H2[j][:, 1, 0:D].rearrange("p (a n) -> p a n", a=2),
                                       PS[0:T, b:b + 2, 0:DH], 1.0 / SW,
                                       H2[j][:, 0, 0:D].rearrange("p (a n) -> p a n", a=2), ALU.mult,
                                       ALU.subtract).then_inc(s_h2l, 1)

            for i in range(NT + 1):
                p_step(H, i)
                if i < NT:
                    h2_lo(i)
            def x2t_lo(i):
                dve.wait_ge(s_x2h, i + 1)
                b = 2 * (i % 2)
                V.tensor_tensor(X2T[:, 1, :, T * i:T * i + T].rearrange("p (a k) n -> p a k n", a=2),
                                PS[:, b:b + 2, 0:375].rearrange("p a (k n) -> p a k n", n=T),
                                X2T[:, 0, :, T * i:T * i + T].rearrange("p (a k) n -> p a k n", a=2),
                                ALU.subtract).then_inc(s_x2lo, 1)

            dve.wait_ge(s_wh, KD * H + 1)
            V.scalar_tensor_tensor(WRS[:, :, 1, :], WRG[:, :, :], SW, WRS[:, :, 0, :], ALU.mult, ALU.subtract
                                   ).then_inc(s_wl, 1)
            for j in range(NT):
                dve.wait_ge(s_at2, j + 1)
                b = 4 + 2 * (j % 2)
                link(V.reciprocal(ZZ[:, j:j + 1], PS[0:T, b + 1, DH - 1:DH]))
                link(V.tensor_scalar(ZZ[:, j:j + 1], ZZ[:, j:j + 1], 1.0 / SX, None, ALU.mult))
                dve.wait_ge(s_xb, j + 1)
                link(V.scalar_tensor_tensor(X2[:, j, 0:DH + 1], PS[0:T, b, 0:DH + 1], ZZ[:, j:j + 1],
                                            X2[:, j, 0:DH + 1], ALU.mult, ALU.add))
                V.scalar_tensor_tensor(X2[:, j, DH + 1:D], PS[0:T, b + 1, 0:DH - 1], ZZ[:, j:j + 1],
                                       X2[:, j, DH + 1:D], ALU.mult, ALU.add).then_inc(s_x2, 1)

                dve.wait_ge(s_x2, j + 1)
                norm(X2, BS, MV, (j,), len(PIECES) + 1 + j)
                if j >= 2:
                    dve.wait_ge(s_x2t, j - 1)
                    dve.wait_ge(s_xns[j % 2], 16 * (j // 2))
                V.tensor_scalar(XN2[:, j % 2, :], X2[:, j, :], MV[:, j, 0:1], SD[:, j:j + 1], ALU.subtract,
                                ALU.mult).then_inc(s_xn2, 1)
                if j:
                    x2t_lo(j - 1)


            def ffn_lo(n, q):
                dve.wait_ge(s_wgh, 3 * n + q + 1)
                V.scalar_tensor_tensor(WS[n % 2][:, 1, HALF * q:HALF * q + HALF],
                                       (WG0 if n == 0 and q < 2 else WG)[:, HALF * q:HALF * q + HALF], SW,
                                       WS[n % 2][:, 0, HALF * q:HALF * q + HALF], ALU.mult, ALU.subtract
                                       ).then_inc(s_wgl, 1)

            ffn_lo(0, 0)
            x2t_lo(NT - 1)
            ffn_lo(0, 1)
            ffn_lo(0, 2)
            dve.wait_ge(s_lg, 1)
            dve.wait_ge(s_const, 22 + KD)
            link(V.tensor_scalar(LG[:, :, :], PS[0:T, 5, 0:NT * E].rearrange("p (j e) -> p j e", e=E),
                                 1.0 / (SX * SW), None, ALU.mult))
            link(V.tensor_reduce(RK[:, 0, :], LG[:, :, :], AX.X, ALU.max))
            V.tensor_tensor(LG[:, :, :], LG[:, :, :], RK[:, 0, :].unsqueeze(2).to_broadcast([T, NT, E]),
                            ALU.subtract).then_inc(s_lgm, 1)

            def gate_up(n, w):
                dve.wait_ge(s_sg, n + 1)
                dve.wait_ge(s_udn, n + 1)
                V.scalar_tensor_tensor(SG[:, n % 2, 0:w], PS[:, 7, 0:w], SA / (SX * SW),
                                       SG[:, n % 2, 0:w], ALU.mult, ALU.mult).then_inc(s_gx, 1)

            dve.wait_ge(s_pe, 1)
            link(V.tensor_reduce(RK[:, 0, :], LG[:, :, :], AX.X, ALU.add))
            link(V.reciprocal(RK[:, 1, :], RK[:, 0, :]))
            link(V.tensor_tensor(LG[:, :, :], LG[:, :, :], RK[:, 1, :].unsqueeze(2).to_broadcast([T, NT, E]),
                                 ALU.mult))
            for j in range(NT):
                link(V.max(M8[:, j, :], LG[:, j, :]))
                link(V.max_index(I8[:, j, :], M8[:, j, :], LG[:, j, :]))
            gate_up(0, BLK[0][1])
            link(V.tensor_copy(IK[:, 0, :], I8[:, :, 0]))
            link(V.tensor_copy(IK[:, 1, :], I8[:, :, 1]))
            link(V.tensor_tensor(RK[:, 0, :], M8[:, :, 0], M8[:, :, 1], ALU.add))
            link(V.tensor_scalar(RK[:, 0, :], RK[:, 0, :], 1e-9, None, ALU.max))
            link(V.reciprocal(RK[:, 1, :], RK[:, 0, :]))
            for k in range(2):
                link(V.tensor_tensor(WK[:, k, :], M8[:, :, k], RK[:, 1, :], ALU.mult))
                link(V.tensor_tensor(OK[k][:, :, :], io8[:, :].unsqueeze(1).to_broadcast([T, NT, E]),
                                     IK[:, k, :].unsqueeze(2).to_broadcast([T, NT, E]), ALU.is_equal))
                link(V.tensor_tensor(OT[k][:, :, :], OK[k][:, :, :],
                                     tokid[:, :].unsqueeze(2).to_broadcast([T, NT, E]), ALU.mult))
                for r in range(3):
                    link(V.tensor_copy(O3[k][:, :, E * r:E * r + E], OK[k][:, :, :]))
            gate_up(1, BLK[1][1])
            link(V.tensor_tensor(SS[:, :, :], OK[0][:, :, :], WK[:, 0, :].unsqueeze(2).to_broadcast([T, NT, E]),
                                 ALU.mult))
            link(V.tensor_tensor(LG[:, :, :], OK[1][:, :, :], WK[:, 1, :].unsqueeze(2).to_broadcast([T, NT, E]),
                                 ALU.mult))
            link(V.tensor_tensor(SS[:, :, :], SS[:, :, :], LG[:, :, :], ALU.add))
            link(V.tensor_tensor(LG[:, :, :], OK[0][:, :, :], OK[1][:, :, :], ALU.add))
            link(V.tensor_scalar(LG[:, :, :], LG[:, :, :], -1.0, None, ALU.add))
            link(V.tensor_tensor(SS[:, :, :], SS[:, :, :], LG[:, :, :], ALU.add))
            for r in range(2):
                link(V.tensor_copy(S3[:, :, E * r:E * r + E], SS[:, :, :]))
                link(V.tensor_tensor(SS[:, :, :], SS[:, :, :], S3[:, :, E * r:E * r + E], ALU.subtract))
            link(V.memset(CA[:, :, :, :], 0.0))
            V.tensor_copy(S3[:, :, 2 * E:3 * E], SS[:, :, :]).then_inc(s_s3, 1)
            ffn_lo(1, 0)
            gate_up(2, BLK[2][1])
            ffn_lo(1, 1)
            for n in range(3):
                dve.wait_ge(s_s3t, n + 1)
                for b in range(2):
                    dve.wait_ge(s_xns[b], 16 * NT // 2)
                dve.wait_ge(s_x2t, NT)
                V.tensor_copy([S3T, O3T[0], O3T[1]][n][:, :].rearrange("p (a j n) -> p a j n", a=2, n=T),
                              blocks16(PB, 24, 2 * n)).then_inc(s_s3c, 1)

            def rank(r):
                j, k = divmod(r, 2)
                t = 3 * (r % 2)
                R = PSF[0:T, 512 * t:512 * t + N]
                own = WK[:, k, j:j + 1]
                dve.wait_ge(s_rr, r + 1)
                if r:
                    dve.wait_ge(s_rk, r)
                if j:
                    V.tensor_scalar(JN2[:, 0:T * j], R[:, 0:T * j], own, None, ALU.is_ge, ALU.add,
                                    accum_out=CA[:, 0, k, j:j + 1]).then_inc(s_dve, 1)
                    made[0] += 1
                    dve.wait_ge(s_dve, made[0])
                link(V.tensor_scalar(JN2[:, T * j:N], R[:, T * j:N], own, None, ALU.is_gt, ALU.add,
                                     accum_out=CA[:, 1, k, j:j + 1]))
                V.scalar_tensor_tensor(JN2[:, 0:T], R[:, T * j:T * j + T], own, TRI[:, :], ALU.is_equal, ALU.mult,
                                       accum_out=CA[:, 2, k, j:j + 1]).then_inc(s_rk, 1)

            for n in range(3, 9):
                if n >= RANK_FROM:
                    rank(3 * (n - RANK_FROM))
                gate_up(n, BLK[n % 3][1])
                if n == 3:
                    ffn_lo(1, 2)
                if n >= RANK_FROM:
                    rank(3 * (n - RANK_FROM) + 1)
                    rank(3 * (n - RANK_FROM) + 2)
            for r in range(3 * (9 - RANK_FROM), 2 * NT):
                rank(r)
            dve.wait_ge(s_rk, 2 * NT)
            link(V.tensor_tensor(RK[:, :, :], CA[:, 0, :, :], CA[:, 1, :, :], ALU.add))
            link(V.tensor_tensor(RK[:, :, :], RK[:, :, :], CA[:, 2, :, :], ALU.add))
            for k in range(2):
                for j in range(NT):
                    V.tensor_scalar(IND[:, k, j, :], io392[:, :], RK[:, k, j:j + 1], None, ALU.is_equal
                                    ).then_inc(s_ind, 1)
            link(V.tensor_scalar(CA[:, 0, :, :], RK[:, :, :], float(CAP), 1.0e6, ALU.is_ge, ALU.mult))
            link(V.tensor_tensor(RK[:, :, :], RK[:, :, :], CA[:, 0, :, :], ALU.add))
            link(V.tensor_scalar(CA[:, 0, :, :], IK[:, :, :], E - 1.0, None, ALU.is_equal))
            link(V.scalar_tensor_tensor(CA[:, 1, :, :], IK[:, :, :], float(SLOTS), RK[:, :, :], ALU.mult, ALU.add))
            link(V.tensor_scalar(CA[:, 2, :, :], CA[:, 1, :, :], -2.0e6, None, ALU.add))
            link(V.tensor_tensor(CA[:, 2, :, :], CA[:, 2, :, :], CA[:, 0, :, :], ALU.mult))
            link(V.tensor_tensor(RK[:, 0, :], CA[:, 2, 0, :], CA[:, 2, 1, :], ALU.add))
            link(V.tensor_scalar(RK[:, 0, :], RK[:, 0, :], 2.0e6, None, ALU.add))
            link(V.tensor_copy(IDX[0:T, 2, :], RK[:, 0, :]))
            link(V.scalar_tensor_tensor(CA[:, 1, :, :], CA[:, 0, :, :], 2.0e6, CA[:, 1, :, :], ALU.mult, ALU.add))
            link(V.tensor_copy(IDX[0:T, 0:2, :], CA[:, 1, :, :]))
            link(V.tensor_tensor(CA[:, 2, :, :], CA[:, 0, :, :], WK[:, :, :], ALU.mult))
            link(V.tensor_tensor(WL[:, :], CA[:, 2, 0, :], CA[:, 2, 1, :], ALU.add))
            dve.wait_ge(s_tk, 1)
            V.tensor_copy(TOK[0:SC, :, :], PS[0:SC, 0, 0:4 * E].rearrange("p (c e) -> p c e", e=E)).then_inc(s_tok, 1)

            def xg_lo(g):
                e, c = divmod(g, 4)
                dve.wait_ge(s_xgh, g + 1)
                b = 2 + 2 * (g % 2)
                V.tensor_tensor(XGT[e % 2][:, 1, :, SC * c:SC * c + SC].rearrange("p (a k) n -> p a k n", a=2),
                                PS[:, b:b + 2, 0:3 * SC].rearrange("p a (k n) -> p a k n", n=SC),
                                XGT[e % 2][:, 0, :, SC * c:SC * c + SC].rearrange("p (a k) n -> p a k n", a=2),
                                ALU.subtract).then_inc(s_xgl, 1)

            def add_back(n):
                j, k = divmod(n, 2)
                b = n % GRN
                if n == 0:
                    dve.wait_ge(s_sdr, NT)
                dve.wait_ge(s_gg[b], 16 * (n // GRN + 1))
                if n:
                    dve.wait_ge(s_g1, n)
                V.scalar_tensor_tensor(X2[:, j, :], GR[0:T, b, :], WK[:, k, j:j + 1], X2[:, j, :], ALU.mult,
                                       ALU.add).then_inc(s_g1, 1)
                if n + GRN < 2 * NT:
                    dve.wait_ge(s_g1, n + 1)
                    V.memset(GR[:, b, :], 0.0).then_inc(s_gz, 1)

            for c in range(4):
                xg_lo(c)
            for e in range(E):
                for m in range(KI):
                    gate_up(9 + KI * e + m, SLOTS)
                    if m < 2 and e + 2 <= E:
                        ffn_lo(e + 2, m)
                    if m == 1 and e == E - 1:
                        add_back(0)
                        add_back(1)
                if e + 1 < E:
                    for c in range(4):
                        xg_lo(4 * (e + 1) + c)
                if e + 2 <= E:
                    ffn_lo(e + 2, 2)
            for n in range(2, 2 * NT):
                add_back(n)
            dve.wait_ge(s_g1, 2 * NT)
            for j in range(NT):
                dve.wait_ge(*last_in[j])
                V.scalar_tensor_tensor(X2[:, j, :], GRL[0:T, j, :], WL[:, j:j + 1], X2[:, j, :], ALU.mult, ALU.add
                                       ).then_inc(s_gl, 1)

        @block.tensor
        def _(pe):
            M = nc.tensor.matmul

            def mm3(out_, lhs, rhs, first, last):
                for a, b in ((0, 0), (0, 1), (1, 0)):
                    ins = M(out_, lhs(a), rhs(b), start=first and a + b == 0, stop=last and a == 1)
                return ins

            pe.wait_ge(s_const, 15)
            pe.wait_ge(s_keys, 1)
            for a in range(2):
                for q in range(2):
                    ins = nc.tensor.transpose(PS[0:T, 7, ET * a + 85 * q:ET * a + 85 * q + 85],
                                              EK[:, a, T * q:T * q + T], idf[0:85, 0:85])
            ins.then_inc(s_once, 1)
            for i in range(NT):
                pe.wait_ge(s_xn, i + 1)
                if i >= 2:
                    pe.wait_ge(s_xtl, i - 1)
                b = 6 - 2 * (i % 2)
                for k in range(KD):
                    ins = nc.tensor.transpose(PS[:, b + k // 3, T * (k % 3):T * (k % 3) + T],
                                              XA[:, i, 128 * k:128 * k + 128], idf[0:T, 0:T])
                ins.then_inc(s_xT, 1)

            def proj(h, tiles=range(NT)):
                pe.wait_ge(s_wl, KD * (h + 1))
                for i in tiles:
                    v = NT + NT * h + i
                    pe.wait_ge(s_xts[v % 3], 16 * (v // 3 + 1))
                    if i == 0 and h == 0:
                        pe.wait_ge(s_xtl, NT)
                    if NT * h + i >= 2:
                        pe.wait_ge(s_hl, NT * h + i - 1)
                    if h == 1 and i == 4:
                        pe.wait_ge(s_aac, 1)
                    if i < 2 and h:
                        pe.wait_ge(s_alc, h)
                        if h >= 2:
                            pe.wait_ge(s_a2r, CH * (h - 1) - 1)
                    for k in range(KD):
                        ins = mm3(PS[0:T, 6 + i % 2, :], lambda a: XTR[:, v % 3, a, k, :],
                                  lambda b: W1S[:, k, b, :], k == 0, k == KD - 1)
                    ins.then_inc(s_proj, 1)

            def chain_row(h):
                if h < H:
                    pe.wait_ge(s_hl, NT * (h + 1))
                else:
                    pe.wait_ge(s_a2r, NCH + 1)
                nc.tensor.transpose(PS[0:NT, 6, 0:T], AL[:, 0, h, :], idf[0:T, 0:T]).then_inc(s_alt, 1)

            def chain_shift(h):
                pe.wait_ge(s_aa, h + 1)
                nc.tensor.transpose(PS[0:2 * NT, 6, 0:T], AA[:, :, :].rearrange("p a i -> p (a i)"),
                                    idf[0:T, 0:T]).then_inc(s_aat, 1)

            proj(0)
            chain_row(0)
            pe.wait_ge(s_ol, NT)
            pe.sem_inc(s_cm, 1)
            pe.sem_inc(s_gu, 1)
            with pe.Fori(0, NC // GC) as g:
                n = 0
                for c in range(GC):
                    pe.wait_ge(s_ce, 1 + GC * g)
                    for q, (kind, t) in enumerate(jobs[c]):
                        col = (t + GT * g) if kind == "e" else (KT + t + 2 * g)
                        if n % PG == 0:
                            pe.wait_ge(s_or, g * NJ + min(n + PG, NJ))
                        ins = M(PS[0:T, c, 0:KC], OL[:, bass.ds(col, 1), :], OR[:, n % RO, :], start=q == 0,
                                stop=q == len(jobs[c]) - 1)
                        ins.then_inc(s_cm, 1)
                        n += 1
            pe.wait_ge(s_cs, 1)
            M(PS[:, 7, 0:1], onesf[:, :], MX[:, 0:1], start=True, stop=True).then_inc(s_once, 1)
            pe.wait_ge(s_cs, 2)
            total = pe.value_load(flag[0:1, 0:1])
            with pe.If(total != TOTAL):
                with pe.Fori(0, NC) as c:
                    pe.wait_ge(s_gk, 2 * c + 1)
                    M(PS[0:T, 5, 0:KC], OL[:, 0, :], iok[:, :], start=True, stop=False)
                    with pe.Fori(0, KA // 2) as t:
                        for u in range(2):
                            pe.wait_ge(s_go, c * KA + 2 * t + u + 1)
                            M(PS[0:T, 5, 0:KC], OL[:, bass.ds(2 * t + u, 1), :], OR[:, u, :], start=False,
                              stop=False).then_inc(s_gu, 1)
                    M(PS[0:T, 5, 0:KC], OL[:, 0, :], iok[:, :], start=False, stop=True).then_inc(s_gd, 1)
            pe.wait_ge(s_ctok, 1)
            for j in range(NT):
                if j >= 3:
                    pe.wait_ge(s_mm, j - 2)
                b = 2 * (j % 3)
                for i in range(NT):
                    ins = nc.tensor.transpose(PH[0:T, col16(b, i):col16(b, i) + T], CT[:, i, T * j:T * j + T], idh[0:T, 0:T])
                ins.then_inc(s_mt, 1)
                if j % 3 == 2:
                    proj(1, (j // 3,))
            pe.wait_ge(s_hl, NT + 3)
            chain_shift(0)
            proj(1, range(NT // 3, NT))

            def att(h, c):
                a_ = 5 * h + c + 1
                t = 3 * (a_ % 2)
                if a_ >= 2:
                    g2 = a_ - 2
                    h0, c0 = divmod(g2, 5)
                    if c0 == 0:
                        pe.wait_ge(s_rd, 3 * (h0 + 1))
                    else:
                        pe.wait_ge(s_y1, 3 * (CH * h0 + c0))
                else:
                    pe.wait_ge(s_mm, NT)
                for i in range(NT):
                    if c < 0:
                        pe.wait_ge(s_p6, NT * h + i + 1)
                        for b, (lo, n) in enumerate(BLK):
                            for part in range(2):
                                ins = M(PS[:, t + b, 0:n], ones[:, :], P[:, i, part, lo:lo + n],
                                        start=i == 0 and part == 0, stop=i == NT - 1 and part == 1)
                    else:
                        hb = HB[h % 2]
                        if c and i == 7:
                            al2(CH * h + c - 1)
                        if c == 2 and i == 5 and h + 1 < H:
                            chain_shift(h + 1)
                        for pa, pb in ((0, 0), (0, 1), (1, 0)):
                            for b, (lo, n) in enumerate(BLK):
                                ins = M(PS[:, t + b, 0:n], hb[:, i, pa, 128 * c:128 * c + 128],
                                        P[:, i, pb, lo:lo + n], start=i == 0 and pa + pb == 0,
                                        stop=i == NT - 1 and pa == 1)
                        if c == CH - 1 and i < NT - 1:
                            ins.then_inc(s_pf, 1)
                ins.then_inc(s_att, 1)

            def al2(g):
                pe.wait_ge(s_y6, 3 * (g + 1))
                if g:
                    pe.wait_ge(s_a2r, g)
                if g % CH == CH - 1 or g == 0:
                    pe.wait_ge(s_hl, NT * min(H, g // CH + (3 if g else 2)))
                for j in range(NT):
                    ins = mm3(PS[0:T, 7, 2 * j:2 * j + 2], lambda a: H1O[:, g % 2, a, T * j:T * j + T],
                              lambda b: V2S[:, g, b, :], True, True)
                ins.then_inc(s_a2, 1)

            for h in range(H):
                att(h, -1)
                if h + 1 < H:
                    chain_row(h + 1)
                if h:
                    al2(CH * h - 1)
                for c in range(CH):
                    att(h, c)
                if h + 2 < H:
                    pe.wait_ge(s_aac, h + 2)
                    proj(h + 2)

            for j in range(NT):
                ht = HT[j % 2]
                if j == 0:
                    ht = HT0
                    pe.wait_ge(s_a2v, 48)
                    pe.wait_ge(s_y1, 3 * NCH)
                else:
                    pe.wait_ge(s_ht[j % 2], 16 * ((j + 1) // 2))
                    if j >= 3:
                        pe.wait_ge(s_h2l, 3 * (j - 2))
                b = 2 * (j % 3)
                for ch in range(NCH):
                    if j == 0:
                        pe.wait_ge(s_w2l, ch + 1)
                        if ch == NCH - CH:
                            al2(NCH - 1)
                            chain_row(H)
                            pe.wait_ge(s_h0, 16)
                    for q in range(2):
                        ins = mm3(PS[0:T, b + q, 0:DH], lambda a: ht[:, a, ch, :],
                                  lambda r: W2S[ch][:, r, DH * q:DH * q + DH], ch == 0, ch == NCH - 1)
                ins.then_inc(s_pj2, 1)
                if j == 2:
                    chain_shift(H)
            def x2_T(i):
                pe.wait_ge(s_xn2, i + 1)
                if i >= 2:
                    pe.wait_ge(s_x2lo, i - 1)
                b = 2 * (i % 2)
                for k in range(KD):
                    ins = nc.tensor.transpose(PS[:, b + k // 3, T * (k % 3):T * (k % 3) + T],
                                              XN2[:, i % 2, 128 * k:128 * k + 128], idf[0:T, 0:T])
                ins.then_inc(s_x2t, 1)

            pe.wait_ge(s_aac, H + 1)
            pe.wait_ge(s_h2l, 3 * (NT - 1))
            for j in range(NT):
                if j >= 2:
                    pe.wait_ge(s_x2, j - 1)
                b = 4 + 2 * (j % 2)
                for i in range(NT):
                    if j == 0:
                        pe.wait_ge(s_p6, NT * H + i + 1)
                        pe.wait_ge(s_h2l, 3 * (i + 1))
                    for q, (lo, n) in enumerate(((0, DH + 1), (DH + 1, DH))):
                        ins = mm3(PS[0:T, b + q, 0:n], lambda a: P[:, i, a, T * j:T * j + T],
                                  lambda r: H2[i][:, r, lo:lo + n], i == 0, i == NT - 1)
                ins.then_inc(s_at2, 1)
                if j:
                    x2_T(j - 1)

            def logits(j):
                for k in range(KD):
                    ins = mm3(PS[0:T, 5, E * j:E * j + E], lambda a: X2T[:, a, k, T * j:T * j + T],
                              lambda r: WRS[:, k, r, :], k == 0, k == KD - 1)
                return ins

            pe.wait_ge(s_wl, KD * H + 1)
            pe.wait_ge(s_x2, NT - 1)
            pe.wait_ge(s_x2lo, NT - 2)
            for j in range(NT - 2):
                logits(j)
            x2_T(NT - 1)
            pe.wait_ge(s_x2lo, NT)
            for j in range(NT - 2, NT):
                ins = logits(j)
            ins.then_inc(s_lg, 1)

            def gate_or_up(n, q, wb, rhs, w, m):
                if n:
                    pe.wait_ge((s_sg, s_gx)[q], n)
                for k in range(KD):
                    ins = mm3(PS[:, 6 + q, 0:w],
                              lambda a: wb[:, a, HALF * q + INNER * k + 128 * m:HALF * q + INNER * k + 128 * m + 128],
                              lambda r: rhs(r, k), k == 0, k == KD - 1)
                ins.then_inc((s_gdn, s_udn)[q], 1)

            def rank_rows(r):
                j, k = divmod(r, 2)
                t = 3 * (r % 2)
                if r >= 2:
                    pe.wait_ge(s_rk, r - 1)
                else:
                    pe.wait_ge(s_s3c, 3)
                for lo in range(0, N, 512):
                    w = min(512, N - lo)
                    ins = M(PSF[0:T, 512 * t + lo:512 * t + lo + w], O3T[k][:, T * j:T * j + T],
                            S3T[:, lo:lo + w], start=True, stop=True)
                ins.then_inc(s_rr, 1)

            def down(lhs, wb, o_):
                for q in range(2):
                    for m in range(KI):
                        ins = mm3(o_(q), lambda a: lhs(a, m),
                                  lambda r: wb[:, r, 2 * HALF + D * m + DH * q:2 * HALF + D * m + DH * q + DH],
                                  m == 0, m == KI - 1)
                return ins

            pe.wait_ge(s_wgl, 2)
            for n in range(9):
                m, b = divmod(n, 3)
                lo, w = BLK[b]
                for q in range(2):
                    gate_or_up(n, q, WS[0], lambda r, k: X2T[:, r, k, lo:lo + w], w, m)
                    if n >= RANK_FROM:
                        for r in ((0,), (1, 2))[q]:
                            rank_rows(3 * (n - RANK_FROM) + r)
                if n == 2:
                    pe.wait_ge(s_s3, 1)
                    for v, S_ in enumerate((S3, O3[0], O3[1])):
                        for j in range(NT):
                            ins = nc.tensor.transpose(PB[0:24, col16(2 * v, j):col16(2 * v, j) + T], S_[:, j, :],
                                                      idb[0:T, 0:T])
                        ins.then_inc(s_s3t, 1)
            pe.wait_ge(s_wgl, 3)
            pe.wait_ge(s_alo, 9)
            pe.wait_ge(s_gx, 9)
            for j in range(NT):
                if j:
                    pe.wait_ge(s_sdc, j)
                down(lambda a, m: AB[:, a, m, T * j:T * j + T], WS[0], lambda q: PS[0:T, 6 + q, 0:DH]
                     ).then_inc(s_sd3, 1)
                if 3 * (9 - RANK_FROM) + j < 2 * NT:
                    rank_rows(3 * (9 - RANK_FROM) + j)
                if j == 7:
                    pe.wait_ge(s_ind, 2 * NT)
                    pe.wait_ge(s_rk, 2 * NT)
                    for c in range(4):
                        for k in range(2):
                            for i in range(NT):
                                ins = M(PS[0:SC, 0, E * c:E * c + E], IND[:, k, i, SC * c:SC * c + SC],
                                        OT[k][:, i, :], start=k + i == 0, stop=k == 1 and i == NT - 1)
                    ins.then_inc(s_tk, 1)

            def rows_T(g):
                if g == 0:
                    pe.wait_ge(s_tok, 1)
                pe.wait_ge(s_xg[g % XGN], 16 * (g // XGN + 1))
                if g >= 2:
                    pe.wait_ge(s_xgl, g - 1)
                b = 2 + 2 * (g % 2)
                for k in range(KD):
                    ins = nc.tensor.transpose(PS[:, b + k // 3, SC * (k % 3):SC * (k % 3) + SC],
                                              XG[0:SC, g % XGN, 128 * k:128 * k + 128], idf[0:SC, 0:SC])
                ins.then_inc(s_xgt, 1)

            for c in range(4):
                rows_T(c)
            for e in range(E):
                wb = WS[(e + 1) % 2]
                pe.wait_ge(s_xgl, 4 * (e + 1))
                pe.wait_ge(s_wgl, 3 * (e + 2) - 1)
                if e == 0:
                    pe.wait_ge(s_sdc, NT)
                else:
                    pe.wait_ge(s_yo, 4 * e - 1)
                for m in range(KI):
                    for q in range(2):
                        gate_or_up(9 + KI * e + m, q, wb, lambda r, k: XGT[e % 2][:, r, k, :], SLOTS, m)
                for c in range(4):
                    g = 4 * e + c
                    if e + 1 < E:
                        for r in ((0, 1), (2,), (3,), ())[c]:
                            rows_T(4 * (e + 1) + r)
                    if c == 0:
                        pe.wait_ge(s_alo, 9 + KI * (e + 1))
                        pe.wait_ge(s_gx, 9 + KI * (e + 1))
                        pe.wait_ge(s_wgl, 3 * (e + 2))
                    if g >= 2:
                        pe.wait_ge(s_yo, g - 1)
                    b = 6 if c % 2 == 0 else 0
                    down(lambda a, m: AE[e % 2][:, a, m, SC * c:SC * c + SC], wb,
                         lambda q: PS[0:SC, b + q, 0:DH]).then_inc(s_ed, 1)


_INS = ['x', 'src', 'dst', 'L0_gnn_W1', 'L0_gnn_att_src1', 'L0_gnn_att_dst1', 'L0_gnn_b1', 'L0_gnn_W2',
        'L0_gnn_att_src2', 'L0_gnn_att_dst2', 'L0_gnn_b2', 'L0_ffn_Wr', 'L0_ffn_w1', 'L0_ffn_w3', 'L0_ffn_w2',
        'L0_ffn_s1', 'L0_ffn_s3', 'L0_ffn_s2']
_OUTS = [((1250, 768), 'float32')]


def kernel(**inputs):
    import numpy as _np
    import concourse.bacc as _bacc
    from concourse import mybir as _mybir
    from concourse.bass_utils import run_bass_kernel_spmd as _run

    nc = _bacc.Bacc("TRN2", target_bir_lowering=False, num_devices=1)
    arrays, args = {}, []
    for name in _INS:
        a = _np.ascontiguousarray(inputs[name])
        arrays[f"in_{name}_dram"] = a
        args.append(nc.dram_tensor(f"in_{name}_dram", a.shape, _mybir.dt.from_np(a.dtype), kind="ExternalInput").ap())
    for i, (shape, dtype) in enumerate(_OUTS):
        dt = _mybir.dt.from_np(_np.dtype(dtype))
        args.append(nc.dram_tensor(f"out_{i}_dram", shape, dt, kind="ExternalOutput").ap())
    build(nc, *args)
    r = _run(nc, [arrays], core_ids=[0])
    return r.results[0]["out_0_dram"]
```
